# Optimizing a Trainium2 kernel written in Bass

```python
import numpy as np
import jax
import jax.numpy as jnp

def _softmax(x, axis=-1):
    return jax.nn.softmax(x, axis=axis)

def _gelu(x):
    return jax.nn.gelu(x, approximate=True)

def _silu(x):
    return jax.nn.silu(x)

def _sigmoid(x):
    return jax.nn.sigmoid(x)

def _layernorm(x, axis=-1, eps=1e-05):
    m = jnp.mean(x, axis=axis, keepdims=True)
    v = jnp.var(x, axis=axis, keepdims=True)
    return (x - m) / jnp.sqrt(v + eps)

def _scatter_add(tgt, idx, src, axis=0):
    return tgt.at[idx].add(src)

def _segment_sum(src, seg, n):
    return jax.ops.segment_sum(src, seg, n)
kernel_name = 'mk_gnn_preln_d4_gnn_r32_c58b31'

def setup_inputs(seed: int=0):
    np.random.seed(seed)
    _w = jnp.asarray

    def _rec_inputs():
        import jax
        import jax.numpy as jnp
        _gk = jax.random.key(seed)
        x = -0.000202 + 1 * jax.random.normal(jax.random.fold_in(_gk, 1), (50000, 128), jnp.float32)
        src = jax.random.randint(jax.random.fold_in(_gk, 2), (25000,), 0, 50000, jnp.int32)
        dst = jnp.minimum((50000 * jax.random.uniform(jax.random.fold_in(_gk, 3), (25000,)) ** 2.0).astype(jnp.int32), 49999)
        _o = jnp.argsort(dst, stable=True)
        src = src[_o]
        dst = dst[_o]
        edge_type_9 = jax.random.randint(jax.random.fold_in(_gk, 12), (25000,), 0, 9, jnp.int32)
        return (x, src, dst, edge_type_9)
    x, src, dst, edge_type_9 = _rec_inputs()

    def _L0_gnn_setup():
        import jax, jax.numpy as jnp
        import numpy as np
        NUM_EDGE_TYPES = 8
        HIDDEN = 128
        N_NODES = 50000
        N_EDGES = 18750

        def _gru_cell(x, h, W_ih, W_hh, b_ih, b_hh):
            H = h.shape[-1]
            gi = x @ W_ih.T + b_ih
            gh = h @ W_hh.T + b_hh
            i_r, i_z, i_n = (gi[:, :H], gi[:, H:2 * H], gi[:, 2 * H:])
            h_r, h_z, h_n = (gh[:, :H], gh[:, H:2 * H], gh[:, 2 * H:])
            r = jax.nn.sigmoid(i_r + h_r)
            z = jax.nn.sigmoid(i_z + h_z)
            n = jnp.tanh(i_n + r * h_n)
            return (1.0 - z) * n + z * h
        key = jax.random.key(seed)
        ks = jax.random.split(key, 10)
        H = HIDDEN
        h = jax.random.normal(ks[0], (N_NODES, H), dtype=jnp.float32)
        edge_index = jax.random.randint(ks[1], (2, N_EDGES), 0, N_NODES, dtype=jnp.int32)
        edge_type = jax.random.randint(ks[2], (N_EDGES,), 0, NUM_EDGE_TYPES + 1, dtype=jnp.int32)
        s = 1.0 / np.sqrt(H)
        W_msg = jax.random.uniform(ks[3], (H, H), jnp.float32, -s, s)
        b_msg = jax.random.uniform(ks[4], (H,), jnp.float32, -s, s)
        edge_embed = jax.random.normal(ks[5], (NUM_EDGE_TYPES + 1, H), dtype=jnp.float32)
        W_ih = jax.random.uniform(ks[6], (3 * H, H), jnp.float32, -s, s)
        W_hh = jax.random.uniform(ks[7], (3 * H, H), jnp.float32, -s, s)
        b_ih = jax.random.uniform(ks[8], (3 * H,), jnp.float32, -s, s)
        b_hh = jax.random.uniform(ks[9], (3 * H,), jnp.float32, -s, s)
        return {'h': h, 'edge_index': edge_index, 'edge_type': edge_type, 'num_nodes': N_NODES, 'W_msg': W_msg, 'b_msg': b_msg, 'edge_embed': edge_embed, 'W_ih': W_ih, 'W_hh': W_hh, 'b_ih': b_ih, 'b_hh': b_hh}
    _L0_gnn_all = _L0_gnn_setup()
    _L0_gnn_in = {k: v for k, v in _L0_gnn_all.items() if k in ('W_msg', 'b_msg', 'edge_embed', 'W_ih', 'W_hh', 'b_ih', 'b_hh')}
    del _L0_gnn_all

    def _L1_gnn_setup():
        import jax, jax.numpy as jnp
        import numpy as np
        N_NODES = 50000
        key = jax.random.key(seed)
        k1, k2, k3 = jax.random.split(key, 3)
        H = jax.random.normal(k1, (N_NODES, 128), dtype=jnp.float32)
        edge_index = jax.random.randint(k2, (2, 25000), 0, N_NODES, dtype=jnp.int64)
        W = jax.random.normal(k3, (128, 128), dtype=jnp.float32) * jnp.sqrt(2.0 / 128.0)
        virtual_node = jnp.zeros((1, 128), dtype=jnp.float32)
        return {'H': H, 'edge_index': edge_index, 'W': W, 'virtual_node': virtual_node}
    _L1_gnn_all = _L1_gnn_setup()
    _L1_gnn_in = {k: v for k, v in _L1_gnn_all.items() if k in ('W', 'virtual_node')}
    del _L1_gnn_all

    def _L2_gnn_setup():
        import jax, jax.numpy as jnp
        import numpy as np
        N = 50000
        E = 18750
        IN = 128
        H = 4
        C = 32
        B = 3
        NEG_SLOPE = 0.2
        key = jax.random.key(seed)
        ks = jax.random.split(key, 6)
        x = jax.random.normal(ks[0], (N, IN), dtype=jnp.float32)
        edge_index = jax.random.randint(ks[1], (2, E), 0, N)
        coeffs_t = jnp.array([0.25, 0.5, 0.25], dtype=jnp.float32)
        glorot_w = float(np.sqrt(2.0) * np.sqrt(6.0 / (H * C + IN)))
        glorot_a = float(np.sqrt(2.0) * np.sqrt(6.0 / (1 + C)))
        lin_weight = jax.random.uniform(ks[2], (B, H * C, IN), jnp.float32, -glorot_w, glorot_w)
        lin_bias = jnp.zeros((B, H * C), dtype=jnp.float32)
        att_src = jax.random.uniform(ks[3], (B, 1, H, C), jnp.float32, -glorot_a, glorot_a)
        att_dst = jax.random.uniform(ks[4], (B, 1, H, C), jnp.float32, -glorot_a, glorot_a)
        return {'x': x, 'edge_index': edge_index, 'coeffs_t': coeffs_t, 'lin_weight': lin_weight, 'lin_bias': lin_bias, 'att_src': att_src, 'att_dst': att_dst}
    _L2_gnn_all = _L2_gnn_setup()
    _L2_gnn_in = {k: v for k, v in _L2_gnn_all.items() if k in ('coeffs_t', 'lin_weight', 'lin_bias', 'att_src', 'att_dst')}
    del _L2_gnn_all

    def _L3_gnn_setup():
        import jax, jax.numpy as jnp
        import numpy as np
        N_NODES = 3125
        N_EDGES = 625000
        D = 128

        def _sage_conv(x, edge_index, W_l, b_l, W_r):
            src, dst = (edge_index[0], edge_index[1])
            msgs = x[src]
            agg = jax.ops.segment_sum(msgs, dst, num_segments=x.shape[0])
            deg = jax.ops.segment_sum(jnp.ones((msgs.shape[0],), x.dtype), dst, num_segments=x.shape[0])
            agg = agg / jnp.maximum(deg, 1.0)[:, None]
            return agg @ W_l.T + b_l + x @ W_r.T
        key = jax.random.key(seed)
        ks = jax.random.split(key, 7)
        s = 1.0 / np.sqrt(D)
        x = jax.random.normal(ks[0], (N_NODES, D), dtype=jnp.float32)
        edge_index = jax.random.randint(ks[1], (2, N_EDGES), 0, N_NODES, dtype=jnp.int64)
        return {'x': x, 'edge_index': edge_index, 'W1_l': jax.random.normal(ks[2], (D, D), dtype=jnp.float32) * s, 'b1': jnp.zeros((D,), dtype=jnp.float32), 'W1_r': jax.random.normal(ks[3], (D, D), dtype=jnp.float32) * s, 'W2_l': jax.random.normal(ks[4], (D, D), dtype=jnp.float32) * s, 'b2': jnp.zeros((D,), dtype=jnp.float32), 'W2_r': jax.random.normal(ks[5], (D, D), dtype=jnp.float32) * s}
    _L3_gnn_all = _L3_gnn_setup()
    _L3_gnn_in = {k: v for k, v in _L3_gnn_all.items() if k in ('W1_l', 'b1', 'W1_r', 'W2_l', 'b2', 'W2_r')}
    del _L3_gnn_all
    return {'x': x, 'src': src, 'dst': dst, 'edge_type_9': edge_type_9, 'L0_gnn_W_msg': _L0_gnn_in['W_msg'], 'L0_gnn_b_msg': _L0_gnn_in['b_msg'], 'L0_gnn_edge_embed': _L0_gnn_in['edge_embed'], 'L0_gnn_W_ih': _L0_gnn_in['W_ih'], 'L0_gnn_W_hh': _L0_gnn_in['W_hh'], 'L0_gnn_b_ih': _L0_gnn_in['b_ih'], 'L0_gnn_b_hh': _L0_gnn_in['b_hh'], 'L1_gnn_W': _L1_gnn_in['W'], 'L1_gnn_virtual_node': _L1_gnn_in['virtual_node'], 'L2_gnn_coeffs_t': _L2_gnn_in['coeffs_t'], 'L2_gnn_lin_weight': _L2_gnn_in['lin_weight'], 'L2_gnn_lin_bias': _L2_gnn_in['lin_bias'], 'L2_gnn_att_src': _L2_gnn_in['att_src'], 'L2_gnn_att_dst': _L2_gnn_in['att_dst'], 'L3_gnn_W1_l': _L3_gnn_in['W1_l'], 'L3_gnn_b1': _L3_gnn_in['b1'], 'L3_gnn_W1_r': _L3_gnn_in['W1_r'], 'L3_gnn_W2_l': _L3_gnn_in['W2_l'], 'L3_gnn_b2': _L3_gnn_in['b2'], 'L3_gnn_W2_r': _L3_gnn_in['W2_r']}

def reference(x, src, dst, edge_type_9, L0_gnn_W_msg, L0_gnn_b_msg, L0_gnn_edge_embed, L0_gnn_W_ih, L0_gnn_W_hh, L0_gnn_b_ih, L0_gnn_b_hh, L1_gnn_W, L1_gnn_virtual_node, L2_gnn_coeffs_t, L2_gnn_lin_weight, L2_gnn_lin_bias, L2_gnn_att_src, L2_gnn_att_dst, L3_gnn_W1_l, L3_gnn_b1, L3_gnn_W1_r, L3_gnn_W2_l, L3_gnn_b2, L3_gnn_W2_r):
    import jax
    import jax.numpy as jnp

    def _L0_gnn_ref(h, edge_index, edge_type, num_nodes, W_msg, b_msg, edge_embed, W_ih, W_hh, b_ih, b_hh):
        import jax, jax.numpy as jnp
        import numpy as np
        NUM_EDGE_TYPES = 8
        HIDDEN = 128
        N_NODES = 50000
        N_EDGES = 18750

        def _gru_cell(x, h, W_ih, W_hh, b_ih, b_hh):
            H = h.shape[-1]
            gi = x @ W_ih.T + b_ih
            gh = h @ W_hh.T + b_hh
            i_r, i_z, i_n = (gi[:, :H], gi[:, H:2 * H], gi[:, 2 * H:])
            h_r, h_z, h_n = (gh[:, :H], gh[:, H:2 * H], gh[:, 2 * H:])
            r = jax.nn.sigmoid(i_r + h_r)
            z = jax.nn.sigmoid(i_z + h_z)
            n = jnp.tanh(i_n + r * h_n)
            return (1.0 - z) * n + z * h
        src = edge_index[0]
        dst = edge_index[1]
        src_h = h[src] @ W_msg.T + b_msg
        emb = edge_embed[jnp.clip(edge_type, 0, NUM_EDGE_TYPES)]
        msg = src_h + emb
        messages = jax.ops.segment_sum(msg, dst, num_segments=num_nodes)
        h_new = _gru_cell(messages, h[:num_nodes], W_ih, W_hh, b_ih, b_hh)
        result = jnp.zeros_like(h).at[:num_nodes].set(h_new)
        return result

    def _L1_gnn_ref(H, edge_index, W, virtual_node):
        import jax, jax.numpy as jnp
        import numpy as np
        N_NODES = 50000
        src, dst = (edge_index[0], edge_index[1])
        agg = jax.ops.segment_sum(H[src], dst, num_segments=H.shape[0])
        out = H + agg
        vmsg = jnp.mean(out, axis=0, keepdims=True)
        out = out + (virtual_node + vmsg)
        out = out @ W
        return jax.nn.relu(out)

    def _L2_gnn_ref(x, edge_index, coeffs_t, lin_weight, lin_bias, att_src, att_dst):
        import jax, jax.numpy as jnp
        import numpy as np
        N = 50000
        E = 18750
        IN = 128
        H = 4
        C = 32
        B = 3
        NEG_SLOPE = 0.2
        W = jnp.einsum('b,boi->oi', coeffs_t, lin_weight)
        bias = jnp.einsum('b,bo->o', coeffs_t, lin_bias)
        a_src = jnp.einsum('b,bqhc->qhc', coeffs_t, att_src)
        a_dst = jnp.einsum('b,bqhc->qhc', coeffs_t, att_dst)
        n = x.shape[0]
        xt = (x @ W.T + bias).reshape(n, H, C)
        alpha_src = jnp.sum(xt * a_src, axis=-1)
        alpha_dst = jnp.sum(xt * a_dst, axis=-1)
        row, col = (edge_index[0], edge_index[1])
        alpha = alpha_src[row] + alpha_dst[col]
        alpha = jax.nn.leaky_relu(alpha, NEG_SLOPE)
        amax = jax.ops.segment_max(alpha, col, num_segments=n)
        ex = jnp.exp(alpha - amax[col])
        denom = jax.ops.segment_sum(ex, col, num_segments=n)
        alpha = ex / (denom[col] + 1e-16)
        msg = xt[row] * alpha[..., None]
        out = jax.ops.segment_sum(msg, col, num_segments=n)
        return out.reshape(n, H * C)

    def _L3_gnn_ref(x, edge_index, W1_l, b1, W1_r, W2_l, b2, W2_r):
        import jax, jax.numpy as jnp
        import numpy as np
        N_NODES = 3125
        N_EDGES = 625000
        D = 128

        def _sage_conv(x, edge_index, W_l, b_l, W_r):
            src, dst = (edge_index[0], edge_index[1])
            msgs = x[src]
            agg = jax.ops.segment_sum(msgs, dst, num_segments=x.shape[0])
            deg = jax.ops.segment_sum(jnp.ones((msgs.shape[0],), x.dtype), dst, num_segments=x.shape[0])
            agg = agg / jnp.maximum(deg, 1.0)[:, None]
            return agg @ W_l.T + b_l + x @ W_r.T
        h = jax.nn.relu(_sage_conv(x, edge_index, W1_l, b1, W1_r))
        out = _sage_conv(h, edge_index, W2_l, b2, W2_r)
        return out
    edge_index = jnp.stack([src, dst])
    h = jnp.maximum(_layernorm(x, axis=-1), 0.0)
    x = x + _L0_gnn_ref(h, edge_index, edge_type_9, 50000, L0_gnn_W_msg, L0_gnn_b_msg, L0_gnn_edge_embed, L0_gnn_W_ih, L0_gnn_W_hh, L0_gnn_b_ih, L0_gnn_b_hh)
    h = jnp.maximum(_layernorm(x, axis=-1), 0.0)
    x = x + _L1_gnn_ref(h, edge_index, L1_gnn_W, L1_gnn_virtual_node)
    h = jnp.maximum(_layernorm(x, axis=-1), 0.0)
    x = x + _L2_gnn_ref(h, edge_index, L2_gnn_coeffs_t, L2_gnn_lin_weight, L2_gnn_lin_bias, L2_gnn_att_src, L2_gnn_att_dst)
    h = jnp.maximum(_layernorm(x, axis=-1), 0.0)
    x = x + _L3_gnn_ref(h, edge_index, L3_gnn_W1_l, L3_gnn_b1, L3_gnn_W1_r, L3_gnn_W2_l, L3_gnn_b2, L3_gnn_W2_r)
    return x

_drawn_inputs = setup_inputs


def setup_inputs(seed=0):
    import zlib

    import numpy as np

    out = dict(_drawn_inputs(seed))
    spreads = {'L1_gnn_virtual_node': (0.0, 0.1),
     'L2_gnn_lin_bias': (0.0, 0.456),
     'L3_gnn_b1': (0.0, 0.1),
     'L3_gnn_b2': (0.0, 0.1)}
    factors = {'L0_gnn_b_msg': 6.861,
     'L0_gnn_b_hh': 4.401,
     'L2_gnn_att_src': 4.899,
     'L2_gnn_att_dst': 8.0}
    for name, (base, spread) in spreads.items():
        noise = np.random.default_rng([zlib.crc32(name.encode()), seed]).standard_normal(out[name].shape)
        drawn = base * np.exp(spread * noise) if base else spread * noise
        out[name] = jnp.asarray(drawn.astype(out[name].dtype))
    for name, factor in factors.items():
        out[name] = (out[name] * factor).astype(out[name].dtype)
    return out
```

```python
import concourse.bass as bass
from concourse import mybir
from concourse.alu_op_type import AluOpType as ALU
from contextlib import ExitStack

F32 = mybir.dt.float32
I32 = mybir.dt.int32
ACT = mybir.ActivationFunctionType
AX_X = mybir.AxisListType.X

P = 128
D = 128
NODES = 50000
EDGES = 25000
TILES = 400
NODES_PAD = P * TILES
REAL_P = NODES // TILES
GROUP = 4
GROUPS = TILES // GROUP
COLS = -(-EDGES // P)
EDGES_PAD = P * COLS
RING = 14
HALF = RING // 2
STEPS = COLS // RING
TYPES = 9
WIDE = 144
HEADS = 4
HD = D // HEADS
XT_W = D + 2 * HEADS
PAD_DST = NODES_PAD + 4096
SKIP = 1.0e5
FAR = 1.0e30
EPS = 1e-5


def held(eng, reg, value):
    if isinstance(value, int):
        return value
    eng.reg_add(reg, value, 0)
    return eng.snap(reg)


def due(value):
    return not isinstance(value, int) or value > 0


def looped(eng, body, count, peel=1, last=False):
    for i in range(peel):
        body(i)
    with eng.Fori(peel, count - 1 if last else count) as i:
        body(i)
    if last:
        body(count - 1)


class Ctx:
    def __init__(self, nc, stack):
        self.nc, self.stack, self.sems = nc, stack, []

    def sb(self, name, shape, dt=F32):
        return self.stack.enter_context(self.nc.sbuf_tensor(name, shape, dt))

    def ps(self, name, shape, dt=F32):
        return self.stack.enter_context(self.nc.psum_tensor(name, shape, dt))

    def sem(self, name):
        s = self.stack.enter_context(self.nc.semaphore(name))
        self.sems.append(s)
        return s

    def phase(self):
        self.stack.callback(self.clear)
        return self.stack.enter_context(self.nc.Block())

    def clear(self):
        with self.nc.Block() as block:
            @block.gpsimd
            def _(pool):
                for s in self.sems:
                    pool.sem_clear(s)


def stepper(eng, sem):
    count = [0]

    def step(ins):
        count[0] += 1
        ins.then_inc(sem, 1)
        eng.wait_ge(sem, count[0])
    return step


def earlier(K, gathers=False, scatters=False, fixes=False):
    at = tuple(K["counts"])
    for n, (used, count) in enumerate(((gathers, 16 * STEPS), (scatters, 16 * STEPS), (fixes, 16))):
        K["counts"][n] += count if used else 0
    return at


def rows_by_group(table, width):
    return table.rearrange("(p j) d -> p (j d)", p=P)


def setup(nc, A, K):
    with ExitStack() as st:
        c = Ctx(nc, st)
        zero = c.sb("zero", [P, 10 * WIDE * 4])
        cur = c.sb("cur", [P, COLS]); prv = c.sb("prv", [P, COLS]); nxt = c.sb("nxt", [P, COLS])
        cur_i = c.sb("cur_i", [P, COLS], I32); prv_i = c.sb("prv_i", [P, COLS], I32)
        nxt_i = c.sb("nxt_i", [P, COLS], I32); typ_i = c.sb("typ_i", [P, COLS], I32)
        typ = c.sb("typ", [P, COLS]); is_end = c.sb("is_end", [P, COLS]); tmp = c.sb("tmp", [P, COLS])
        iota = c.sb("iota16", [P, 16]); tri = c.sb("tri", [P, P]); tri_t = c.sb("tri_t", [P, P])
        cur_bc = c.sb("cur_bc", [P, 2, P]); small = c.sb("small", [P, 8])
        lw = c.sb("lw", [P, 3, D]); lwt = c.sb("lwt", [P, 3, D]); w2 = c.sb("w2", [P, D])
        coef = c.sb("coef", [P, 3]); cols = c.sb("att_cols", [P, 3, 3]); acol = c.sb("acol", [P, 3])
        blk = c.sb("blk", [P, HEADS]); ab = c.sb("ab", [P, XT_W]); bias_bc = c.sb("bias_bc", [P, P])
        bm = c.sb("bm", [TYPES, D]); bb = c.sb("bb", [P, 2, 3])
        pt = c.ps("pt", [P, 512]); pu = c.ps("pu", [P, 512])
        s_ld = c.sem("setup_loaded"); s_z = c.sem("zero_ready"); s_clr = c.sem("tables_cleared")
        s_v = c.sem("setup_vector"); s_pe = c.sem("setup_tensor"); s_bc = c.sem("setup_ready")
        block = c.phase()
        loads = [
            (cur_i, A["dst"][1:1 + EDGES_PAD].rearrange("(p c) -> p c", p=P)),
            (prv_i, A["dst"][0:EDGES_PAD].rearrange("(p c) -> p c", p=P)),
            (nxt_i, A["dst"][2:2 + EDGES_PAD].rearrange("(p c) -> p c", p=P)),
            (K["src_idx"], A["src"].rearrange("(p c) -> p c", p=P)),
            (typ_i, A["etype"].rearrange("(p c) -> p c", p=P)),
            (iota, A["iota"]), (tri, A["tri"]), (tri_t, A["tri_t"]), (K["ident"], A["ident"]),
            (lw, A["lin_w"]), (lwt, A["lin_wt"]), (coef, A["coef"].partition_broadcast(P)),
            (cols, A["att_cols"]), (blk, A["blk"]), (bm, A["b_msg"].partition_broadcast(TYPES)),
            (K["emb"], A["emb"]), (K["w_msg"], A["w_msg"]), (K["w_ih"], A["w_ih"]), (K["w_hh"], A["w_hh"]),
            (bb, A["b_gru"]), (K["w1"], A["w1"]), (K["vn"], A["vn"]), (K["w1l"], A["w1l"]),
            (K["w1r"], A["w1r"]), (K["w2lr"], A["w2lr"]), (K["b1"], A["b1"]),
            (K["b2_bc"], A["b2"].partition_broadcast(P)), (K["real"], A["real"]), (K["valid"], A["valid"]),
        ]

        @block.sync
        def _(sp):
            for t, src in loads:
                sp.dma_start(t[:], src).then_inc(s_ld, 16)
            sp.wait_ge(s_z, 1)
            for table, width in ((K["ag_wide"], WIDE), (K["ag"], D)):
                part = TILES * width // 10
                for k in range(10):
                    sp.dma_start(rows_by_group(table, width)[:, k * part:(k + 1) * part],
                                 zero[:, 0:part]).then_inc(s_clr, 16)
            sp.wait_ge(s_clr, 20 * 16)

        @block.vector
        def _(v):
            step = stepper(v, s_v)
            v.memset(zero[:], 0.0).then_inc(s_z, 1)
            step(v.memset(K["ones"][:], 1.0))
            step(v.memset(K["eps"][:], EPS))
            v.wait_ge(s_ld, 16 * len(loads))
            for f, i in ((cur, cur_i), (prv, prv_i), (nxt, nxt_i), (typ, typ_i)):
                step(v.tensor_copy(f[:], i[:]))
            step(v.tensor_tensor(K["same"][:], prv[:], cur[:], ALU.is_equal))
            step(v.tensor_tensor(tmp[:], nxt[:], cur[:], ALU.is_equal))
            step(v.tensor_scalar(is_end[:], tmp[:], -1.0, 1.0, ALU.mult, ALU.add))
            step(v.tensor_scalar(tmp[:], cur[:], -SKIP, None, ALU.add))
            step(v.tensor_tensor(tmp[:], tmp[:], is_end[:], ALU.mult))
            step(v.tensor_scalar(K["dst_idx"][:], tmp[:], SKIP, None, ALU.add))
            step(v.tensor_copy(K["dst_row"][:], cur_i[:]))
            step(v.tensor_scalar(tmp[:], cur[:], cur[:, 0:1], None, ALU.is_equal))
            step(v.tensor_tensor(tmp[:], tmp[:], is_end[:], ALU.mult))
            step(v.tensor_reduce(small[:, 0:1], tmp[:], AX_X, ALU.max))
            step(v.tensor_tensor(small[:, 1:2], small[:, 0:1], K["same"][:, 0:1], ALU.mult))
            step(v.tensor_scalar(small[:, 2:3], cur[:, 0:1], -SKIP, None, ALU.add))
            step(v.tensor_tensor(small[:, 3:4], small[:, 1:2], small[:, 2:3], ALU.mult))
            step(v.tensor_scalar(K["head_idx"][:], small[:, 3:4], SKIP, None, ALU.add))
            step(v.tensor_scalar(typ[:], typ[:], 0.0, float(TYPES - 1), ALU.max, ALU.min))
            step(v.tensor_tensor(K["onehot"][:], typ[:].unsqueeze(2).to_broadcast([P, COLS, 16]),
                                 iota[:].unsqueeze(1).to_broadcast([P, COLS, 16]), ALU.is_equal))
            step(v.tensor_copy(cur_bc[:, 0, :], cur[:, 0:1].to_broadcast([P, P])))
            step(v.tensor_copy(cur_bc[:, 1, :], cur[:, COLS - 1:COLS].to_broadcast([P, P])))
            for o, w in ((w2[:], lw), (K["w_cat"][:, 0:D], lwt), (acol[:], cols)):
                step(v.tensor_scalar(o, w[:, 0, :], coef[:, 0:1], None, ALU.mult))
                for b in (1, 2):
                    step(v.scalar_tensor_tensor(o, w[:, b, :], coef[:, b:b + 1], o, ALU.mult, ALU.add))
            step(v.tensor_copy(ab[:, 0:D], K["ident"][:]))
            step(v.tensor_scalar(ab[:, D:D + HEADS], blk[:], acol[:, 0:1], None, ALU.mult))
            step(v.tensor_scalar(ab[:, D + HEADS:XT_W], blk[:], acol[:, 1:2], None, ALU.mult))
            step(v.tensor_copy(bias_bc[:], acol[:, 2:3].to_broadcast([P, P])))
            step(v.tensor_tensor(K["emb"][:], K["emb"][:], bm[:], ALU.add))
            step(v.tensor_tensor(K["b_rz"][:], bb[:, 0, 0:2], bb[:, 1, 0:2], ALU.add))
            step(v.tensor_copy(K["b_n"][:], bb[:, :, 2]))
            v.tensor_copy(small[:, 4:5], small[:, 3:4]).then_inc(s_bc, 1)
            v.wait_ge(s_pe, 1)
            step(v.scalar_tensor_tensor(K["carry_qp"][:], pt[:, 0:P], cur[:, COLS - 1:COLS], tri[:],
                                        ALU.is_equal, ALU.mult))
            step(v.scalar_tensor_tensor(K["carry_pq"][:], pt[:, P:2 * P], cur[:, 0:1], tri_t[:],
                                        ALU.is_equal, ALU.mult))
            step(v.tensor_copy(K["w_cat"][:, D:XT_W], pu[:, 0:2 * HEADS]))
            step(v.tensor_copy(K["xt_bias"][:], pu[:, 2 * HEADS:2 * HEADS + XT_W]))

        @block.tensor
        def _(pe):
            pe.wait_ge(s_bc, 1)
            pe.transpose(pt[:, 0:P], cur_bc[:, 0, :], K["ident"][:])
            pe.transpose(pt[:, P:2 * P], cur_bc[:, 1, :], K["ident"][:])
            pe.matmul(pu[:, 0:2 * HEADS], w2[:], ab[:, D:XT_W], start=True, stop=True)
            pe.matmul(pu[:, 2 * HEADS:2 * HEADS + XT_W], bias_bc[:], ab[:],
                      start=True, stop=True).then_inc(s_pe, 1)


def edge_pass(nc, K, tag, table, sums, width, norm, node_stream=None):
    onehot = width > D
    g0, sc0, f0 = earlier(K, gathers=True, scatters=True, fixes=True)
    with ExitStack() as st:
        c = Ctx(nc, st)
        n = lambda s: f"{tag}_{s}"
        gi = c.sb(n("gather_idx"), [P, RING], I32)
        si = c.sb(n("scatter_idx"), [P, RING], I32)
        g = c.sb(n("rows"), [P, RING, D])
        h = c.sb(n("norm_rows"), [P, RING, D]) if norm else g
        run = c.sb(n("run"), [P, RING, width])
        bs = c.sb(n("bn"), [P, RING, 6]); mv = c.sb(n("mean_var"), [P, RING, 2])
        sd = c.sb(n("std"), [P, RING]); rs = c.sb(n("rstd"), [P, RING]); nm = c.sb(n("shift"), [P, RING])
        fix = c.sb(n("fix"), [P, width]); fixed = c.sb(n("fixed"), [P, width])
        carry = c.ps(n("carry"), [P, width])
        s_start = c.sem(n("fix_cleared")); s_clear = c.sem(n("run_cleared")); clears = 1 + (node_stream == "colsum")
        s_gi = c.sem(n("gather_idx_ready")); s_si = c.sem(n("scatter_idx_ready"))
        s_g = K["gather_sems"]
        s_sc = K["scatter_sems"]
        s_bn = c.sem(n("bn_done")); s_mv = c.sem(n("mean_var_done")); s_sd = c.sem(n("std_done"))
        s_rs = c.sem(n("rstd_done")); s_nm = c.sem(n("shift_done")); s_h = c.sem(n("normed"))
        s_run = c.sem(n("run_done")); s_fx, s_out = K["fix_sems"]; s_ca = c.sem(n("carry_done"))
        s_fd = c.sem(n("fixed_done"))
        stream = node_stream is not None
        if stream:
            PER = 7
            REST = GROUPS - STEPS * PER
            nx = c.sb(n("node_rows"), [P, PER, GROUP * D])
            s_nx = [c.sem(n(f"node_loaded{m}")) for m in range(PER)]
            s_nu = c.sem(n("node_used"))
        if node_stream == "stats":
            nbn = c.sb(n("node_bn"), [P, PER, GROUP, 6]); nmv = c.sb(n("node_mv"), [P, PER, GROUP * 2])
            s_nb = c.sem(n("node_bn_done")); s_nmv = c.sem(n("node_mv_done"))
        if node_stream == "colsum":
            nr = c.sb(n("node_rn"), [P, PER, GROUP * 2]); nh = c.sb(n("node_h"), [P, PER, GROUP * D])
            acc = c.sb(n("edge_acc"), [P, D]); row = c.sb(n("sum_row"), [1, GROUP * D])
            prow = c.ps(n("node_sum"), [1, GROUP * D]); pcol = c.ps(n("sum_col"), [P, 8])
            s_nr = c.sem(n("node_rn_done")); s_nh = c.sem(n("node_h_done")); s_np = c.sem(n("node_summed"))
            s_ac = c.sem(n("edge_acc_done")); s_row = c.sem(n("row_done")); s_col = c.sem(n("col_done"))
            s_v = c.sem(n("v_done"))
        block = c.phase()
        last_step = STEPS - 1

        if stream:
            @block.sync
            def _(sp):
                rows = rows_by_group(table, D)

                def load(i, m):
                    q = i * PER + m
                    if due(q - PER + 1):
                        if node_stream == "stats":
                            sp.wait_ge(s_nu, q - PER + 1)
                        else:
                            sp.wait_ge(s_nh, (q - PER + 1) * GROUP)
                    sp.dma_start(nx[:, m, :], rows[:, bass.ds(q * (GROUP * D), GROUP * D)]).then_inc(s_nx[m], 16)

                def body(i):
                    for m in range(PER):
                        load(i, m)
                looped(sp, body, STEPS)
                for m in range(REST):
                    load(STEPS, m)

        @block.gpsimd
        def _(pool):
            reg = pool.alloc_register(n("pool_count"))
            pool.memset(fix[:], 0.0).then_inc(s_start, 1)
            pool.wait_ge(s_start, 1)

            def gather_index(i, half):
                a = half * HALF
                pool.tensor_copy(gi[:, a:a + HALF], K["src_idx"][:, bass.ds(i * RING + a, HALF)]).then_inc(s_gi, 1)

            def gather(i, k):
                if norm:
                    used, count = s_h, i * RING + k + 1 - RING
                else:
                    used, count = s_run, i * RING + k + 1 - RING
                idx_count = held(pool, reg, i * 2 + k // HALF + 1)
                pool.wait_ge(s_start, 1)
                pool.wait_ge(s_gi, idx_count)
                if due(count):
                    count = held(pool, reg, count)
                    pool.wait_ge(s_start, 1)
                    pool.wait_ge(used, count)
                pool.indirect_dma_start(g[:, k, :], None, table,
                                        bass.IndirectOffsetOnAxis(gi[:, k:k + 1], 0),
                                        bounds_check=NODES_PAD - 1, oob_is_err=False).then_inc(s_g[k], 16)

            for half in (0, 1):
                gather_index(0, half)
            for k in range(RING):
                gather(0, k)

            def body(i):
                last = isinstance(i, int) and i == STEPS - 1
                for k in range(RING):
                    if k % HALF == 0:
                        half = k // HALF
                        if not last:
                            for kk in range(k, k + HALF):
                                pool.wait_ge(s_g[kk], g0 + i * 16 + 16)
                            gather_index(i + 1, half)
                        if due(i):
                            for kk in range(k, k + HALF):
                                pool.wait_ge(s_sc[kk], sc0 + i * 16)
                        pool.wait_ge(s_start, 1)
                        pool.tensor_copy(si[:, k:k + HALF],
                                         K["dst_idx"][:, bass.ds(i * RING + k, HALF)]).then_inc(s_si, 1)
                    if not last:
                        gather(i + 1, k)
                    idx_count = held(pool, reg, i * 2 + k // HALF + 1)
                    pool.wait_ge(s_start, 1)
                    pool.wait_ge(s_si, idx_count)
                    run_count = held(pool, reg, i * RING + k + 1)
                    pool.wait_ge(s_start, 1)
                    pool.wait_ge(s_run, run_count)
                    pool.indirect_dma_start(sums, bass.IndirectOffsetOnAxis(si[:, k:k + 1], 0),
                                            run[:, k, :], None, bounds_check=NODES_PAD - 1,
                                            oob_is_err=False).then_inc(s_sc[k], 16)
            looped(pool, body, STEPS, last=True)
            for k in range(RING):
                pool.wait_ge(s_sc[k], sc0 + 16 * STEPS)
            head = bass.IndirectOffsetOnAxis(K["head_idx"][:, 0:1], 0)
            pool.indirect_dma_start(fix[:], None, sums, head, bounds_check=NODES_PAD - 1,
                                    oob_is_err=False).then_inc(s_fx, 16)
            pool.wait_ge(s_fd, 1)
            pool.indirect_dma_start(sums, head, fixed[:], None, bounds_check=NODES_PAD - 1,
                                    oob_is_err=False).then_inc(s_out, 16)
            pool.wait_ge(s_out, f0 + 16)

        @block.vector
        def _(v):
            reg = v.alloc_register(n("vector_count"))
            v.memset(run[:], 0.0).then_inc(s_clear, 1)
            if node_stream == "colsum":
                v.memset(acc[:], 0.0).then_inc(s_clear, 1)
            v.wait_ge(s_clear, clears)

            def node_group(i, m):
                q = i * PER + m
                v.wait_ge(s_nx[m], i * 16 + 16)
                for j in range(GROUP):
                    ins = v.bn_stats(nbn[:, m, j, :], nx[:, m, j * D:(j + 1) * D])
                ins.then_inc(s_nb, 1)
                count = held(v, reg, q + 1)
                v.wait_ge(s_clear, clears)
                v.wait_ge(s_nb, count)
                for j in range(GROUP):
                    ins = v.bn_aggr(nmv[:, m, 2 * j:2 * j + 2], nbn[:, m, j, :])
                ins.then_inc(s_nmv, 1)
                v.wait_ge(s_nmv, q + 1)
                v.tensor_copy(K["node_mv"][:, bass.ds(q * (2 * GROUP), 2 * GROUP)], nmv[:, m, :]).then_inc(s_nu, 1)

            def body(i):
                for half in (0, 1):
                    a = half * HALF
                    u = i * 2 + half
                    if norm:
                        for k in range(a, a + HALF):
                            v.wait_ge(s_g[k], g0 + i * 16 + 16)
                            ins = v.bn_stats(bs[:, k, :], g[:, k, :])
                        ins.then_inc(s_bn, 1)
                        count = held(v, reg, u + 1)
                        v.wait_ge(s_clear, clears)
                        v.wait_ge(s_bn, count)
                        for k in range(a, a + HALF):
                            ins = v.bn_aggr(mv[:, k, :], bs[:, k, :])
                        ins.then_inc(s_mv, 1)
                        v.wait_ge(s_sd, u + 1)
                        v.reciprocal(rs[:, a:a + HALF], sd[:, a:a + HALF]).then_inc(s_rs, 1)
                        v.wait_ge(s_rs, u + 1)
                        v.scalar_tensor_tensor(nm[:, a:a + HALF], mv[:, a:a + HALF, 0], -1.0,
                                               rs[:, a:a + HALF], ALU.mult, ALU.mult).then_inc(s_nm, 1)
                    if node_stream == "stats":
                        for m in (range(0, 4) if half == 0 else range(4, PER)):
                            node_group(i, m)
                    for k in range(a, a + HALF):
                        col = i * RING + k
                        if norm:
                            v.wait_ge(s_h, col + 1)
                        else:
                            v.wait_ge(s_g[k], g0 + i * 16 + 16)
                        if due(col):
                            v.wait_ge(s_run, col)
                        if due(i):
                            v.wait_ge(s_sc[k], sc0 + i * 16)
                        same = K["same"][:, bass.ds(col, 1)]
                        prev = run[:, (k - 1) % RING, :]
                        if onehot:
                            v.scalar_tensor_tensor(run[:, k, D:width], prev[:, D:width], same,
                                                   K["onehot"][:, bass.ds(col, 1), :].rearrange("p a t -> p (a t)"),
                                                   ALU.mult, ALU.add)
                        v.scalar_tensor_tensor(run[:, k, 0:D], prev[:, 0:D], same, h[:, k, :],
                                               ALU.mult, ALU.add).then_inc(s_run, 1)
                        if node_stream == "colsum":
                            if due(col):
                                v.wait_ge(s_ac, col)
                            v.scalar_tensor_tensor(acc[:], h[:, k, :], K["valid"][:, bass.ds(col, 1)], acc[:],
                                                   ALU.mult, ALU.add).then_inc(s_ac, 1)
            looped(v, body, STEPS)
            if node_stream == "stats":
                for m in range(REST):
                    node_group(STEPS, m)
            if node_stream == "colsum":
                v.wait_ge(s_np, GROUPS)
                v.tensor_copy(row[:], prow[:]).then_inc(s_row, 1)
                v.wait_ge(s_col, 1)
                v.scalar_tensor_tensor(K["v_col"][:], pcol[:, 0:1], 1.0 / NODES, K["vn"][:],
                                       ALU.mult, ALU.add).then_inc(s_v, 1)
            v.wait_ge(s_ca, 1)
            v.wait_ge(s_fx, f0 + 16)
            v.tensor_tensor(fixed[:], fix[:], carry[:], ALU.add).then_inc(s_fd, 1)

        if norm:
            @block.scalar
            def _(act):
                reg = act.alloc_register(n("act_count"))

                def node_group(i, m):
                    q = i * PER + m
                    if due(q - PER + 1):
                        act.wait_ge(s_np, q - PER + 1)
                    act.wait_ge(s_clear, clears)
                    act.copy(nr[:, m, :], K["node_rn"][:, bass.ds(q * (2 * GROUP), 2 * GROUP)]).then_inc(s_nr, 1)
                    act.wait_ge(s_nx[m], i * 16 + 16)
                    act.wait_ge(s_nr, q + 1)
                    for j in range(GROUP):
                        ins = act.activation(nh[:, m, j * D:(j + 1) * D], nx[:, m, j * D:(j + 1) * D], ACT.Relu,
                                             bias=nr[:, m, 2 * j + 1:2 * j + 2], scale=nr[:, m, 2 * j:2 * j + 1])
                        ins.then_inc(s_nh, 1)

                def body(i):
                    for half in (0, 1):
                        a = half * HALF
                        u = i * 2 + half
                        act.wait_ge(s_mv, u + 1)
                        if due(u - 1):
                            act.wait_ge(s_rs, u - 1)
                        act.activation(sd[:, a:a + HALF], mv[:, a:a + HALF, 1], ACT.Sqrt,
                                       bias=K["eps"][:, 0:1]).then_inc(s_sd, 1)
                        if node_stream == "colsum":
                            for m in (range(0, 4) if half == 0 else range(4, PER)):
                                node_group(i, m)
                        act.wait_ge(s_nm, u + 1)
                        for k in range(a, a + HALF):
                            if due(i):
                                act.wait_ge(s_run, (i - 1) * RING + k + 1)
                                if node_stream == "colsum":
                                    act.wait_ge(s_ac, (i - 1) * RING + k + 1)
                            act.activation(h[:, k, :], g[:, k, :], ACT.Relu, bias=nm[:, k:k + 1],
                                           scale=rs[:, k:k + 1]).then_inc(s_h, 1)
                looped(act, body, STEPS)
                if node_stream == "colsum":
                    for m in range(REST):
                        node_group(STEPS, m)

        @block.tensor
        def _(pe):
            if node_stream == "colsum":
                def node_group(i, m):
                    q = i * PER + m
                    pe.wait_ge(s_nh, q * GROUP + GROUP)
                    start = isinstance(i, int) and i == 0 and m == 0
                    end = isinstance(i, int) and i == STEPS and m == REST - 1
                    pe.matmul(prow[:], K["real"][:, 0:1], nh[:, m, :], start=start, stop=end,
                              skip_group_check=True).then_inc(s_np, 1)

                def body(i):
                    for m in range(PER):
                        node_group(i, m)
                looped(pe, body, STEPS)
                for m in range(REST):
                    node_group(STEPS, m)
                pe.wait_ge(s_row, 1)
                pe.wait_ge(s_ac, COLS)
                for j in range(GROUP):
                    pe.matmul(pcol[:, 0:1], row[0:1, j * D:(j + 1) * D], K["ones"][0:1, 0:1],
                              start=(j == 0), stop=False)
                pe.matmul(pcol[:, 0:1], acc[:], K["ones"][:, 0:1], start=False, stop=True).then_inc(s_col, 1)
            pe.wait_ge(s_run, COLS)
            pe.matmul(carry[:], K["carry_qp"][:], run[:, RING - 1, :], start=True, stop=True).then_inc(s_ca, 1)


def finish_stats(nc, K, tag):
    with ExitStack() as st:
        c = Ctx(nc, st)
        sd = c.sb(f"{tag}_sd", [P, TILES])
        s_sd = c.sem(f"{tag}_sd_done"); s_v = c.sem(f"{tag}_rstd_done")
        block = c.phase()
        mv = K["node_mv"][:].rearrange("p (j t) -> p j t", t=2)
        rn = K["node_rn"][:].rearrange("p (j t) -> p j t", t=2)

        @block.scalar
        def _(act):
            act.activation(sd[:], mv[:, :, 1], ACT.Sqrt, bias=K["eps"][:, 0:1]).then_inc(s_sd, 1)

        @block.vector
        def _(v):
            v.wait_ge(s_sd, 1)
            v.reciprocal(rn[:, :, 0], sd[:]).then_inc(s_v, 1)
            v.wait_ge(s_v, 1)
            v.scalar_tensor_tensor(rn[:, :, 1], mv[:, :, 0], -1.0, rn[:, :, 0], ALU.mult, ALU.mult)



def gru_nodes(nc, K, x_in, x_out):
    with ExitStack() as st:
        c = Ctx(nc, st)
        x = c.sb("gru_x", [P, GROUP, GROUP * D]); ag = c.sb("gru_sum", [P, GROUP, GROUP, WIDE])
        rn = c.sb("gru_rn", [P, GROUP, 2 * GROUP])
        hn = c.sb("gru_hn", [P, 2, GROUP * D]); hT = c.sb("gru_hT", [P, 2, GROUP * D])
        aT = c.sb("gru_aT", [P, 2, GROUP * D]); cT = c.sb("gru_cT", [TYPES, 2, GROUP * D])
        mT = c.sb("gru_mT", [P, 2, GROUP * D])
        r = c.sb("gru_r", [P, 2, GROUP * D]); z = c.sb("gru_z", [P, 2, GROUP * D])
        t = c.sb("gru_t", [P, 2, GROUP * D]); u = c.sb("gru_u", [P, 2, GROUP * D])
        nn = c.sb("gru_n", [P, 2, GROUP * D]); d = c.sb("gru_d", [P, 2, GROUP * D])
        e = c.sb("gru_e", [P, 2, GROUP * D]); hw = c.sb("gru_new", [P, 2, GROUP * D])
        xo = c.sb("gru_xo", [P, GROUP, GROUP * D])
        bs = c.sb("gru_bn", [P, GROUP, GROUP, 6]); mv = c.sb("gru_mv", [P, GROUP, 2 * GROUP])
        dg = c.sb("gru_deg", [P, GROUP, GROUP]); dm = c.sb("gru_degm", [P, GROUP, GROUP])
        pA, pB, pC, pM, pR, pZ, pI, pH = (c.ps(f"gru_p{k}", [P, GROUP * D]) for k in "ABCMRZIH")
        s_x = [c.sem(f"gru_x_in{k}") for k in range(GROUP)]
        s_a = [c.sem(f"gru_sum_in{k}") for k in range(GROUP)]
        s_o = [c.sem(f"gru_out{k}") for k in range(GROUP)]
        s_rn = c.sem("gru_rn_done"); s_hn = c.sem("gru_hn_done"); s_ta = c.sem("gru_h_transposed")
        s_tb = c.sem("gru_sum_transposed"); s_tc = c.sem("gru_counts_transposed")
        s_hT = c.sem("gru_hT_done"); s_aT = c.sem("gru_aT_done"); s_cT = c.sem("gru_cT_done")
        s_m = c.sem("gru_msg"); s_mT = c.sem("gru_mT_done")
        s_gr = c.sem("gru_gate_r"); s_gh = c.sem("gru_gate_h"); s_gi = c.sem("gru_gate_i"); s_gz = c.sem("gru_gate_z")
        s_r = c.sem("gru_r_done"); s_z = c.sem("gru_z_done"); s_t = c.sem("gru_t_done"); s_u = c.sem("gru_u_done")
        s_n = c.sem("gru_n_done"); s_d = c.sem("gru_d_done"); s_e = c.sem("gru_e_done"); s_h = c.sem("gru_new_done")
        s_to = c.sem("gru_new_transposed"); s_xo = c.sem("gru_xo_done"); s_bn = c.sem("gru_bn_done")
        s_mv = c.sem("gru_mv_done"); s_st = c.sem("gru_stats_done"); s_dg = c.sem("gru_deg_done")
        s_dm = c.sem("gru_degm_done"); s_di = c.sem("gru_deginv_done"); s_k = c.sem("gru_const")
        block = c.phase()
        xr, ar, xw = rows_by_group(x_in, D), rows_by_group(K["ag_wide"], WIDE), rows_by_group(x_out, D)
        W = GROUP * D

        @block.sync
        def _(sp):
            def store(q, k):
                sp.wait_ge(s_xo, q + 1)
                sp.dma_start(xw[:, bass.ds(q * W, W)], xo[:, k, :]).then_inc(s_o[k], 16)

            def body(i):
                for k in range(GROUP):
                    q = i * GROUP + k
                    if due(q - GROUP + 1):
                        sp.wait_ge(s_xo, q - GROUP + 1)
                        sp.wait_ge(s_hn, q - GROUP + 1)
                    sp.dma_start(x[:, k, :], xr[:, bass.ds(q * W, W)]).then_inc(s_x[k], 16)
                    if due(q - GROUP + 1):
                        sp.wait_ge(s_tc, q - GROUP + 1)
                        sp.wait_ge(s_dg, q - GROUP + 1)
                    sp.dma_start(ag[:, k, :, :], ar[:, bass.ds(q * (GROUP * WIDE), GROUP * WIDE)]
                                 .rearrange("p (j w) -> p j w", w=WIDE)).then_inc(s_a[k], 16)
                    if due(q - 2):
                        store(q - 3, (k - 3) % GROUP)
            looped(sp, body, GROUPS // GROUP)
            for q in range(GROUPS - 3, GROUPS):
                store(q, q % GROUP)
            for k in range(GROUP):
                sp.wait_ge(s_o[k], 16 * (GROUPS // GROUP))

        @block.gpsimd
        def _(pool):
            reg = pool.alloc_register("gru_pool")

            def normalise(i, q, k):
                pool.tensor_copy(rn[:, k, :], K["node_rn"][:, bass.ds(q * (2 * GROUP), 2 * GROUP)]).then_inc(s_rn, 1)
                n1 = held(pool, reg, q + 1)
                pool.wait_ge(s_k, 1)
                pool.wait_ge(s_rn, n1)
                n2 = held(pool, reg, i * 16 + 16)
                pool.wait_ge(s_k, 1)
                pool.wait_ge(s_x[k], n2)
                if due(q - 1):
                    n3 = held(pool, reg, q - 1)
                    pool.wait_ge(s_k, 1)
                    pool.wait_ge(s_ta, n3)
                for j in range(GROUP):
                    ins = pool.tensor_scalar(hn[:, k % 2, j * D:(j + 1) * D], x[:, k, j * D:(j + 1) * D],
                                             rn[:, k, 2 * j:2 * j + 1], rn[:, k, 2 * j + 1:2 * j + 2],
                                             ALU.mult, ALU.add)
                ins.then_inc(s_hn, 1)

            def mix(q, b):
                pool.wait_ge(s_n, q + 1)
                pool.tensor_tensor(d[:, b, :], hT[:, b, :], nn[:, b, :], ALU.subtract).then_inc(s_d, 1)
                pool.wait_ge(s_d, q + 1)
                pool.wait_ge(s_z, q + 1)
                if due(q - 1):
                    pool.wait_ge(s_h, q - 1)
                pool.tensor_tensor(e[:, b, :], d[:, b, :], z[:, b, :], ALU.mult).then_inc(s_e, 1)

            def body(i):
                for k in range(GROUP):
                    q = i * GROUP + k
                    normalise(i, q, k)
                    if due(q):
                        mix(q - 1, (k - 1) % 2)
            looped(pool, body, GROUPS // GROUP)
            mix(GROUPS - 1, 1)

        @block.scalar
        def _(act):
            def gates(q, b):
                act.wait_ge(s_gr, q + 1)
                act.activation(r[:, b, :], pR[:], ACT.Sigmoid, bias=K["b_rz"][:, 0:1]).then_inc(s_r, 1)
                act.wait_ge(s_u, q + 1)
                if due(q - 1):
                    act.wait_ge(s_h, q - 1)
                act.activation(nn[:, b, :], u[:, b, :], ACT.Tanh, bias=K["b_n"][:, 0:1]).then_inc(s_n, 1)
                act.wait_ge(s_gz, q + 1)
                if due(q - 1):
                    act.wait_ge(s_e, q - 1)
                act.activation(z[:, b, :], pZ[:], ACT.Sigmoid, bias=K["b_rz"][:, 1:2]).then_inc(s_z, 1)

            def head(q, b):
                act.wait_ge(s_ta, q + 1)
                if due(q - 1):
                    act.wait_ge(s_d, q - 1)
                act.activation(hT[:, b, :], pA[:], ACT.Relu).then_inc(s_hT, 1)
                act.wait_ge(s_m, q + 1)
                act.activation(mT[:, b, :], pM[:], ACT.Identity).then_inc(s_mT, 1)

            def body(i):
                for k in range(GROUP):
                    q = i * GROUP + k
                    if due(q):
                        gates(q - 1, (k - 1) % 2)
                    head(q, k % 2)
            looped(act, body, GROUPS // GROUP)
            gates(GROUPS - 1, 1)

        @block.vector
        def _(v):
            reg = v.alloc_register("gru_vector")
            v.memset(dm[:], 1.0).then_inc(s_k, 1)

            def new(q, b):
                v.wait_ge(s_e, q + 1)
                if due(q - 1):
                    v.wait_ge(s_to, q - 1)
                v.tensor_tensor(hw[:, b, :], e[:, b, :], nn[:, b, :], ALU.add).then_inc(s_h, 1)

            def copies(q, b):
                v.wait_ge(s_tb, q + 1)
                v.tensor_copy(aT[:, b, :], pB[:]).then_inc(s_aT, 1)
                v.wait_ge(s_tc, q + 1)
                v.tensor_copy(cT[:, b, :], pC[0:TYPES, :]).then_inc(s_cT, 1)

            def add(i, q, k, stored):
                v.wait_ge(s_to, q + 1)
                if due(stored):
                    v.wait_ge(s_o[k], stored)
                v.tensor_tensor(xo[:, k, :], x[:, k, :], pA[:], ALU.add).then_inc(s_xo, 1)

            def n_input(q, b):
                v.wait_ge(s_r, q + 1)
                v.wait_ge(s_gh, q + 1)
                v.scalar_tensor_tensor(t[:, b, :], pH[:], K["b_n"][:, 1:2], r[:, b, :], ALU.add, ALU.mult).then_inc(s_t, 1)
                v.wait_ge(s_t, q + 1)
                v.wait_ge(s_gi, q + 1)
                if due(q - 1):
                    v.wait_ge(s_n, q - 1)
                v.tensor_tensor(u[:, b, :], t[:, b, :], pI[:], ALU.add).then_inc(s_u, 1)

            def stats(q, k):
                v.wait_ge(s_xo, q + 1)
                for j in range(GROUP):
                    ins = v.bn_stats(bs[:, k, j, :], xo[:, k, j * D:(j + 1) * D])
                ins.then_inc(s_bn, 1)
                count = held(v, reg, q + 1)
                v.wait_ge(s_k, 1)
                v.wait_ge(s_bn, count)
                for j in range(GROUP):
                    ins = v.bn_aggr(mv[:, k, 2 * j:2 * j + 2], bs[:, k, j, :])
                ins.then_inc(s_mv, 1)
                v.wait_ge(s_mv, q + 1)
                v.tensor_copy(K["node_mv"][:, bass.ds(q * (2 * GROUP), 2 * GROUP)], mv[:, k, :]).then_inc(s_st, 1)

            def degree(i, q, k):
                v.wait_ge(s_a[k], i * 16 + 16)
                v.tensor_reduce(dg[:, k, :], ag[:, k, :, D:D + TYPES], AX_X, ALU.add).then_inc(s_dg, 1)
                v.wait_ge(s_dg, q + 1)
                v.tensor_scalar(dm[:, k, :], dg[:, k, :], 1.0, None, ALU.max).then_inc(s_dm, 1)
                v.wait_ge(s_dm, q + 1)
                v.reciprocal(K["inv_deg"][:, bass.ds(q * GROUP, GROUP)], dm[:, k, :]).then_inc(s_di, 1)

            def body(i):
                for k in range(GROUP):
                    q = i * GROUP + k
                    old, ok = q - 2, (k - 2) % GROUP
                    if due(q - 1):
                        new(old, ok % 2)
                    copies(q, k % 2)
                    if due(q - 1):
                        add(i, old, ok, (i if k >= 2 else i - 1) * 16)
                    if due(q):
                        n_input(q - 1, (k - 1) % 2)
                    if due(q - 1):
                        stats(old, ok)
                    degree(i, q, k)
            looped(v, body, GROUPS // GROUP, peel=2)
            new(GROUPS - 2, 0)
            add(0, GROUPS - 2, GROUP - 2, (GROUPS // GROUP - 1) * 16)
            n_input(GROUPS - 1, 1)
            stats(GROUPS - 2, GROUP - 2)
            new(GROUPS - 1, 1)
            add(0, GROUPS - 1, GROUP - 1, (GROUPS // GROUP - 1) * 16)
            stats(GROUPS - 1, GROUP - 1)

        @block.tensor
        def _(pe):
            ident = K["ident"]

            def turn_sums(i, q, k):
                pe.wait_ge(s_a[k], i * 16 + 16)
                if due(q):
                    pe.wait_ge(s_aT, q)
                for j in range(GROUP):
                    ins = pe.transpose(pB[:, j * D:(j + 1) * D], ag[:, k, j, 0:D], ident[:])
                ins.then_inc(s_tb, 1)
                if due(q):
                    pe.wait_ge(s_cT, q)
                for j in range(GROUP):
                    ins = pe.transpose(pC[0:TYPES, j * D:(j + 1) * D], ag[:, k, j, D:D + TYPES], ident[:])
                ins.then_inc(s_tc, 1)

            def back(q, b):
                pe.wait_ge(s_h, q + 1)
                pe.wait_ge(s_hT, q + 2)
                for j in range(GROUP):
                    ins = pe.transpose(pA[:, j * D:(j + 1) * D], hw[:, b, j * D:(j + 1) * D], ident[:])
                ins.then_inc(s_to, 1)

            def gates(q, b):
                pe.wait_ge(s_mT, q + 1)
                pe.wait_ge(s_hT, q + 1)
                for p, g, parts, done, free in ((pR, 0, "ih", s_gr, s_r), (pH, 2, "h", s_gh, s_t),
                                                (pI, 2, "i", s_gi, s_u), (pZ, 1, "ih", s_gz, s_z)):
                    if due(q):
                        pe.wait_ge(free, q)
                    for part in parts:
                        w, rhs = (K["w_ih"], mT) if part == "i" else (K["w_hh"], hT)
                        ins = pe.matmul(p[:], w[:, g * D:(g + 1) * D], rhs[:, b, :],
                                        start=(part == parts[0]), stop=(part == parts[-1]))
                    ins.then_inc(done, 1)

            def turn_rows(q, b):
                pe.wait_ge(s_hn, q + 1)
                if due(q - 1):
                    pe.wait_ge(s_xo, q - 1)
                for j in range(GROUP):
                    ins = pe.transpose(pA[:, j * D:(j + 1) * D], hn[:, b, j * D:(j + 1) * D], ident[:])
                ins.then_inc(s_ta, 1)

            def message(q, b):
                pe.wait_ge(s_aT, q + 1)
                pe.wait_ge(s_cT, q + 1)
                if due(q):
                    pe.wait_ge(s_mT, q)
                pe.matmul(pM[:], K["w_msg"][:], aT[:, b, :], start=True, stop=False)
                pe.matmul(pM[:], K["emb"][:], cT[:, b, :], start=False, stop=True).then_inc(s_m, 1)

            def body(i):
                for k in range(GROUP):
                    q = i * GROUP + k
                    turn_sums(i, q, k)
                    if due(q - 1):
                        back(q - 2, k % 2)
                    if due(q):
                        gates(q - 1, (k - 1) % 2)
                    turn_rows(q, k % 2)
                    message(q, k % 2)
            looped(pe, body, GROUPS // GROUP)
            back(GROUPS - 2, 0)
            gates(GROUPS - 1, 1)
            pe.wait_ge(s_xo, GROUPS - 1)
            pe.wait_ge(s_h, GROUPS)
            for j in range(GROUP):
                ins = pe.transpose(pA[:, j * D:(j + 1) * D], hw[:, 1, j * D:(j + 1) * D], ident[:])
            ins.then_inc(s_to, 1)


def gin_nodes(nc, K, x_in, x_out):
    with ExitStack() as st:
        c = Ctx(nc, st)
        W = GROUP * D
        x = c.sb("gin_x", [P, GROUP, W]); ag = c.sb("gin_sum", [P, GROUP, W])
        rn = c.sb("gin_rn", [P, GROUP, 2 * GROUP]); hn = c.sb("gin_hn", [P, 2, W]); tr = c.sb("gin_t", [P, 2, W])
        tT = c.sb("gin_tT", [P, 2, W]); xo = c.sb("gin_xo", [P, GROUP, W])
        bs = c.sb("gin_bn", [P, 2, GROUP, 6]); mv = c.sb("gin_mv", [P, 2, GROUP, 2])
        sd = c.sb("gin_sd", [P, 2, GROUP]); rs = c.sb("gin_rs", [P, 2, GROUP]); nm = c.sb("gin_nm", [P, 2, GROUP])
        h2 = c.sb("gin_h2", [P, 2, W]); h2T = c.sb("gin_h2T", [P, 2, W])
        xt = c.sb("gin_xt", [P, GROUP, GROUP, XT_W]); ad = c.sb("gin_ad", [P, GROUP, GROUP, HEADS])
        pA = [c.ps(f"gin_pA{b}", [P, W]) for b in range(2)]; pB = [c.ps(f"gin_pB{b}", [P, W]) for b in range(2)]
        pC = [c.ps(f"gin_pC{b}", [P, W]) for b in range(2)]; pD = [c.ps(f"gin_pD{b}", [P, 2, XT_W]) for b in range(2)]
        s_x = [c.sem(f"gin_x_in{k}") for k in range(GROUP)]; s_a = [c.sem(f"gin_sum_in{k}") for k in range(GROUP)]
        s_o = [c.sem(f"gin_x_out{k}") for k in range(GROUP)]; s_xs = [c.sem(f"gin_xt_out{k}") for k in range(GROUP)]
        s_as = [c.sem(f"gin_ad_out{k}") for k in range(GROUP)]
        s_k = c.sem("gin_const"); s_rn = c.sem("gin_rn_done"); s_hn = c.sem("gin_hn_done"); s_tr = c.sem("gin_t_done")
        s_ta = c.sem("gin_t_turned"); s_tT = c.sem("gin_tT_done"); s_mb = c.sem("gin_product"); s_xo = c.sem("gin_xo_done")
        s_bn = c.sem("gin_bn_done"); s_mv = c.sem("gin_mv_done"); s_sd = c.sem("gin_sd_done"); s_rs = c.sem("gin_rs_done")
        s_nm = c.sem("gin_nm_done"); s_h2 = c.sem("gin_h2_done"); s_tc = c.sem("gin_h2_turned")
        s_h2T = c.sem("gin_h2T_done"); s_md = c.sem("gin_xt_product"); s_xt = c.sem("gin_xt_done"); s_ad = c.sem("gin_ad_done")
        block = c.phase()
        xr, ar, xw = rows_by_group(x_in, D), rows_by_group(K["ag"], D), rows_by_group(x_out, D)
        xtw, adw = rows_by_group(K["xt"], XT_W), rows_by_group(K["ad"], HEADS)
        N = GROUPS // GROUP

        @block.sync
        def _(sp):
            def store_x(q, k):
                sp.wait_ge(s_xo, q + 1)
                sp.dma_start(xw[:, bass.ds(q * W, W)], xo[:, k, :]).then_inc(s_o[k], 16)

            def store_xt(q, k):
                sp.wait_ge(s_ad, q + 1)
                sp.dma_start(xtw[:, bass.ds(q * (GROUP * XT_W), GROUP * XT_W)].rearrange("p (j w) -> p j w", w=XT_W),
                             xt[:, k, :, :]).then_inc(s_xs[k], 16)
                sp.dma_start(adw[:, bass.ds(q * (GROUP * HEADS), GROUP * HEADS)].rearrange("p (j w) -> p j w", w=HEADS),
                             ad[:, k, :, :]).then_inc(s_as[k], 16)

            def body(i):
                for k in range(GROUP):
                    q = i * GROUP + k
                    if due(q - GROUP + 1):
                        sp.wait_ge(s_xo, q - GROUP + 1)
                    sp.dma_start(x[:, k, :], xr[:, bass.ds(q * W, W)]).then_inc(s_x[k], 16)
                    sp.dma_start(ag[:, k, :], ar[:, bass.ds(q * W, W)]).then_inc(s_a[k], 16)
                    if due(q - 1):
                        store_x(q - 2, (k - 2) % GROUP)
                    if due(q - 2):
                        store_xt(q - 3, (k - 3) % GROUP)
            looped(sp, body, N)
            for q in range(GROUPS - 2, GROUPS):
                store_x(q, q % GROUP)
            for q in range(GROUPS - 3, GROUPS):
                store_xt(q, q % GROUP)
            for k in range(GROUP):
                sp.wait_ge(s_o[k], 16 * N)
                sp.wait_ge(s_xs[k], 16 * N)
                sp.wait_ge(s_as[k], 16 * N)

        @block.gpsimd
        def _(pool):
            reg = pool.alloc_register("gin_pool")

            def normalise(i, q, k):
                pool.tensor_copy(rn[:, k, :], K["node_rn"][:, bass.ds(q * (2 * GROUP), 2 * GROUP)]).then_inc(s_rn, 1)
                n1 = held(pool, reg, q + 1)
                pool.wait_ge(s_k, 1)
                pool.wait_ge(s_rn, n1)
                n2 = held(pool, reg, i * 16 + 16)
                pool.wait_ge(s_k, 1)
                pool.wait_ge(s_x[k], n2)
                if due(q - 1):
                    n3 = held(pool, reg, q - 1)
                    pool.wait_ge(s_k, 1)
                    pool.wait_ge(s_tr, n3)
                for j in range(GROUP):
                    ins = pool.tensor_scalar(hn[:, k % 2, j * D:(j + 1) * D], x[:, k, j * D:(j + 1) * D],
                                             rn[:, k, 2 * j:2 * j + 1], rn[:, k, 2 * j + 1:2 * j + 2],
                                             ALU.mult, ALU.add)
                ins.then_inc(s_hn, 1)

            def normalise_new(q, k):
                b = k % 2
                n1 = held(pool, reg, q + 1)
                pool.wait_ge(s_k, 1)
                pool.wait_ge(s_nm, n1)
                if due(q - 1):
                    n2 = held(pool, reg, q - 1)
                    pool.wait_ge(s_k, 1)
                    pool.wait_ge(s_tc, n2)
                for j in range(GROUP):
                    ins = pool.tensor_scalar(h2[:, b, j * D:(j + 1) * D], xo[:, k, j * D:(j + 1) * D],
                                             rs[:, b, j:j + 1], nm[:, b, j:j + 1], ALU.mult, ALU.add)
                ins.then_inc(s_h2, 1)

            def body(i):
                for k in range(GROUP):
                    q = i * GROUP + k
                    normalise(i, q, k)
                    if due(q - 1):
                        normalise_new(q - 2, (k - 2) % GROUP)
            looped(pool, body, N)
            normalise_new(GROUPS - 2, GROUP - 2)
            normalise_new(GROUPS - 1, GROUP - 1)

        @block.scalar
        def _(act):
            def turned(q, b):
                act.wait_ge(s_ta, q + 1)
                act.activation(tT[:, b, :], pA[b][:], ACT.Identity, bias=K["v_col"][:, 0:1]).then_inc(s_tT, 1)

            def deviation(q, b):
                act.wait_ge(s_mv, q + 1)
                if due(q - 1):
                    act.wait_ge(s_rs, q - 1)
                act.activation(sd[:, b, :], mv[:, b, :, 1], ACT.Sqrt, bias=K["eps"][:, 0:1]).then_inc(s_sd, 1)

            def turned_new(q, b):
                act.wait_ge(s_tc, q + 1)
                act.activation(h2T[:, b, :], pC[b][:], ACT.Relu).then_inc(s_h2T, 1)

            def body(i):
                for k in range(GROUP):
                    q = i * GROUP + k
                    turned(q, k % 2)
                    if due(q):
                        deviation(q - 1, (k - 1) % 2)
                    if due(q - 2):
                        turned_new(q - 3, (k - 3) % 2)
            looped(act, body, N)
            deviation(GROUPS - 1, 1)
            for q in range(GROUPS - 3, GROUPS):
                turned_new(q, q % 2)

        @block.vector
        def _(v):
            reg = v.alloc_register("gin_vector")
            v.memset(sd[:], 1.0).then_inc(s_k, 1)

            def add_sums(i, q, k):
                v.wait_ge(s_hn, q + 1)
                v.wait_ge(s_a[k], i * 16 + 16)
                if due(q - 1):
                    v.wait_ge(s_ta, q - 1)
                v.scalar_tensor_tensor(tr[:, k % 2, :], hn[:, k % 2, :], 0.0, ag[:, k, :], ALU.max, ALU.add).then_inc(s_tr, 1)

            def add(q, k, stored):
                v.wait_ge(s_mb, q + 1)
                if due(stored):
                    v.wait_ge(s_o[k], stored)
                if due(q - 3):
                    v.wait_ge(s_h2, q - 3)
                v.scalar_tensor_tensor(xo[:, k, :], pB[k % 2][:], 0.0, x[:, k, :], ALU.max, ALU.add).then_inc(s_xo, 1)

            def stats(q, k):
                b = k % 2
                v.wait_ge(s_xo, q + 1)
                for j in range(GROUP):
                    ins = v.bn_stats(bs[:, b, j, :], xo[:, k, j * D:(j + 1) * D])
                ins.then_inc(s_bn, 1)
                if due(q - 1):
                    v.wait_ge(s_nm, q - 1)
                count = held(v, reg, q + 1)
                v.wait_ge(s_k, 1)
                v.wait_ge(s_bn, count)
                v.bn_aggr(mv[:, b, 0, :], bs[:, b, 0, :])
                for j in range(1, GROUP):
                    ins = v.bn_aggr(mv[:, b, j, :], bs[:, b, j, :])
                ins.then_inc(s_mv, 1)

            def scale(q, b):
                v.wait_ge(s_sd, q + 1)
                if due(q - 1):
                    v.wait_ge(s_h2, q - 1)
                v.reciprocal(rs[:, b, :], sd[:, b, :]).then_inc(s_rs, 1)
                v.wait_ge(s_rs, q + 1)
                v.scalar_tensor_tensor(nm[:, b, :], mv[:, b, :, 0], -1.0, rs[:, b, :], ALU.mult, ALU.mult).then_inc(s_nm, 1)

            def rows(q, k, stored):
                v.wait_ge(s_md, q + 1)
                if due(stored):
                    v.wait_ge(s_xs[k], stored)
                    v.wait_ge(s_as[k], stored)
                bias = K["xt_bias"][:].unsqueeze(1).to_broadcast([P, 2, XT_W])
                v.tensor_tensor(xt[:, k, 0:2, :], pD[0][:], bias, ALU.add)
                v.tensor_tensor(xt[:, k, 2:4, :], pD[1][:], bias, ALU.add).then_inc(s_xt, 1)
                v.wait_ge(s_xt, q + 1)
                v.tensor_copy(ad[:, k, :, :], xt[:, k, :, D + HEADS:XT_W]).then_inc(s_ad, 1)

            def body(i):
                for k in range(GROUP):
                    q = i * GROUP + k
                    add_sums(i, q, k)
                    if due(q):
                        add(q - 1, (k - 1) % GROUP, (i if k >= 1 else i - 1) * 16)
                        stats(q - 1, (k - 1) % GROUP)
                    if due(q - 2):
                        rows(q - 3, (k - 3) % GROUP, (i if k >= 3 else i - 1) * 16)
                    if due(q):
                        scale(q - 1, (k - 1) % 2)
            looped(v, body, N, peel=2)
            last = GROUPS - 1
            add(last, GROUP - 1, (N - 1) * 16)
            stats(last, GROUP - 1)
            scale(last, 1)
            for q in range(GROUPS - 3, GROUPS):
                rows(q, q % GROUP, (N - 1) * 16)

        @block.tensor
        def _(pe):
            ident = K["ident"]

            def turn(q, b):
                pe.wait_ge(s_tr, q + 1)
                if due(q - 1):
                    pe.wait_ge(s_tT, q - 1)
                for j in range(GROUP):
                    ins = pe.transpose(pA[b][:, j * D:(j + 1) * D], tr[:, b, j * D:(j + 1) * D], ident[:])
                ins.then_inc(s_ta, 1)

            def product(q, b):
                pe.wait_ge(s_tT, q + 1)
                if due(q - 1):
                    pe.wait_ge(s_xo, q - 1)
                for j in range(GROUP):
                    ins = pe.matmul(pB[b][:, j * D:(j + 1) * D], tT[:, b, j * D:(j + 1) * D], K["w1"][:],
                                    start=True, stop=True)
                ins.then_inc(s_mb, 1)

            def turn_new(q, b):
                pe.wait_ge(s_h2, q + 1)
                if due(q - 1):
                    pe.wait_ge(s_h2T, q - 1)
                for j in range(GROUP):
                    ins = pe.transpose(pC[b][:, j * D:(j + 1) * D], h2[:, b, j * D:(j + 1) * D], ident[:])
                ins.then_inc(s_tc, 1)

            def transform(q, b):
                pe.wait_ge(s_h2T, q + 1)
                if due(q):
                    pe.wait_ge(s_xt, q)
                for j in range(GROUP):
                    ins = pe.matmul(pD[j // 2][:, j % 2, :], h2T[:, b, j * D:(j + 1) * D], K["w_cat"][:],
                                    start=True, stop=True)
                ins.then_inc(s_md, 1)

            def body(i):
                for k in range(GROUP):
                    q = i * GROUP + k
                    turn(q, k % 2)
                    if due(q - 2):
                        turn_new(q - 3, (k - 3) % 2)
                    product(q, k % 2)
                    if due(q - 2):
                        transform(q - 3, (k - 3) % 2)
            looped(pe, body, N)
            for q in range(GROUPS - 3, GROUPS):
                turn_new(q, q % 2)
                transform(q, q % 2)


def gat_gather(nc, K, G):
    g0, sc0, _ = earlier(K, gathers=True, scatters=True)
    with ExitStack() as st:
        c = Ctx(nc, st)
        gi = c.sb("gat_src", [P, RING], I32); di = c.sb("gat_dst", [P, RING], I32)
        g = c.sb("gat_rows", [P, RING, XT_W]); a = c.sb("gat_alpha", [P, RING, HEADS])
        s_start = c.sem("gat_start"); s_gi = c.sem("gat_src_ready"); s_di = c.sem("gat_dst_ready")
        s_g = K["gather_sems"]; s_a = K["scatter_sems"]
        s_cp = c.sem("gat_row_kept"); s_al = c.sem("gat_alpha_kept")
        block = c.phase()

        @block.gpsimd
        def _(pool):
            reg = pool.alloc_register("gat_pool")
            pool.memset(a[:], 0.0).then_inc(s_start, 1)
            pool.wait_ge(s_start, 1)

            def body(i):
                for k in range(RING):
                    if k % HALF == 0:
                        if due(i):
                            for kk in range(k, k + HALF):
                                pool.wait_ge(s_g[kk], g0 + i * 16)
                                pool.wait_ge(s_a[kk], sc0 + i * 16)
                        pool.wait_ge(s_start, 1)
                        pool.tensor_copy(gi[:, k:k + HALF], K["src_idx"][:, bass.ds(i * RING + k, HALF)]).then_inc(s_gi, 1)
                        pool.tensor_copy(di[:, k:k + HALF], K["dst_row"][:, bass.ds(i * RING + k, HALF)]).then_inc(s_di, 1)
                    n = held(pool, reg, i * 2 + k // HALF + 1)
                    pool.wait_ge(s_start, 1)
                    pool.wait_ge(s_gi, n)
                    pool.wait_ge(s_di, n)
                    if due(i):
                        n = held(pool, reg, i * RING - RING + k + 1)
                        pool.wait_ge(s_start, 1)
                        pool.wait_ge(s_cp, n)
                        pool.wait_ge(s_al, n)
                    pool.indirect_dma_start(g[:, k, :], None, K["xt"], bass.IndirectOffsetOnAxis(gi[:, k:k + 1], 0),
                                            bounds_check=NODES_PAD - 1, oob_is_err=False).then_inc(s_g[k], 16)
                    pool.indirect_dma_start(a[:, k, :], None, K["ad"], bass.IndirectOffsetOnAxis(di[:, k:k + 1], 0),
                                            bounds_check=NODES_PAD - 1, oob_is_err=False).then_inc(s_a[k], 16)
            looped(pool, body, STEPS)

        @block.scalar
        def _(act):
            def body(i):
                for k in range(RING):
                    act.wait_ge(s_start, 1)
                    act.wait_ge(s_g[k], g0 + i * 16 + 16)
                    act.copy(G["rows"][:, bass.ds(i * RING + k, 1), :].rearrange("p a w -> p (a w)"),
                             g[:, k, :]).then_inc(s_cp, 1)
            looped(act, body, STEPS)

        @block.vector
        def _(v):
            def body(i):
                for k in range(RING):
                    v.wait_ge(s_g[k], g0 + i * 16 + 16)
                    v.wait_ge(s_a[k], sc0 + i * 16 + 16)
                    v.tensor_tensor(G["alpha"][:, bass.ds(i * RING + k, 1), :].rearrange("p a w -> p (a w)"),
                                    g[:, k, D:D + HEADS], a[:, k, :], ALU.add).then_inc(s_al, 1)
            looped(v, body, STEPS)


def gat_weights(nc, K, G):
    with ExitStack() as st:
        c = Ctx(nc, st)
        pen = c.sb("gat_pen", [P, COLS]); d = c.sb("gat_drop", [P, COLS, HEADS])
        s_v = c.sem("gat_vector"); s_d = c.sem("gat_differences"); s_e = c.sem("gat_exponentials")
        block = c.phase()
        al, top, rescale, w = G["alpha"], G["top"], G["rescale"], G["weight"]

        @block.vector
        def _(v):
            step = stepper(v, s_v)
            step(v.scalar_tensor_tensor(al[:], al[:], 0.2, al[:], ALU.mult, ALU.max))
            step(v.tensor_scalar(pen[:], K["same"][:], -1.0, FAR, ALU.add, ALU.mult))
            for h in range(HEADS):
                step(v.tensor_tensor_scan(top[:, :, h], pen[:], al[:, :, h], -FAR, ALU.add, ALU.max))
            step(v.memset(d[:, 0:1, :], 0.0))
            step(v.tensor_tensor(d[:, 1:COLS, :], top[:, 0:COLS - 1, :], top[:, 1:COLS, :], ALU.subtract))
            step(v.tensor_scalar(d[:], d[:], 0.0, None, ALU.min))
            step(v.tensor_tensor(w[:], al[:], top[:], ALU.subtract))
            v.tensor_copy(G["rows"][:, :, D + HEADS:XT_W], top[:]).then_inc(s_d, 1)
            v.wait_ge(s_e, 2)
            step(v.tensor_tensor(rescale[:], rescale[:], K["same"][:].unsqueeze(2).to_broadcast([P, COLS, HEADS]), ALU.mult))
            for h in range(HEADS):
                step(v.tensor_tensor_scan(al[:, :, h], rescale[:, :, h], w[:, :, h], 0.0, ALU.mult, ALU.add))
            step(v.tensor_copy(G["rows"][:, :, D:D + HEADS], al[:]))

        @block.scalar
        def _(act):
            act.wait_ge(s_d, 1)
            act.activation(rescale[:], d[:], ACT.Exp).then_inc(s_e, 1)
            act.activation(w[:], w[:], ACT.Exp).then_inc(s_e, 1)


def gat_sum(nc, K, G):
    _, sc0, f0 = earlier(K, scatters=True, fixes=True)
    with ExitStack() as st:
        c = Ctx(nc, st)
        si = c.sb("gsum_idx", [P, RING], I32); run = c.sb("gsum_run", [P, RING, WIDE]); tmp = c.sb("gsum_tmp", [P, 2, D])
        wr = c.sb("gsum_rows", [P, RING, D])
        fix = c.sb("gsum_fix", [P, WIDE]); fixed = c.sb("gsum_fixed", [P, WIDE])
        tb = c.sb("gsum_tail_bc", [P, HEADS, P]); mb = c.sb("gsum_top_bc", [P, HEADS, P])
        pen = c.sb("gsum_pen", [P, P]); cm = c.sb("gsum_cmp", [P, HEADS, P]); tm = c.sb("gsum_tail_top", [P, HEADS])
        mt = c.sb("gsum_top", [P, HEADS]); hs = c.sb("gsum_head_scale", [P, HEADS]); dd = c.sb("gsum_diff", [P, HEADS, P])
        ge = c.sb("gsum_factor", [P, HEADS, P])
        pt = c.ps("gsum_pt", [P, HEADS, P]); pm = c.ps("gsum_pm", [P, HEADS, P]); pc = c.ps("gsum_pc", [P, XT_W])
        s_start = c.sem("gsum_fix_cleared"); s_clear = c.sem("gsum_run_cleared"); s_si = c.sem("gsum_idx_ready"); s_w = c.sem("gsum_weighted")
        s_t = c.sem("gsum_rescaled"); s_run = c.sem("gsum_run_done"); s_side = c.sem("gsum_side_done")
        s_sc = K["scatter_sems"]
        s_fx, s_out = K["fix_sems"]; s_v = c.sem("gsum_vector"); s_tb = c.sem("gsum_tail_spread")
        s_pt = c.sem("gsum_tail_turned"); s_mb = c.sem("gsum_top_spread"); s_pm = c.sem("gsum_top_turned")
        s_dd = c.sem("gsum_diff_done"); s_ex = c.sem("gsum_exp_done"); s_ge = c.sem("gsum_factor_done")
        s_pc = c.sem("gsum_carry_done"); s_fd = c.sem("gsum_fixed_done")
        block = c.phase()

        @block.gpsimd
        def _(pool):
            reg = pool.alloc_register("gsum_pool")
            pool.memset(fix[:], 0.0).then_inc(s_start, 1)
            pool.wait_ge(s_start, 1)

            def body(i):
                for k in range(RING):
                    if k % HALF == 0:
                        if due(i):
                            for kk in range(k, k + HALF):
                                pool.wait_ge(s_sc[kk], sc0 + i * 16)
                        pool.wait_ge(s_start, 1)
                        pool.tensor_copy(si[:, k:k + HALF], K["dst_idx"][:, bass.ds(i * RING + k, HALF)]).then_inc(s_si, 1)
                    n = held(pool, reg, i * 2 + k // HALF + 1)
                    pool.wait_ge(s_start, 1)
                    pool.wait_ge(s_si, n)
                    n = held(pool, reg, i * RING + k + 1)
                    pool.wait_ge(s_start, 1)
                    pool.wait_ge(s_run, n)
                    pool.wait_ge(s_side, n)
                    pool.indirect_dma_start(K["ag_wide"], bass.IndirectOffsetOnAxis(si[:, k:k + 1], 0), run[:, k, :], None,
                                            bounds_check=NODES_PAD - 1, oob_is_err=False).then_inc(s_sc[k], 16)
            looped(pool, body, STEPS)
            for k in range(RING):
                pool.wait_ge(s_sc[k], sc0 + 16 * STEPS)
            head = bass.IndirectOffsetOnAxis(K["head_idx"][:, 0:1], 0)
            pool.indirect_dma_start(fix[:], None, K["ag_wide"], head, bounds_check=NODES_PAD - 1,
                                    oob_is_err=False).then_inc(s_fx, 16)
            pool.wait_ge(s_fd, 1)
            pool.indirect_dma_start(K["ag_wide"], head, fixed[:], None, bounds_check=NODES_PAD - 1,
                                    oob_is_err=False).then_inc(s_out, 16)
            pool.wait_ge(s_out, f0 + 16)

        @block.scalar
        def _(act):
            act.wait_ge(s_clear, 1)

            def body(i):
                for k in range(RING):
                    col = i * RING + k
                    act.wait_ge(s_clear, 1)
                    if due(i):
                        act.wait_ge(s_sc[k], sc0 + i * 16)
                    act.copy(run[:, k, D:XT_W], G["rows"][:, bass.ds(col, 1), D:XT_W].rearrange("p a w -> p (a w)")).then_inc(s_side, 1)
            looped(act, body, STEPS)
            act.wait_ge(s_dd, 1)
            act.activation(hs[:], hs[:], ACT.Exp).then_inc(s_ex, 1)
            act.activation(ge[:], dd[:], ACT.Exp, scale=-1.0).then_inc(s_ex, 1)

        @block.vector
        def _(v):
            v.memset(run[:], 0.0).then_inc(s_clear, 1)
            v.wait_ge(s_clear, 1)

            def body(i):
                if due(i):
                    v.wait_ge(s_run, i * RING)
                rows = G["rows"][:, bass.ds(i * RING, RING), 0:D].rearrange("p c (h e) -> p c h e", h=HEADS)
                w = G["weight"][:, bass.ds(i * RING, RING), :].unsqueeze(3).to_broadcast([P, RING, HEADS, HD])
                v.tensor_tensor(wr[:].rearrange("p c (h e) -> p c h e", h=HEADS), rows, w, ALU.mult).then_inc(s_w, 1)
                v.wait_ge(s_w, i + 1)
                for k in range(RING):
                    col = i * RING + k
                    if due(col):
                        v.wait_ge(s_run, col)
                    r = G["rescale"][:, bass.ds(col, 1), :].rearrange("p a h -> p (a h)").unsqueeze(2).to_broadcast([P, HEADS, HD])
                    v.tensor_tensor(tmp[:, k % 2, :].rearrange("p (h e) -> p h e", h=HEADS),
                                    run[:, (k - 1) % RING, 0:D].rearrange("p (h e) -> p h e", h=HEADS), r, ALU.mult).then_inc(s_t, 1)
                    v.wait_ge(s_t, col + 1)
                    if due(i):
                        v.wait_ge(s_sc[k], sc0 + i * 16)
                    v.tensor_tensor(run[:, k, 0:D], tmp[:, k % 2, :], wr[:, k, :], ALU.add).then_inc(s_run, 1)
            looped(v, body, STEPS)

            step = stepper(v, s_v)
            tail = run[:, RING - 1, :]
            v.wait_ge(s_side, COLS)
            step(v.tensor_copy(tm[:], tail[:, D + HEADS:XT_W]))
            v.tensor_copy(tb[:], tm[:].unsqueeze(2).to_broadcast([P, HEADS, P])).then_inc(s_tb, 1)
            step(v.tensor_scalar(pen[:], K["carry_pq"][:], -1.0, FAR, ALU.add, ALU.mult))
            v.wait_ge(s_pt, 1)
            step(v.tensor_tensor(cm[:], pt[:], pen[:].unsqueeze(1).to_broadcast([P, HEADS, P]), ALU.add))
            step(v.tensor_reduce(mt[:], cm[:], AX_X, ALU.max))
            v.wait_ge(s_fx, f0 + 16)
            step(v.tensor_tensor(mt[:], mt[:], fix[:, D + HEADS:XT_W], ALU.max))
            v.tensor_copy(mb[:], mt[:].unsqueeze(2).to_broadcast([P, HEADS, P])).then_inc(s_mb, 1)
            step(v.tensor_tensor(hs[:], fix[:, D + HEADS:XT_W], mt[:], ALU.subtract))
            v.wait_ge(s_pm, 1)
            for h in range(HEADS):
                ins = v.tensor_scalar(dd[:, h, :], pm[:, h, :], tm[:, h:h + 1], 0.0, ALU.subtract, ALU.max)
            ins.then_inc(s_dd, 1)
            v.wait_ge(s_ex, 2)
            v.tensor_tensor(ge[:], ge[:], K["carry_qp"][:].unsqueeze(1).to_broadcast([P, HEADS, P]), ALU.mult).then_inc(s_ge, 1)
            step(v.tensor_tensor(fixed[:, 0:D].rearrange("p (h e) -> p h e", h=HEADS),
                                 fix[:, 0:D].rearrange("p (h e) -> p h e", h=HEADS),
                                 hs[:].unsqueeze(2).to_broadcast([P, HEADS, HD]), ALU.mult))
            step(v.tensor_tensor(fixed[:, D:D + HEADS], fix[:, D:D + HEADS], hs[:], ALU.mult))
            step(v.memset(fixed[:, XT_W:WIDE], 0.0))
            step(v.tensor_copy(fixed[:, D + HEADS:XT_W], mt[:]))
            v.wait_ge(s_pc, 1)
            v.tensor_tensor(fixed[:, 0:D + HEADS], fixed[:, 0:D + HEADS], pc[:, 0:D + HEADS], ALU.add).then_inc(s_fd, 1)

        @block.tensor
        def _(pe):
            pe.wait_ge(s_tb, 1)
            for h in range(HEADS):
                ins = pe.transpose(pt[:, h, :], tb[:, h, :], K["ident"][:])
            ins.then_inc(s_pt, 1)
            pe.wait_ge(s_mb, 1)
            for h in range(HEADS):
                ins = pe.transpose(pm[:, h, :], mb[:, h, :], K["ident"][:])
            ins.then_inc(s_pm, 1)
            pe.wait_ge(s_ge, 1)
            for h in range(HEADS):
                pe.matmul(pc[:, h * HD:(h + 1) * HD], ge[:, h, :], run[:, RING - 1, h * HD:(h + 1) * HD],
                          start=True, stop=True)
                ins = pe.matmul(pc[:, D + h:D + h + 1], ge[:, h, :], run[:, RING - 1, D + h:D + h + 1],
                                start=True, stop=True)
            ins.then_inc(s_pc, 1)


def gat_nodes(nc, K, x_in, x_out):
    with ExitStack() as st:
        c = Ctx(nc, st)
        W = GROUP * D
        x = c.sb("gn_x", [P, GROUP, W]); ag = c.sb("gn_sum", [P, GROUP, GROUP, WIDE])
        dn = c.sb("gn_den", [P, 2, GROUP, HEADS]); rd = c.sb("gn_rden", [P, 2, GROUP, HEADS])
        t = c.sb("gn_t", [P, 2, W]); xo = c.sb("gn_xo", [P, GROUP, W])
        bs = c.sb("gn_bn", [P, GROUP, GROUP, 6]); mv = c.sb("gn_mv", [P, GROUP, 2 * GROUP])
        s_x = [c.sem(f"gn_x_in{k}") for k in range(GROUP)]; s_a = [c.sem(f"gn_sum_in{k}") for k in range(GROUP)]
        s_o = [c.sem(f"gn_out{k}") for k in range(GROUP)]
        s_k = c.sem("gn_const"); s_dn = c.sem("gn_den_done"); s_rd = c.sem("gn_rden_done"); s_t = c.sem("gn_t_done")
        s_xo = c.sem("gn_xo_done"); s_bn = c.sem("gn_bn_done"); s_mv = c.sem("gn_mv_done"); s_st = c.sem("gn_stats_done")
        block = c.phase()
        xr, ar, xw = rows_by_group(x_in, D), rows_by_group(K["ag_wide"], WIDE), rows_by_group(x_out, D)
        N = GROUPS // GROUP

        @block.sync
        def _(sp):
            def store(q, k):
                sp.wait_ge(s_xo, q + 1)
                sp.dma_start(xw[:, bass.ds(q * W, W)], xo[:, k, :]).then_inc(s_o[k], 16)

            def body(i):
                for k in range(GROUP):
                    q = i * GROUP + k
                    if due(q - GROUP + 1):
                        sp.wait_ge(s_xo, q - GROUP + 1)
                    sp.dma_start(x[:, k, :], xr[:, bass.ds(q * W, W)]).then_inc(s_x[k], 16)
                    sp.dma_start(ag[:, k, :, :], ar[:, bass.ds(q * (GROUP * WIDE), GROUP * WIDE)]
                                 .rearrange("p (j w) -> p j w", w=WIDE)).then_inc(s_a[k], 16)
                    if due(q - 2):
                        store(q - 3, (k - 3) % GROUP)
            looped(sp, body, N)
            for q in range(GROUPS - 3, GROUPS):
                store(q, q % GROUP)
            for k in range(GROUP):
                sp.wait_ge(s_o[k], 16 * N)

        @block.gpsimd
        def _(pool):
            def body(i):
                for k in range(GROUP):
                    q = i * GROUP + k
                    pool.wait_ge(s_x[k], i * 16 + 16)
                    pool.wait_ge(s_t, q + 1)
                    if due(i):
                        pool.wait_ge(s_o[k], i * 16)
                        pool.wait_ge(s_bn, q - GROUP + 1)
                    pool.tensor_tensor(xo[:, k, :], x[:, k, :], t[:, k % 2, :], ALU.add).then_inc(s_xo, 1)
            looped(pool, body, N)

        @block.vector
        def _(v):
            reg = v.alloc_register("gn_vector")
            v.memset(mv[:], 0.0).then_inc(s_k, 1)

            def divide(i, q, k):
                b = k % 2
                v.wait_ge(s_a[k], i * 16 + 16)
                v.tensor_scalar(dn[:, b, :, :], ag[:, k, :, D:D + HEADS], 1e-16, None, ALU.add).then_inc(s_dn, 1)
                v.wait_ge(s_dn, q + 1)
                v.reciprocal(rd[:, b, :, :], dn[:, b, :, :]).then_inc(s_rd, 1)
                v.wait_ge(s_rd, q + 1)
                if due(q - 1):
                    v.wait_ge(s_xo, q - 1)
                v.tensor_tensor(t[:, b, :].rearrange("p (j h e) -> p j h e", j=GROUP, h=HEADS),
                                ag[:, k, :, 0:D].rearrange("p j (h e) -> p j h e", h=HEADS),
                                rd[:, b, :, :].unsqueeze(3).to_broadcast([P, GROUP, HEADS, HD]), ALU.mult).then_inc(s_t, 1)

            def stats(q, k):
                v.wait_ge(s_xo, q + 1)
                for j in range(GROUP):
                    ins = v.bn_stats(bs[:, k, j, :], xo[:, k, j * D:(j + 1) * D])
                ins.then_inc(s_bn, 1)
                count = held(v, reg, q + 1)
                v.wait_ge(s_k, 1)
                v.wait_ge(s_bn, count)
                for j in range(GROUP):
                    ins = v.bn_aggr(mv[:, k, 2 * j:2 * j + 2], bs[:, k, j, :])
                ins.then_inc(s_mv, 1)
                v.wait_ge(s_mv, q + 1)
                v.tensor_copy(K["node_mv"][:, bass.ds(q * (2 * GROUP), 2 * GROUP)], mv[:, k, :]).then_inc(s_st, 1)

            def body(i):
                for k in range(GROUP):
                    q = i * GROUP + k
                    divide(i, q, k)
                    if due(q):
                        stats(q - 1, (k - 1) % GROUP)
            looped(v, body, N)
            stats(GROUPS - 1, GROUP - 1)


def sage_first(nc, K, x_in, u_out, y_out):
    with ExitStack() as st:
        c = Ctx(nc, st)
        W = GROUP * D
        x = c.sb("s1_x", [P, GROUP, W]); ag = c.sb("s1_sum", [P, GROUP, W]); rn = c.sb("s1_rn", [P, GROUP, 2 * GROUP])
        hn = c.sb("s1_hn", [P, 2, W]); am = c.sb("s1_mean", [P, 2, W]); hT = c.sb("s1_hT", [P, 2, W])
        aT = c.sb("s1_aT", [P, 2, W]); hA = c.sb("s1_h1", [P, 2, W]); xb = c.sb("s1_xb", [P, GROUP, W])
        uo = c.sb("s1_u", [P, GROUP, W]); yo = c.sb("s1_y", [P, GROUP, W])
        pA = c.ps("s1_pA", [P, W]); pB = c.ps("s1_pB", [P, W]); pC = c.ps("s1_pC", [P, W])
        pU = [c.ps(f"s1_pU{b}", [P, W]) for b in range(2)]; pY = [c.ps(f"s1_pY{b}", [P, W]) for b in range(2)]
        s_x = [c.sem(f"s1_x_in{k}") for k in range(GROUP)]; s_a = [c.sem(f"s1_sum_in{k}") for k in range(GROUP)]
        s_uo = [c.sem(f"s1_u_out{k}") for k in range(GROUP)]; s_yo = [c.sem(f"s1_y_out{k}") for k in range(GROUP)]
        s_k = c.sem("s1_const"); s_rn = c.sem("s1_rn_done"); s_hn = c.sem("s1_hn_done"); s_xb = c.sem("s1_xb_done")
        s_am = c.sem("s1_mean_done"); s_ta = c.sem("s1_h_turned"); s_tb = c.sem("s1_mean_turned"); s_hT = c.sem("s1_hT_done")
        s_aT = c.sem("s1_aT_done"); s_mc = c.sem("s1_product"); s_hA = c.sem("s1_h1_done"); s_md = c.sem("s1_product2")
        s_u = c.sem("s1_u_done"); s_y = c.sem("s1_y_done")
        block = c.phase()
        xr, ar = rows_by_group(x_in, D), rows_by_group(K["ag"], D)
        uw, yw = rows_by_group(u_out, D), rows_by_group(y_out, D)
        N = GROUPS // GROUP

        @block.sync
        def _(sp):
            def store(q, k):
                sp.wait_ge(s_u, q + 1)
                sp.dma_start(uw[:, bass.ds(q * W, W)], uo[:, k, :]).then_inc(s_uo[k], 16)
                sp.wait_ge(s_y, q + 1)
                sp.dma_start(yw[:, bass.ds(q * W, W)], yo[:, k, :]).then_inc(s_yo[k], 16)

            def body(i):
                for k in range(GROUP):
                    q = i * GROUP + k
                    if due(q - GROUP + 1):
                        sp.wait_ge(s_xb, q - GROUP + 1)
                        sp.wait_ge(s_am, q - GROUP + 1)
                    sp.dma_start(x[:, k, :], xr[:, bass.ds(q * W, W)]).then_inc(s_x[k], 16)
                    sp.dma_start(ag[:, k, :], ar[:, bass.ds(q * W, W)]).then_inc(s_a[k], 16)
                    if due(q - 1):
                        store(q - 2, (k - 2) % GROUP)
            looped(sp, body, N)
            for q in range(GROUPS - 2, GROUPS):
                store(q, q % GROUP)
            for k in range(GROUP):
                sp.wait_ge(s_uo[k], 16 * N)
                sp.wait_ge(s_yo[k], 16 * N)

        @block.gpsimd
        def _(pool):
            reg = pool.alloc_register("s1_pool")

            def body(i):
                for k in range(GROUP):
                    q = i * GROUP + k
                    pool.tensor_copy(rn[:, k, :], K["node_rn"][:, bass.ds(q * (2 * GROUP), 2 * GROUP)]).then_inc(s_rn, 1)
                    n1 = held(pool, reg, q + 1)
                    pool.wait_ge(s_k, 1)
                    pool.wait_ge(s_rn, n1)
                    n2 = held(pool, reg, i * 16 + 16)
                    pool.wait_ge(s_k, 1)
                    pool.wait_ge(s_x[k], n2)
                    if due(q - 1):
                        n3 = held(pool, reg, q - 1)
                        pool.wait_ge(s_k, 1)
                        pool.wait_ge(s_ta, n3)
                    for j in range(GROUP):
                        ins = pool.tensor_scalar(hn[:, k % 2, j * D:(j + 1) * D], x[:, k, j * D:(j + 1) * D],
                                                 rn[:, k, 2 * j:2 * j + 1], rn[:, k, 2 * j + 1:2 * j + 2],
                                                 ALU.mult, ALU.add)
                    ins.then_inc(s_hn, 1)
                    if due(q - GROUP + 1):
                        pool.wait_ge(s_y, q - GROUP + 1)
                    pool.tensor_tensor(xb[:, k, :].rearrange("p (j d) -> p j d", d=D),
                                       x[:, k, :].rearrange("p (j d) -> p j d", d=D),
                                       K["b2_bc"][:].unsqueeze(1).to_broadcast([P, GROUP, D]), ALU.add).then_inc(s_xb, 1)
            looped(pool, body, N)

        @block.scalar
        def _(act):
            def body(i):
                for k in range(GROUP):
                    q = i * GROUP + k
                    act.wait_ge(s_ta, q + 1)
                    act.activation(hT[:, k % 2, :], pA[:], ACT.Relu).then_inc(s_hT, 1)
                    if due(q):
                        copy_u(q - 1, (k - 1) % GROUP, (i if k >= 1 else i - 1) * 16)
                    act.wait_ge(s_mc, q + 1)
                    act.activation(hA[:, k % 2, :], pC[:], ACT.Relu, bias=K["b1"][:, 0:1]).then_inc(s_hA, 1)

            def copy_u(q, k, stored):
                act.wait_ge(s_md, q + 1)
                if due(stored):
                    act.wait_ge(s_uo[k], stored)
                act.activation(uo[:, k, :], pU[k % 2][:], ACT.Identity).then_inc(s_u, 1)
            looped(act, body, N, peel=2)
            copy_u(GROUPS - 1, GROUP - 1, (N - 1) * 16)

        @block.vector
        def _(v):
            v.memset(am[:], 0.0).then_inc(s_k, 1)
            v.wait_ge(s_k, 1)

            def add(q, k, stored):
                v.wait_ge(s_md, q + 1)
                v.wait_ge(s_xb, q + 1)
                if due(stored):
                    v.wait_ge(s_yo[k], stored)
                v.tensor_tensor(yo[:, k, :], pY[k % 2][:], xb[:, k, :], ALU.add).then_inc(s_y, 1)

            def body(i):
                for k in range(GROUP):
                    q = i * GROUP + k
                    v.wait_ge(s_a[k], i * 16 + 16)
                    if due(q - 1):
                        v.wait_ge(s_tb, q - 1)
                    v.tensor_tensor(am[:, k % 2, :].rearrange("p (j d) -> p j d", d=D),
                                    ag[:, k, :].rearrange("p (j d) -> p j d", d=D),
                                    K["inv_deg"][:, bass.ds(q * GROUP, GROUP)].unsqueeze(2).to_broadcast([P, GROUP, D]),
                                    ALU.mult).then_inc(s_am, 1)
                    v.wait_ge(s_tb, q + 1)
                    v.tensor_copy(aT[:, k % 2, :], pB[:]).then_inc(s_aT, 1)
                    if due(q):
                        add(q - 1, (k - 1) % GROUP, (i if k >= 1 else i - 1) * 16)
            looped(v, body, N, peel=2)
            add(GROUPS - 1, GROUP - 1, (N - 1) * 16)

        @block.tensor
        def _(pe):
            def second(q, k):
                pe.wait_ge(s_hA, q + 1)
                if due(q - 1):
                    pe.wait_ge(s_u, q - 1)
                    pe.wait_ge(s_y, q - 1)
                for bank, w in ((pU, 0), (pY, D)):
                    for j in range(GROUP):
                        ins = pe.matmul(bank[k % 2][:, j * D:(j + 1) * D], hA[:, k % 2, j * D:(j + 1) * D],
                                        K["w2lr"][:, w:w + D], start=True, stop=True)
                ins.then_inc(s_md, 1)

            def body(i):
                for k in range(GROUP):
                    q = i * GROUP + k
                    b = k % 2
                    pe.wait_ge(s_hn, q + 1)
                    if due(q):
                        pe.wait_ge(s_hT, q)
                    for j in range(GROUP):
                        ins = pe.transpose(pA[:, j * D:(j + 1) * D], hn[:, b, j * D:(j + 1) * D], K["ident"][:])
                    ins.then_inc(s_ta, 1)
                    pe.wait_ge(s_am, q + 1)
                    if due(q):
                        pe.wait_ge(s_aT, q)
                    for j in range(GROUP):
                        ins = pe.transpose(pB[:, j * D:(j + 1) * D], am[:, b, j * D:(j + 1) * D], K["ident"][:])
                    ins.then_inc(s_tb, 1)
                    if due(q):
                        second(q - 1, k - 1)
                    pe.wait_ge(s_hT, q + 1)
                    pe.matmul(pC[:], K["w1r"][:], hT[:, b, :], start=True, stop=False)
                    pe.wait_ge(s_aT, q + 1)
                    pe.matmul(pC[:], K["w1l"][:], aT[:, b, :], start=False, stop=True).then_inc(s_mc, 1)
            looped(pe, body, N)
            second(GROUPS - 1, GROUP - 1)


def sage_second(nc, K, y_in, out):
    with ExitStack() as st:
        c = Ctx(nc, st)
        W = GROUP * D
        y = c.sb("s2_y", [P, GROUP, W]); ag = c.sb("s2_sum", [P, GROUP, W]); t = c.sb("s2_t", [P, 2, W])
        o = c.sb("s2_o", [P, GROUP, W])
        s_x = [c.sem(f"s2_y_in{k}") for k in range(GROUP)]; s_a = [c.sem(f"s2_sum_in{k}") for k in range(GROUP)]
        s_o = [c.sem(f"s2_out{k}") for k in range(GROUP)]; s_t = c.sem("s2_t_done"); s_y = c.sem("s2_o_done")
        block = c.phase()
        yr, ar, ow = rows_by_group(y_in, D), rows_by_group(K["ag"], D), rows_by_group(out, D)
        N = GROUPS // GROUP

        @block.sync
        def _(sp):
            def store(q, k):
                sp.wait_ge(s_y, q + 1)
                sp.dma_start(ow[:, bass.ds(q * W, W)], o[:, k, :]).then_inc(s_o[k], 16)

            def body(i):
                for k in range(GROUP):
                    q = i * GROUP + k
                    if due(q - GROUP + 1):
                        sp.wait_ge(s_y, q - GROUP + 1)
                    sp.dma_start(y[:, k, :], yr[:, bass.ds(q * W, W)]).then_inc(s_x[k], 16)
                    sp.dma_start(ag[:, k, :], ar[:, bass.ds(q * W, W)]).then_inc(s_a[k], 16)
                    if due(q - 2):
                        store(q - 3, (k - 3) % GROUP)
            looped(sp, body, N)
            for q in range(GROUPS - 3, GROUPS):
                store(q, q % GROUP)
            for k in range(GROUP):
                sp.wait_ge(s_o[k], 16 * N)

        @block.vector
        def _(v):
            def body(i):
                for k in range(GROUP):
                    q = i * GROUP + k
                    v.wait_ge(s_a[k], i * 16 + 16)
                    v.tensor_tensor(t[:, k % 2, :].rearrange("p (j d) -> p j d", d=D),
                                    ag[:, k, :].rearrange("p (j d) -> p j d", d=D),
                                    K["inv_deg"][:, bass.ds(q * GROUP, GROUP)].unsqueeze(2).to_broadcast([P, GROUP, D]),
                                    ALU.mult).then_inc(s_t, 1)
                    v.wait_ge(s_t, q + 1)
                    v.wait_ge(s_x[k], i * 16 + 16)
                    if due(i):
                        v.wait_ge(s_o[k], i * 16)
                    v.tensor_tensor(o[:, k, :], y[:, k, :], t[:, k % 2, :], ALU.add).then_inc(s_y, 1)
            looped(v, body, N)


def program(nc, A, out):
    with ExitStack() as st:
        c = Ctx(nc, st)
        K = {"counts": [0, 0, 0]}
        for name, shape in (("ident", [P, P]), ("ones", [P, 1]), ("eps", [P, 1]), ("real", [P, 1]), ("valid", [P, COLS]),
                            ("same", [P, COLS]), ("carry_qp", [P, P]), ("carry_pq", [P, P]),
                            ("node_mv", [P, 2 * TILES]), ("node_rn", [P, 2 * TILES]), ("inv_deg", [P, TILES]),
                            ("emb", [TYPES, D]), ("w_msg", [P, D]), ("w_ih", [P, 3 * D]), ("w_hh", [P, 3 * D]),
                            ("b_rz", [P, 2]), ("b_n", [P, 2]), ("w1", [P, D]), ("vn", [P, 1]), ("v_col", [P, 1]),
                            ("w_cat", [P, XT_W]), ("xt_bias", [P, XT_W]), ("w1l", [P, D]), ("w1r", [P, D]),
                            ("w2lr", [P, 2 * D]), ("b1", [P, 1]), ("b2_bc", [P, D])):
            K[name] = c.sb(name, shape)
        for name in ("src_idx", "dst_idx", "dst_row"):
            K[name] = c.sb(name, [P, COLS], I32)
        K["gather_sems"] = [c.sem(f"gathered{k}") for k in range(RING)]
        K["scatter_sems"] = [c.sem(f"scattered{k}") for k in range(RING)]
        K["fix_sems"] = [c.sem("fix_rows"), c.sem("fix_written")]
        K["head_idx"] = c.sb("head_idx", [P, 1], I32)

        def dram(name, width):
            return nc.dram_tensor(name, [NODES_PAD, width], F32, kind="Internal").ap()
        K["ag_wide"], K["ag"] = dram("sums_wide", WIDE), dram("sums", D)
        K["xt"], K["ad"] = dram("gat_rows_t", XT_W), dram("gat_alpha_t", HEADS)
        x1, x2, x3, u, y = (dram(n, D) for n in ("x1", "x2", "x3", "u_rows", "y_rows"))

        with ExitStack() as s0:
            K["onehot"] = s0.enter_context(nc.sbuf_tensor("onehot", [P, COLS, 16], F32))
            setup(nc, A, K)
            edge_pass(nc, K, "e0", A["x"], K["ag_wide"], WIDE, True, "stats")
        finish_stats(nc, K, "f0")
        gru_nodes(nc, K, A["x"], x1)
        finish_stats(nc, K, "f1")
        edge_pass(nc, K, "e1", x1, K["ag"], D, True, "colsum")
        gin_nodes(nc, K, x1, x2)
        with ExitStack() as s2:
            G = {"rows": s2.enter_context(nc.sbuf_tensor("edge_rows", [P, COLS, XT_W], F32))}
            for name in ("alpha", "top", "rescale", "weight"):
                G[name] = s2.enter_context(nc.sbuf_tensor("edge_" + name, [P, COLS, HEADS], F32))
            gat_gather(nc, K, G)
            gat_weights(nc, K, G)
            gat_sum(nc, K, G)
        gat_nodes(nc, K, x2, x3)
        finish_stats(nc, K, "f3")
        edge_pass(nc, K, "e3", x3, K["ag"], D, True)
        sage_first(nc, K, x3, u, y)
        edge_pass(nc, K, "e4", u, K["ag"], D, False)
        sage_second(nc, K, y, out)


def kernel(**inputs):
    import numpy as np
    import concourse.bacc as bacc
    from concourse.bass_utils import run_bass_kernel_spmd as run

    a = {k: np.asarray(v) for k, v in inputs.items()}
    pad_e = EDGES_PAD - EDGES
    q = np.arange(P)
    e = np.arange(EDGES_PAD)

    def by_partition(v, parts):
        return np.ascontiguousarray(v.reshape(parts, D).T)
    arrays = {
        "x": np.pad(a["x"], ((0, NODES_PAD - NODES), (0, 0))),
        "src": np.pad(a["src"], (0, pad_e)),
        "dst": np.concatenate([np.array([-1], np.int32), a["dst"], np.full(pad_e, PAD_DST, np.int32),
                               np.array([-1], np.int32)]),
        "etype": np.pad(a["edge_type_9"], (0, pad_e)),
        "ident": np.eye(P, dtype=np.float32),
        "iota": np.tile(np.arange(16, dtype=np.float32), (P, 1)),
        "tri": (q[:, None] < q[None, :]).astype(np.float32),
        "tri_t": (q[:, None] > q[None, :]).astype(np.float32),
        "real": (q < NODES // TILES).astype(np.float32)[:, None],
        "valid": (e < EDGES).astype(np.float32).reshape(P, COLS),
        "blk": (q[:, None] // HD == np.arange(HEADS)[None, :]).astype(np.float32),
        "emb": a["L0_gnn_edge_embed"],
        "b_msg": a["L0_gnn_b_msg"],
        "w_msg": a["L0_gnn_W_msg"].T, "w_ih": a["L0_gnn_W_ih"].T, "w_hh": a["L0_gnn_W_hh"].T,
        "b_gru": np.stack([by_partition(a["L0_gnn_b_ih"], 3), by_partition(a["L0_gnn_b_hh"], 3)], 1),
        "w1": a["L1_gnn_W"], "vn": a["L1_gnn_virtual_node"].T,
        "coef": a["L2_gnn_coeffs_t"],
        "lin_w": a["L2_gnn_lin_weight"].transpose(1, 0, 2), "lin_wt": a["L2_gnn_lin_weight"].transpose(2, 0, 1),
        "att_cols": np.stack([a["L2_gnn_att_src"].reshape(3, D).T, a["L2_gnn_att_dst"].reshape(3, D).T,
                              a["L2_gnn_lin_bias"].reshape(3, D).T], 2).transpose(0, 1, 2),
        "w1l": a["L3_gnn_W1_l"].T, "w1r": a["L3_gnn_W1_r"].T,
        "w2lr": np.concatenate([a["L3_gnn_W2_l"].T, a["L3_gnn_W2_r"].T], 1),
        "b1": a["L3_gnn_b1"][:, None], "b2": a["L3_gnn_b2"],
    }
    arrays = {"in_" + k: np.ascontiguousarray(v) for k, v in arrays.items()}
    nc = bacc.Bacc("TRN2", target_bir_lowering=False, num_devices=1)
    A = {k[3:]: nc.dram_tensor(k, v.shape, mybir.dt.from_np(v.dtype), kind="ExternalInput").ap()
         for k, v in arrays.items()}
    out = nc.dram_tensor("out_rows", [NODES_PAD, D], F32, kind="ExternalOutput").ap()
    program(nc, A, out)
    r = run(nc, [arrays], core_ids=[0])
    return r.results[0]["out_rows"][:NODES]
```

```python
import concourse.bass as bass
from concourse import mybir
from concourse.alu_op_type import AluOpType as ALU
from contextlib import ExitStack

F32 = mybir.dt.float32
I32 = mybir.dt.int32
BF16 = mybir.dt.bfloat16
ACT = mybir.ActivationFunctionType
AX_X = mybir.AxisListType.X

P = 128
D = 128
NODES = 50000
EDGES = 25000
TILES = 400
NODES_PAD = P * TILES
GROUP = 4
GROUPS = TILES // GROUP
COLS = -(-EDGES // P)
EDGES_PAD = P * COLS
RING = 14
HALF = RING // 2
STEPS = COLS // RING
TYPES = 9
WIDE = 144
SLOTS = WIDE - D
SPLIT = 3
STACK = 2 * SPLIT * SLOTS
HEADS = 4
HD = D // HEADS
XT_W = D + 2 * HEADS
PAD_DST = NODES_PAD + 4096
SKIP = 1.0e5
FAR = 1.0e30
EPS = 1e-5
CLEAR = 3200


def held(eng, reg, value):
    if isinstance(value, int):
        return value
    eng.reg_add(reg, value, 0)
    return eng.snap(reg)


def due(value):
    return not isinstance(value, int) or value > 0


def looped(eng, body, count, peel=1, last=False):
    for i in range(peel):
        body(i)
    with eng.Fori(peel, count - 1 if last else count) as i:
        body(i)
    if last:
        body(count - 1)


class Ctx:
    def __init__(self, nc, stack):
        self.nc, self.stack, self.sems = nc, stack, []

    def sb(self, name, shape, dt=F32):
        return self.stack.enter_context(self.nc.sbuf_tensor(name, shape, dt))

    def ps(self, name, shape, dt=F32):
        return self.stack.enter_context(self.nc.psum_tensor(name, shape, dt))

    def sem(self, name):
        s = self.stack.enter_context(self.nc.semaphore(name))
        self.sems.append(s)
        return s

    def phase(self):
        self.stack.push(lambda kind, *_: self.clear() if kind is None else None)
        return self.stack.enter_context(self.nc.Block())

    def clear(self):
        with self.nc.Block() as block:
            @block.gpsimd
            def _(pool):
                for s in self.sems:
                    pool.sem_clear(s)


def stepper(eng, sem):
    count = [0]

    def step(ins):
        count[0] += 1
        ins.then_inc(sem, 1)
        eng.wait_ge(sem, count[0])
    return step


def earlier(K, **added):
    at = dict(K["counts"])
    for name, count in added.items():
        K["counts"][name] += count
    return at


def rows_by_group(table, width):
    return table.rearrange("(p j) d -> p (j d)", p=P)


def setup(nc, A, K):
    with ExitStack() as st:
        c = Ctx(nc, st)
        cur = c.sb("cur", [P, COLS]); prv = c.sb("prv", [P, COLS]); nxt = c.sb("nxt", [P, COLS])
        cur_i = c.sb("cur_i", [P, COLS], I32); prv_i = c.sb("prv_i", [P, COLS], I32)
        nxt_i = c.sb("nxt_i", [P, COLS], I32); typ_i = c.sb("typ_i", [P, COLS], I32)
        typ = c.sb("typ", [P, COLS]); is_end = c.sb("is_end", [P, COLS]); tmp = c.sb("tmp", [P, COLS])
        iota = c.sb("iota16", [P, 16]); tri = c.sb("tri", [P, P]); tri_t = c.sb("tri_t", [P, P])
        cur_bc = c.sb("cur_bc", [P, 2, P]); small = c.sb("small", [P, 8])
        lw = c.sb("lw", [P, 3, D]); lwt = c.sb("lwt", [P, 3, D]); w2 = c.sb("w2", [P, D])
        coef = c.sb("coef", [P, 3]); cols = c.sb("att_cols", [P, 3, 3]); acol = c.sb("acol", [P, 3])
        blk = c.sb("blk", [P, HEADS]); ab = c.sb("ab", [P, XT_W]); bias_bc = c.sb("bias_bc", [P, P])
        bm = c.sb("bm", [P, 1]); emb = c.sb("emb_cols", [P, STACK]); w_msg = c.sb("w_msg", [P, D])
        w_ih = c.sb("w_ih", [P, 3 * D]); part = c.sb("part_mask", [STACK, SPLIT]); pick = c.sb("pick_rows", [STACK, P])
        part_b = c.sb("emb_part", [STACK, 3 * D], BF16); part_f = c.sb("emb_part_f", [STACK, 3 * D])
        rest = c.sb("emb_rest", [STACK, 3 * D]); chosen = c.sb("emb_chosen", [STACK, 3 * D])
        bb = c.sb("bb", [P, 2, 3])
        pt = c.ps("pt", [P, 512]); pu = c.ps("pu", [P, 512]); pk = c.ps("pk", [P, 8])
        pw = c.ps("pw", [P, 512]); pe_ = c.ps("pe", [P, 512])
        head = c.sb("head_cols", [P, COLS]); one = c.sb("one_cols", [P, COLS]); count = c.sb("edge_count", [P, COLS])
        deg = c.sb("edge_deg", [P, COLS]); spare = c.sb("spare_rows", [P, COLS])
        s_ld = c.sem("setup_loaded"); s_z = c.sem("zero_ready"); s_cm = c.sem("carry_mask_ready")
        s_cc = c.sem("carry_count_ready"); s_v = c.sem("setup_vector"); s_pe = c.sem("setup_tensor"); s_bc = c.sem("setup_ready")
        s_em = c.sem("setup_emb_ready"); s_gw = c.sem("setup_gru_weights")
        block = c.phase()
        loads = [
            (cur_i, A["dst"][1:1 + EDGES_PAD].rearrange("(p c) -> p c", p=P)),
            (prv_i, A["dst"][0:EDGES_PAD].rearrange("(p c) -> p c", p=P)),
            (nxt_i, A["dst"][2:2 + EDGES_PAD].rearrange("(p c) -> p c", p=P)),
            (K["src_idx"], A["src"].rearrange("(p c) -> p c", p=P)),
            (typ_i, A["etype"].rearrange("(p c) -> p c", p=P)),
            (iota, A["iota"]), (tri, A["tri"]), (tri_t, A["tri_t"]), (K["ident"], A["ident"]),
            (lw, A["lin_w"]), (lwt, A["lin_wt"]), (coef, A["coef"].partition_broadcast(P)),
            (cols, A["att_cols"]), (blk, A["blk"]), (bm, A["b_msg"]),
            (emb, A["emb"]), (w_msg, A["w_msg"]), (w_ih, A["w_ih"]), (part, A["part"]), (pick, A["pick"]), (K["w_hh"], A["w_hh"]),
            (bb, A["b_gru"]), (K["w1"], A["w1"]), (K["vn"], A["vn"]), (K["w1l"], A["w1l"]),
            (K["w1r"], A["w1r"]), (K["w2lr"], A["w2lr"]), (K["b1"], A["b1"]),
            (K["b2_bc"], A["b2"].partition_broadcast(P)), (K["real"], A["real"]), (K["valid"], A["valid"]),
            (spare, A["spare"]),
        ]

        @block.sync
        def _(sp):
            for t, src in loads:
                sp.dma_start(t[:], src).then_inc(s_ld, 16)
            sp.wait_ge(s_z, 1)
            for k in range(TILES * WIDE // CLEAR):
                sp.dma_start(rows_by_group(K["ag_wide"], WIDE)[:, k * CLEAR:(k + 1) * CLEAR],
                             K["zero"][:]).then_inc(K["wide_cleared"], 16)

        @block.vector
        def _(v):
            step = stepper(v, s_v)
            v.memset(K["zero"][:], 0.0).then_inc(s_z, 1)
            step(v.memset(K["ones"][:], 1.0))
            step(v.memset(K["eps"][:], EPS))
            step(v.memset(one[:], 1.0))
            v.wait_ge(s_ld, 16 * len(loads))
            for f, i in ((cur, cur_i), (prv, prv_i), (nxt, nxt_i), (typ, typ_i)):
                step(v.tensor_copy(f[:], i[:]))
            step(v.tensor_tensor(K["same"][:], prv[:], cur[:], ALU.is_equal))
            step(v.tensor_tensor(tmp[:], nxt[:], cur[:], ALU.is_equal))
            step(v.tensor_scalar(is_end[:], tmp[:], -1.0, 1.0, ALU.mult, ALU.add))
            step(v.tensor_scalar(tmp[:], cur[:], -SKIP, None, ALU.add))
            step(v.tensor_tensor(tmp[:], tmp[:], is_end[:], ALU.mult))
            step(v.tensor_scalar(K["dst_idx"][:], tmp[:], SKIP, None, ALU.add))
            step(v.tensor_copy(K["dst_row"][:], cur_i[:]))
            step(v.tensor_scalar(head[:], cur[:], cur[:, 0:1], K["same"][:, 0:1], ALU.is_equal, ALU.mult))
            step(v.tensor_tensor(K["head_end"][:], head[:], is_end[:], ALU.mult))
            step(v.tensor_reduce(small[:, 1:2], K["head_end"][:], AX_X, ALU.max))
            step(v.tensor_tensor(is_end[:], is_end[:], K["valid"][:], ALU.mult))
            step(v.tensor_tensor(cur[:], cur[:], spare[:], ALU.subtract))
            step(v.tensor_tensor(tmp[:], cur[:], is_end[:], ALU.mult))
            step(v.tensor_tensor(K["add_idx"][:], tmp[:], spare[:], ALU.add))
            step(v.tensor_tensor(is_end[:], is_end[:], K["head_end"][:], ALU.subtract))
            step(v.tensor_scalar(is_end[:], is_end[:], 0.0, None, ALU.max))
            step(v.tensor_tensor(tmp[:], cur[:], is_end[:], ALU.mult))
            step(v.tensor_tensor(K["add_idx_whole"][:], tmp[:], spare[:], ALU.add))
            step(v.tensor_tensor(small[:, 7:8], small[:, 1:2], K["valid"][:, 0:1], ALU.mult))
            step(v.tensor_tensor(small[:, 7:8], small[:, 7:8], cur[:, 0:1], ALU.mult))
            step(v.tensor_tensor(K["head_add_idx"][:], small[:, 7:8], spare[:, 0:1], ALU.add))
            step(v.tensor_tensor(cur[:], cur[:], spare[:], ALU.add))
            step(v.tensor_tensor_scan(count[:], K["same"][:], one[:], 0.0, ALU.mult, ALU.add))
            step(v.tensor_scalar(small[:, 2:3], cur[:, 0:1], -SKIP, None, ALU.add))
            step(v.tensor_tensor(small[:, 3:4], small[:, 1:2], small[:, 2:3], ALU.mult))
            step(v.tensor_scalar(K["head_idx"][:], small[:, 3:4], SKIP, None, ALU.add))
            step(v.tensor_scalar(typ[:], typ[:], 0.0, float(TYPES - 1), ALU.max, ALU.min))
            step(v.tensor_tensor(K["onehot"][:], typ[:].unsqueeze(2).to_broadcast([P, COLS, 16]),
                                 iota[:].unsqueeze(1).to_broadcast([P, COLS, 16]), ALU.is_equal))
            step(v.tensor_copy(cur_bc[:, 0, :], cur[:, 0:1].to_broadcast([P, P])))
            step(v.tensor_copy(cur_bc[:, 1, :], cur[:, COLS - 1:COLS].to_broadcast([P, P])))
            for o, w in ((w2[:], lw), (K["w_cat"][:, 0:D], lwt), (acol[:], cols)):
                step(v.tensor_scalar(o, w[:, 0, :], coef[:, 0:1], None, ALU.mult))
                for b in (1, 2):
                    step(v.scalar_tensor_tensor(o, w[:, b, :], coef[:, b:b + 1], o, ALU.mult, ALU.add))
            step(v.tensor_copy(ab[:, 0:D], K["ident"][:]))
            step(v.tensor_scalar(ab[:, D:D + HEADS], blk[:], acol[:, 0:1], None, ALU.mult))
            step(v.tensor_scalar(ab[:, D + HEADS:XT_W], blk[:], acol[:, 1:2], None, ALU.mult))
            step(v.tensor_copy(bias_bc[:], acol[:, 2:3].to_broadcast([P, P])))
            v.tensor_scalar(emb[:], emb[:], bm[:, 0:1], None, ALU.add).then_inc(s_em, 1)
            step(v.tensor_tensor(K["b_rz"][:], bb[:, 0, 0:2], bb[:, 1, 0:2], ALU.add))
            step(v.tensor_copy(K["b_n"][:], bb[:, :, 2]))
            v.tensor_copy(small[:, 4:5], small[:, 3:4]).then_inc(s_bc, 1)
            v.wait_ge(s_pe, 1)
            step(v.scalar_tensor_tensor(K["carry_qp"][:], pt[:, 0:P], cur[:, COLS - 1:COLS], tri[:],
                                        ALU.is_equal, ALU.mult))
            v.tensor_copy(small[:, 5:6], count[:, COLS - 1:COLS]).then_inc(s_cm, 1)
            step(v.scalar_tensor_tensor(K["carry_pq"][:], pt[:, P:2 * P], cur[:, 0:1], tri_t[:],
                                        ALU.is_equal, ALU.mult))
            step(v.tensor_copy(K["w_cat"][:, D:XT_W], pu[:, 0:2 * HEADS]))
            v.wait_ge(s_gw, 1)
            step(v.tensor_copy(K["w_in"][:], pw[:, 0:3 * D]))

            def parts(out, values, width):
                step(v.tensor_copy(rest[:, 0:width], values))
                for n in range(SPLIT):
                    step(v.tensor_copy(part_b[:, 0:width], rest[:, 0:width]))
                    step(v.tensor_copy(part_f[:, 0:width], part_b[:, 0:width]))
                    if n == 0:
                        step(v.tensor_scalar(chosen[:, 0:width], part_f[:, 0:width], part[:, 0:1], None, ALU.mult))
                    else:
                        step(v.scalar_tensor_tensor(chosen[:, 0:width], part_f[:, 0:width], part[:, n:n + 1],
                                                    chosen[:, 0:width], ALU.mult, ALU.add))
                    step(v.tensor_tensor(rest[:, 0:width], rest[:, 0:width], part_f[:, 0:width], ALU.subtract))
                step(v.tensor_copy(out, chosen[:, 0:width]))
            parts(K["emb_in"][:], pe_[0:STACK, 0:3 * D], 3 * D)
            parts(K["xt_bias"][:], pu[0:STACK, 2 * HEADS:2 * HEADS + XT_W], XT_W)
            step(v.tensor_copy(K["one_row"][:], pick[:]))
            v.wait_ge(s_cc, 1)
            step(v.tensor_copy(small[:, 6:7], pk[:, 0:1]))
            step(v.scalar_tensor_tensor(deg[:], head[:], small[:, 6:7], count[:], ALU.mult, ALU.add))
            step(v.reciprocal(K["inv_edge"][:], deg[:]))
            step(v.tensor_tensor(tmp[:], K["inv_edge"][:], K["head_end"][:], ALU.mult))
            step(v.tensor_reduce(K["inv_head"][:], tmp[:], AX_X, ALU.max))

        @block.tensor
        def _(pe):
            pe.wait_ge(s_bc, 1)
            pe.transpose(pt[:, 0:P], cur_bc[:, 0, :], K["ident"][:])
            pe.transpose(pt[:, P:2 * P], cur_bc[:, 1, :], K["ident"][:])
            pe.matmul(pu[:, 0:2 * HEADS], w2[:], ab[:, D:XT_W], start=True, stop=True)
            pe.matmul(pu[:, 2 * HEADS:2 * HEADS + XT_W], bias_bc[:], ab[:],
                      start=True, stop=True).then_inc(s_pe, 1)
            pe.wait_ge(s_em, 1)
            pe.matmul(pw[:, 0:3 * D], w_msg[:], w_ih[:], start=True, stop=True)
            pe.matmul(pe_[0:STACK, 0:3 * D], emb[:], w_ih[:], start=True, stop=True).then_inc(s_gw, 1)
            pe.wait_ge(s_cm, 1)
            pe.matmul(pk[:, 0:1], K["carry_qp"][:], small[:, 5:6], start=True, stop=True).then_inc(s_cc, 1)


def edge_pass(nc, K, tag, table, sums, width, norm, node_stream=None, mean=False, into=False):
    onehot = width > D
    at = earlier(K, gathered=16 * STEPS, scattered=16 * STEPS, fix_rows=0 if into else 16, fix_written=16)
    g0, sc0 = at["gathered"], at["scattered"]
    with ExitStack() as st:
        c = Ctx(nc, st)
        n = lambda s: f"{tag}_{s}"
        gi = c.sb(n("gather_idx"), [P, RING], I32)
        si = c.sb(n("scatter_idx"), [P, RING], I32)
        g = c.sb(n("rows"), [P, RING, D])
        h = c.sb(n("norm_rows"), [P, RING, D]) if norm else g
        run = c.sb(n("run"), [P, RING, width])
        res = c.sb(n("mean"), [P, RING, width]) if mean else run
        s_res = c.sem(n("mean_done")) if mean else None
        s_hot = c.sem(n("counts_done")) if onehot else None
        bs = c.sb(n("bn"), [P, RING, 6]); mv = c.sb(n("mean_var"), [P, RING, 2])
        sd = c.sb(n("std"), [P, RING]); rs = c.sb(n("rstd"), [P, RING]); nm = c.sb(n("shift"), [P, RING])
        fix = c.sb(n("fix"), [P, width]); fixed = c.sb(n("fixed"), [P, width])
        carry = c.ps(n("carry"), [P, width])
        s_start = c.sem(n("fix_cleared")); s_clear = c.sem(n("run_cleared")); clears = 1 + (node_stream == "colsum")
        s_gi = c.sem(n("gather_idx_ready")); s_si = c.sem(n("scatter_idx_ready"))
        s_g = K["gather_sems"]
        s_sc = K["scatter_sems"]
        s_bn = c.sem(n("bn_done")); s_mv = c.sem(n("mean_var_done")); s_sd = c.sem(n("std_done"))
        s_rs = c.sem(n("rstd_done")); s_nm = c.sem(n("shift_done")); s_h = c.sem(n("normed"))
        s_run = c.sem(n("run_done")); s_fx, s_out = K["fix_sems"]; s_ca = c.sem(n("carry_done"))
        s_fd = c.sem(n("fixed_done"))
        stream = node_stream is not None
        if stream:
            PER = 7
            REST = GROUPS - STEPS * PER
            nx = c.sb(n("node_rows"), [P, PER, GROUP * D])
            s_nx = [c.sem(n(f"node_loaded{m}")) for m in range(PER)]
            s_nu = c.sem(n("node_used"))
        if node_stream == "stats":
            nbn = c.sb(n("node_bn"), [P, PER, GROUP, 6]); nmv = c.sb(n("node_mv"), [P, PER, GROUP * 2])
            s_nb = c.sem(n("node_bn_done")); s_nmv = c.sem(n("node_mv_done"))
        if node_stream == "colsum":
            nr = c.sb(n("node_rn"), [P, PER, GROUP * 2]); nh = c.sb(n("node_h"), [P, PER, GROUP * D])
            acc = c.sb(n("edge_acc"), [P, D]); row = c.sb(n("sum_row"), [1, GROUP * D])
            prow = c.ps(n("node_sum"), [1, GROUP * D]); pcol = c.ps(n("sum_col"), [P, 8])
            s_nr = c.sem(n("node_rn_done")); s_nh = c.sem(n("node_h_done")); s_np = c.sem(n("node_summed"))
            s_ac = c.sem(n("edge_acc_done")); s_row = c.sem(n("row_done")); s_col = c.sem(n("col_done"))
            s_v = c.sem(n("v_done"))
        block = c.phase()

        if stream:
            @block.sync
            def _(sp):
                rows = rows_by_group(table, D)

                def load(i, m):
                    q = i * PER + m
                    if due(q - PER + 1):
                        if node_stream == "stats":
                            sp.wait_ge(s_nu, q - PER + 1)
                        else:
                            sp.wait_ge(s_nh, (q - PER + 1) * GROUP)
                    sp.dma_start(nx[:, m, :], rows[:, bass.ds(q * (GROUP * D), GROUP * D)]).then_inc(s_nx[m], 16)

                def body(i):
                    for m in range(PER):
                        load(i, m)
                looped(sp, body, STEPS)
                for m in range(REST):
                    load(STEPS, m)

        @block.gpsimd
        def _(pool):
            reg = pool.alloc_register(n("pool_count"))
            idx, head_idx = (K["add_idx"], K["head_add_idx"]) if into else (K["dst_idx"], K["head_idx"])
            pool.memset(fix[:], 0.0).then_inc(s_start, 1)
            pool.wait_ge(s_start, 1)

            def gather_index(i, half):
                a = half * HALF
                pool.tensor_copy(gi[:, a:a + HALF], K["src_idx"][:, bass.ds(i * RING + a, HALF)]).then_inc(s_gi, 1)

            def gather(i, k):
                if norm:
                    used, count = s_h, i * RING + k + 1 - RING
                else:
                    used, count = s_run, i * RING + k + 1 - RING
                idx_count = held(pool, reg, i * 2 + k // HALF + 1)
                pool.wait_ge(s_start, 1)
                pool.wait_ge(s_gi, idx_count)
                if due(count):
                    count = held(pool, reg, count)
                    pool.wait_ge(s_start, 1)
                    pool.wait_ge(used, count)
                pool.indirect_dma_start(g[:, k, :], None, table,
                                        bass.IndirectOffsetOnAxis(gi[:, k:k + 1], 0),
                                        bounds_check=NODES_PAD - 1, oob_is_err=False).then_inc(s_g[k], 16)

            for half in (0, 1):
                gather_index(0, half)
            for k in range(RING):
                gather(0, k)

            def body(i):
                last = isinstance(i, int) and i == STEPS - 1
                for k in range(RING):
                    if k % HALF == 0:
                        half = k // HALF
                        if not last:
                            for kk in range(k, k + HALF):
                                pool.wait_ge(s_g[kk], g0 + i * 16 + 16)
                            gather_index(i + 1, half)
                        if due(i):
                            for kk in range(k, k + HALF):
                                pool.wait_ge(s_sc[kk], sc0 + i * 16)
                        pool.wait_ge(s_start, 1)
                        pool.tensor_copy(si[:, k:k + HALF],
                                         idx[:, bass.ds(i * RING + k, HALF)]).then_inc(s_si, 1)
                    if not last:
                        gather(i + 1, k)
                    idx_count = held(pool, reg, i * 2 + k // HALF + 1)
                    pool.wait_ge(s_start, 1)
                    pool.wait_ge(s_si, idx_count)
                    if isinstance(i, int) and i == 0 and k == 0 and onehot:
                        pool.wait_ge(K["wide_cleared"], 16 * (TILES * WIDE // CLEAR))
                    run_count = held(pool, reg, i * RING + k + 1)
                    pool.wait_ge(s_start, 1)
                    if onehot:
                        pool.wait_ge(s_hot, run_count)
                    pool.wait_ge(s_res if mean else s_run, run_count)
                    if into:
                        if k >= HALF or due(i):
                            turn = held(pool, reg, sc0 + (i * 16 + 16 if k >= HALF else i * 16))
                            pool.wait_ge(s_start, 1)
                            pool.wait_ge(s_sc[(k - HALF) % RING], turn)
                    pool.indirect_dma_start(sums, bass.IndirectOffsetOnAxis(si[:, k:k + 1], 0),
                                            res[:, k, :], None, bounds_check=NODES_PAD - 1,
                                            oob_is_err=into, compute_op=ALU.add if into else ALU.bypass).then_inc(s_sc[k], 16)
            looped(pool, body, STEPS, last=True)
            for k in range(RING):
                pool.wait_ge(s_sc[k], sc0 + 16 * STEPS)
            head = bass.IndirectOffsetOnAxis(head_idx[:, 0:1], 0)
            if not into:
                pool.indirect_dma_start(fix[:], None, sums, head, bounds_check=NODES_PAD - 1,
                                        oob_is_err=False).then_inc(s_fx, 16)
            pool.wait_ge(s_fd, 1)
            pool.indirect_dma_start(sums, head, fixed[:], None, bounds_check=NODES_PAD - 1,
                                    oob_is_err=into, compute_op=ALU.add if into else ALU.bypass).then_inc(s_out, 16)
            pool.wait_ge(s_out, at["fix_written"] + 16)

        @block.vector
        def _(v):
            reg = v.alloc_register(n("vector_count"))
            v.memset(run[:], 0.0).then_inc(s_clear, 1)
            if node_stream == "colsum":
                v.memset(acc[:], 0.0).then_inc(s_clear, 1)
            v.wait_ge(s_clear, clears)
            v.wait_ge(s_start, 1)

            def node_group(i, m):
                q = i * PER + m
                v.wait_ge(s_nx[m], i * 16 + 16)
                for j in range(GROUP):
                    ins = v.bn_stats(nbn[:, m, j, :], nx[:, m, j * D:(j + 1) * D])
                ins.then_inc(s_nb, 1)
                count = held(v, reg, q + 1)
                v.wait_ge(s_clear, clears)
                v.wait_ge(s_nb, count)
                for j in range(GROUP):
                    ins = v.bn_aggr(nmv[:, m, 2 * j:2 * j + 2], nbn[:, m, j, :])
                ins.then_inc(s_nmv, 1)
                v.wait_ge(s_nmv, q + 1)
                v.tensor_copy(K["node_mv"][:, bass.ds(q * (2 * GROUP), 2 * GROUP)], nmv[:, m, :]).then_inc(s_nu, 1)

            def body(i):
                for half in (0, 1):
                    a = half * HALF
                    u = i * 2 + half
                    if norm:
                        for k in range(a, a + HALF):
                            v.wait_ge(s_g[k], g0 + i * 16 + 16)
                            ins = v.bn_stats(bs[:, k, :], g[:, k, :])
                        ins.then_inc(s_bn, 1)
                        count = held(v, reg, u + 1)
                        v.wait_ge(s_clear, clears)
                        v.wait_ge(s_bn, count)
                        for k in range(a, a + HALF):
                            ins = v.bn_aggr(mv[:, k, :], bs[:, k, :])
                        ins.then_inc(s_mv, 1)
                        v.wait_ge(s_sd, u + 1)
                        v.reciprocal(rs[:, a:a + HALF], sd[:, a:a + HALF]).then_inc(s_rs, 1)
                        v.wait_ge(s_rs, u + 1)
                        v.scalar_tensor_tensor(nm[:, a:a + HALF], mv[:, a:a + HALF, 0], -1.0,
                                               rs[:, a:a + HALF], ALU.mult, ALU.mult).then_inc(s_nm, 1)
                    if node_stream == "stats":
                        for m in (range(0, 4) if half == 0 else range(4, PER)):
                            node_group(i, m)
                    for k in range(a, a + HALF):
                        col = i * RING + k
                        if norm:
                            v.wait_ge(s_h, col + 1)
                        else:
                            v.wait_ge(s_g[k], g0 + i * 16 + 16)
                        if due(col):
                            v.wait_ge(s_run, col)
                        if due(i) and not mean:
                            v.wait_ge(s_sc[k], sc0 + i * 16)
                        same = K["same"][:, bass.ds(col, 1)]
                        prev = run[:, (k - 1) % RING, :]
                        v.scalar_tensor_tensor(run[:, k, 0:D], prev[:, 0:D], same, h[:, k, :],
                                               ALU.mult, ALU.add).then_inc(s_run, 1)
                        if onehot:
                            if due(col):
                                v.wait_ge(s_hot, col)
                            v.scalar_tensor_tensor(run[:, k, D:width], prev[:, D:width], same,
                                                   K["onehot"][:, bass.ds(col, 1), :].rearrange("p a t -> p (a t)"),
                                                   ALU.mult, ALU.add).then_inc(s_hot, 1)
                        if mean:
                            v.wait_ge(s_run, col + 1)
                            if due(i):
                                v.wait_ge(s_sc[k], sc0 + i * 16)
                            v.tensor_scalar(res[:, k, :], run[:, k, :], K["inv_edge"][:, bass.ds(col, 1)], None,
                                            ALU.mult).then_inc(s_res, 1)
                        if node_stream == "colsum":
                            if due(col):
                                v.wait_ge(s_ac, col)
                            v.scalar_tensor_tensor(acc[:], h[:, k, :], K["valid"][:, bass.ds(col, 1)], acc[:],
                                                   ALU.mult, ALU.add).then_inc(s_ac, 1)
            looped(v, body, STEPS)
            if node_stream == "stats":
                for m in range(REST):
                    node_group(STEPS, m)
            if node_stream == "colsum":
                v.wait_ge(s_np, GROUPS)
                v.tensor_copy(row[:], prow[:]).then_inc(s_row, 1)
                v.wait_ge(s_col, 1)
                v.scalar_tensor_tensor(K["v_col"][:], pcol[:, 0:1], 1.0 / NODES, K["vn"][:],
                                       ALU.mult, ALU.add).then_inc(s_v, 1)
            v.wait_ge(s_ca, 1)
            if not into:
                v.wait_ge(s_fx, at["fix_rows"] + 16)
            if mean:
                v.scalar_tensor_tensor(fixed[:], carry[:], K["inv_head"][:, 0:1], fix[:],
                                       ALU.mult, ALU.add).then_inc(s_fd, 1)
            else:
                v.tensor_tensor(fixed[:], fix[:], carry[:], ALU.add).then_inc(s_fd, 1)

        if norm:
            @block.scalar
            def _(act):
                reg = act.alloc_register(n("act_count"))

                def node_group(i, m):
                    q = i * PER + m
                    if due(q - PER + 1):
                        act.wait_ge(s_np, q - PER + 1)
                    act.wait_ge(s_clear, clears)
                    act.copy(nr[:, m, :], K["node_rn"][:, bass.ds(q * (2 * GROUP), 2 * GROUP)]).then_inc(s_nr, 1)
                    act.wait_ge(s_nx[m], i * 16 + 16)
                    act.wait_ge(s_nr, q + 1)
                    for j in range(GROUP):
                        ins = act.activation(nh[:, m, j * D:(j + 1) * D], nx[:, m, j * D:(j + 1) * D], ACT.Relu,
                                             bias=nr[:, m, 2 * j + 1:2 * j + 2], scale=nr[:, m, 2 * j:2 * j + 1])
                        ins.then_inc(s_nh, 1)

                def body(i):
                    for half in (0, 1):
                        a = half * HALF
                        u = i * 2 + half
                        act.wait_ge(s_mv, u + 1)
                        if due(u - 1):
                            act.wait_ge(s_rs, u - 1)
                        act.activation(sd[:, a:a + HALF], mv[:, a:a + HALF, 1], ACT.Sqrt,
                                       bias=K["eps"][:, 0:1]).then_inc(s_sd, 1)
                        if node_stream == "colsum":
                            for m in (range(0, 4) if half == 0 else range(4, PER)):
                                node_group(i, m)
                        act.wait_ge(s_nm, u + 1)
                        for k in range(a, a + HALF):
                            if due(i):
                                act.wait_ge(s_run, (i - 1) * RING + k + 1)
                                if node_stream == "colsum":
                                    act.wait_ge(s_ac, (i - 1) * RING + k + 1)
                            act.activation(h[:, k, :], g[:, k, :], ACT.Relu, bias=nm[:, k:k + 1],
                                           scale=rs[:, k:k + 1]).then_inc(s_h, 1)
                looped(act, body, STEPS)
                if node_stream == "colsum":
                    for m in range(REST):
                        node_group(STEPS, m)

        @block.tensor
        def _(pe):
            if node_stream == "colsum":
                def node_group(i, m):
                    q = i * PER + m
                    pe.wait_ge(s_nh, q * GROUP + GROUP)
                    start = isinstance(i, int) and i == 0 and m == 0
                    end = isinstance(i, int) and i == STEPS and m == REST - 1
                    pe.matmul(prow[:], K["real"][:, 0:1], nh[:, m, :], start=start, stop=end,
                              skip_group_check=True).then_inc(s_np, 1)

                def body(i):
                    for m in range(PER):
                        node_group(i, m)
                looped(pe, body, STEPS)
                for m in range(REST):
                    node_group(STEPS, m)
                pe.wait_ge(s_row, 1)
                pe.wait_ge(s_ac, COLS)
                for j in range(GROUP):
                    pe.matmul(pcol[:, 0:1], row[0:1, j * D:(j + 1) * D], K["ones"][0:1, 0:1],
                              start=(j == 0), stop=False)
                pe.matmul(pcol[:, 0:1], acc[:], K["ones"][:, 0:1], start=False, stop=True).then_inc(s_col, 1)
            pe.wait_ge(s_run, COLS)
            if onehot:
                pe.wait_ge(s_hot, COLS)
            pe.matmul(carry[:], K["carry_qp"][:], run[:, RING - 1, :], start=True, stop=True).then_inc(s_ca, 1)


def finish_stats(nc, K, tag):
    with ExitStack() as st:
        c = Ctx(nc, st)
        sd = c.sb(f"{tag}_sd", [P, TILES])
        s_sd = c.sem(f"{tag}_sd_done"); s_v = c.sem(f"{tag}_rstd_done")
        block = c.phase()
        mv = K["node_mv"][:].rearrange("p (j t) -> p j t", t=2)
        rn = K["node_rn"][:].rearrange("p (j t) -> p j t", t=2)

        @block.scalar
        def _(act):
            act.activation(sd[:], mv[:, :, 1], ACT.Sqrt, bias=K["eps"][:, 0:1]).then_inc(s_sd, 1)

        @block.vector
        def _(v):
            v.wait_ge(s_sd, 1)
            v.reciprocal(rn[:, :, 0], sd[:]).then_inc(s_v, 1)
            v.wait_ge(s_v, 1)
            v.scalar_tensor_tensor(rn[:, :, 1], mv[:, :, 0], -1.0, rn[:, :, 0], ALU.mult, ALU.mult)



def gru_nodes(nc, K, x_in, x_out):
    with ExitStack() as st:
        c = Ctx(nc, st)
        x = c.sb("gru_x", [P, GROUP, GROUP * D]); ag = c.sb("gru_sum", [P, GROUP, GROUP, WIDE])
        rn = c.sb("gru_rn", [P, GROUP, 2 * GROUP])
        hn = c.sb("gru_hn", [P, 2, GROUP * D]); hT = c.sb("gru_hT", [P, 2, GROUP * D])
        aT = c.sb("gru_aT", [P, 2, GROUP * D]); cT = c.sb("gru_cT", [STACK, 2, GROUP * D], BF16)
        cb = c.sb("gru_counts", [P, 2, GROUP, STACK], BF16); ident_b = c.sb("gru_ident", [P, P], BF16)
        r = c.sb("gru_r", [P, 2, GROUP * D]); z = c.sb("gru_z", [P, 2, GROUP * D])
        t = c.sb("gru_t", [P, 2, GROUP * D]); u = c.sb("gru_u", [P, 2, GROUP * D])
        nn = c.sb("gru_n", [P, 2, GROUP * D]); d = c.sb("gru_d", [P, 2, GROUP * D])
        e = c.sb("gru_e", [P, 2, GROUP * D]); hw = c.sb("gru_new", [P, 2, GROUP * D])
        xo = c.sb("gru_xo", [P, GROUP, GROUP * D])
        bs = c.sb("gru_bn", [P, GROUP, GROUP, 6]); mv = c.sb("gru_mv", [P, GROUP, 2 * GROUP])
        pA, pB, pO, pR, pZ, pI, pH = (c.ps(f"gru_p{k}", [P, GROUP * D]) for k in "ABORZIH")
        pC = c.ps("gru_pC", [STACK, GROUP * D], BF16)
        s_x = [c.sem(f"gru_x_in{k}") for k in range(GROUP)]
        s_a = [c.sem(f"gru_sum_in{k}") for k in range(GROUP)]
        s_o = [c.sem(f"gru_out{k}") for k in range(GROUP)]
        s_rn = c.sem("gru_rn_done"); s_hn = c.sem("gru_hn_done"); s_ta = c.sem("gru_h_transposed")
        s_tb = c.sem("gru_sum_transposed"); s_tc = c.sem("gru_counts_transposed")
        s_hT = c.sem("gru_hT_done"); s_aT = c.sem("gru_aT_done"); s_cT = c.sem("gru_cT_done")
        s_hi = c.sem("gru_counts_high"); s_lo = c.sem("gru_counts_low")
        s_gr = c.sem("gru_gate_r"); s_gh = c.sem("gru_gate_h"); s_gi = c.sem("gru_gate_i"); s_gz = c.sem("gru_gate_z")
        s_r = c.sem("gru_r_done"); s_z = c.sem("gru_z_done"); s_t = c.sem("gru_t_done"); s_u = c.sem("gru_u_done")
        s_n = c.sem("gru_n_done"); s_d = c.sem("gru_d_done"); s_e = c.sem("gru_e_done"); s_h = c.sem("gru_new_done")
        s_to = c.sem("gru_new_transposed"); s_xo = c.sem("gru_xo_done"); s_bn = c.sem("gru_bn_done")
        s_mv = c.sem("gru_mv_done"); s_st = c.sem("gru_stats_done")
        s_k = c.sem("gru_const")
        zero = c.sb("gru_zero", [P, GROUP * D]); s_zero = c.sem("gru_zero_ready"); s_clr = c.sem("gru_cleared")
        block = c.phase()
        xr, ar, xw = rows_by_group(x_in, D), rows_by_group(K["ag_wide"], WIDE), rows_by_group(x_out, D)
        clear = rows_by_group(K["ag"], D)
        W = GROUP * D

        @block.sync
        def _(sp):
            def store(q, k):
                sp.wait_ge(s_xo, q + 1)
                sp.dma_start(xw[:, bass.ds(q * W, W)], xo[:, k, :]).then_inc(s_o[k], 16)

            def body(i):
                for k in range(GROUP):
                    q = i * GROUP + k
                    if due(q - GROUP + 1):
                        sp.wait_ge(s_xo, q - GROUP + 1)
                        sp.wait_ge(s_hn, q - GROUP + 1)
                    sp.dma_start(x[:, k, :], xr[:, bass.ds(q * W, W)]).then_inc(s_x[k], 16)
                    if due(q - GROUP + 1):
                        sp.wait_ge(s_tb, q - GROUP + 1)
                        sp.wait_ge(s_lo, q - GROUP + 1)
                    sp.dma_start(ag[:, k, :, :], ar[:, bass.ds(q * (GROUP * WIDE), GROUP * WIDE)]
                                 .rearrange("p (j w) -> p j w", w=WIDE)).then_inc(s_a[k], 16)
                    if not due(q):
                        sp.wait_ge(s_zero, 1)
                    sp.dma_start(clear[:, bass.ds(q * W, W)], zero[:]).then_inc(s_clr, 16)
                    if due(q - 2):
                        store(q - 3, (k - 3) % GROUP)
            looped(sp, body, GROUPS // GROUP)
            for q in range(GROUPS - 3, GROUPS):
                store(q, q % GROUP)
            for k in range(GROUP):
                sp.wait_ge(s_o[k], 16 * (GROUPS // GROUP))
            sp.wait_ge(s_clr, 16 * GROUPS)

        @block.gpsimd
        def _(pool):
            reg = pool.alloc_register("gru_pool")

            def normalise(i, q, k):
                if k == 0:
                    if due(i):
                        n0 = held(pool, reg, i * GROUP)
                        pool.wait_ge(s_k, 1)
                        pool.wait_ge(s_hn, n0)
                    pool.tensor_copy(rn[:].rearrange("p k c -> p (k c)"),
                                     K["node_rn"][:, bass.ds(i * (2 * GROUP * GROUP), 2 * GROUP * GROUP)]).then_inc(s_rn, 1)
                    n1 = held(pool, reg, i + 1)
                    pool.wait_ge(s_k, 1)
                    pool.wait_ge(s_rn, n1)
                n2 = held(pool, reg, i * 16 + 16)
                pool.wait_ge(s_k, 1)
                pool.wait_ge(s_x[k], n2)
                if due(q - 1):
                    n3 = held(pool, reg, q - 1)
                    pool.wait_ge(s_k, 1)
                    pool.wait_ge(s_ta, n3)
                for j in range(GROUP):
                    ins = pool.tensor_scalar(hn[:, k % 2, j * D:(j + 1) * D], x[:, k, j * D:(j + 1) * D],
                                             rn[:, k, 2 * j:2 * j + 1], rn[:, k, 2 * j + 1:2 * j + 2],
                                             ALU.mult, ALU.add)
                ins.then_inc(s_hn, 1)

            def mix(q, b):
                pool.wait_ge(s_n, q + 1)
                pool.tensor_tensor(d[:, b, :], hT[:, b, :], nn[:, b, :], ALU.subtract).then_inc(s_d, 1)
                pool.wait_ge(s_d, q + 1)
                pool.wait_ge(s_z, q + 1)
                if due(q - 1):
                    pool.wait_ge(s_h, q - 1)
                pool.tensor_tensor(e[:, b, :], d[:, b, :], z[:, b, :], ALU.mult).then_inc(s_e, 1)

            def body(i):
                for k in range(GROUP):
                    q = i * GROUP + k
                    normalise(i, q, k)
                    if due(q - 1):
                        mix(q - 2, k % 2)
            looped(pool, body, GROUPS // GROUP)
            mix(GROUPS - 2, 0)
            mix(GROUPS - 1, 1)

        @block.scalar
        def _(act):
            def gates(q, b):
                act.wait_ge(s_gr, q + 1)
                act.activation(r[:, b, :], pR[:], ACT.Sigmoid, bias=K["b_rz"][:, 0:1]).then_inc(s_r, 1)
                act.wait_ge(s_u, q + 1)
                if due(q - 1):
                    act.wait_ge(s_h, q - 1)
                act.activation(nn[:, b, :], u[:, b, :], ACT.Tanh, bias=K["b_n"][:, 0:1]).then_inc(s_n, 1)
                act.wait_ge(s_gz, q + 1)
                if due(q - 1):
                    act.wait_ge(s_e, q - 1)
                act.activation(z[:, b, :], pZ[:], ACT.Sigmoid, bias=K["b_rz"][:, 1:2]).then_inc(s_z, 1)

            def copies(q, b):
                act.wait_ge(s_tb, q + 1)
                if due(q - 1):
                    act.wait_ge(s_gz, q - 1)
                act.activation(aT[:, b, :], pB[:], ACT.Identity).then_inc(s_aT, 1)
                act.wait_ge(s_ta, q + 1)
                if due(q - 1):
                    act.wait_ge(s_d, q - 1)
                act.activation(hT[:, b, :], pA[:], ACT.Relu).then_inc(s_hT, 1)

            def body(i):
                for k in range(GROUP):
                    q = i * GROUP + k
                    copies(q, k % 2)
                    if due(q):
                        gates(q - 1, (k - 1) % 2)
            looped(act, body, GROUPS // GROUP)
            gates(GROUPS - 1, 1)

        @block.vector
        def _(v):
            reg = v.alloc_register("gru_vector")
            v.tensor_copy(ident_b[:], K["ident"][:]).then_inc(s_k, 1)
            v.memset(zero[:], 0.0).then_inc(s_zero, 1)

            def split(i, q, k):
                counts = ag[:, k, :, D:WIDE].unsqueeze(2).to_broadcast([P, GROUP, SPLIT, SLOTS])
                high, low = (cb[:, k % 2, :, a:a + STACK // 2].rearrange("p j (n t) -> p j n t", t=SLOTS)
                             for a in (0, STACK // 2))
                v.wait_ge(s_a[k], i * 16 + 16)
                if due(q - 1):
                    v.wait_ge(s_tc, q - 1)
                v.tensor_copy(high, counts).then_inc(s_hi, 1)
                v.wait_ge(s_hi, q + 1)
                v.tensor_tensor(low, counts, high, ALU.subtract).then_inc(s_lo, 1)

            def new(q, b):
                v.wait_ge(s_e, q + 1)
                if due(q - 1):
                    v.wait_ge(s_to, q - 1)
                v.tensor_tensor(hw[:, b, :], e[:, b, :], nn[:, b, :], ALU.add).then_inc(s_h, 1)

            def copy_counts(q, b):
                v.wait_ge(s_tc, q + 1)
                if due(q - 1):
                    v.wait_ge(s_gz, q - 1)
                v.tensor_copy(cT[:, b, :], pC[:]).then_inc(s_cT, 1)

            def add(i, q, k, stored):
                v.wait_ge(s_to, q + 1)
                if due(stored):
                    v.wait_ge(s_o[k], stored)
                v.tensor_tensor(xo[:, k, :], x[:, k, :], pO[:], ALU.add).then_inc(s_xo, 1)

            def n_input(q, b):
                v.wait_ge(s_r, q + 1)
                v.wait_ge(s_gh, q + 1)
                v.scalar_tensor_tensor(t[:, b, :], pH[:], K["b_n"][:, 1:2], r[:, b, :], ALU.add, ALU.mult).then_inc(s_t, 1)
                v.wait_ge(s_t, q + 1)
                v.wait_ge(s_gi, q + 1)
                if due(q - 1):
                    v.wait_ge(s_n, q - 1)
                v.tensor_tensor(u[:, b, :], t[:, b, :], pI[:], ALU.add).then_inc(s_u, 1)

            def stats(q, k):
                v.wait_ge(s_xo, q + 1)
                for j in range(GROUP):
                    ins = v.bn_stats(bs[:, k, j, :], xo[:, k, j * D:(j + 1) * D])
                ins.then_inc(s_bn, 1)
                count = held(v, reg, q + 1)
                v.wait_ge(s_k, 1)
                v.wait_ge(s_bn, count)
                for j in range(GROUP):
                    ins = v.bn_aggr(mv[:, k, 2 * j:2 * j + 2], bs[:, k, j, :])
                ins.then_inc(s_mv, 1)
                v.wait_ge(s_mv, q + 1)
                v.tensor_copy(K["node_mv"][:, bass.ds(q * (2 * GROUP), 2 * GROUP)], mv[:, k, :]).then_inc(s_st, 1)

            def body(i):
                for k in range(GROUP):
                    q = i * GROUP + k
                    old, ok = q - 2, (k - 2) % GROUP
                    split(i, q, k)
                    if due(q - 1):
                        new(old, ok % 2)
                    copy_counts(q, k % 2)
                    if due(q - 1):
                        add(i, old, ok, (i if k >= 2 else i - 1) * 16)
                    if due(q):
                        n_input(q - 1, (k - 1) % 2)
                    if due(q - 1):
                        stats(old, ok)
            looped(v, body, GROUPS // GROUP, peel=2)
            new(GROUPS - 2, 0)
            add(0, GROUPS - 2, GROUP - 2, (GROUPS // GROUP - 1) * 16)
            n_input(GROUPS - 1, 1)
            stats(GROUPS - 2, GROUP - 2)
            new(GROUPS - 1, 1)
            add(0, GROUPS - 1, GROUP - 1, (GROUPS // GROUP - 1) * 16)
            stats(GROUPS - 1, GROUP - 1)

        @block.tensor
        def _(pe):
            ident = K["ident"]

            def turn_sums(i, q, k):
                pe.wait_ge(s_a[k], i * 16 + 16)
                if due(q):
                    pe.wait_ge(s_aT, q)
                for j in range(GROUP):
                    ins = pe.transpose(pB[:, j * D:(j + 1) * D], ag[:, k, j, 0:D], ident[:])
                ins.then_inc(s_tb, 1)

            def turn_counts(q, b):
                pe.wait_ge(s_lo, q + 1)
                if due(q):
                    pe.wait_ge(s_cT, q)
                for j in range(GROUP):
                    ins = pe.transpose(pC[:, j * D:(j + 1) * D], cb[:, b, j, :], ident_b[:])
                ins.then_inc(s_tc, 1)

            def back(q, b):
                pe.wait_ge(s_h, q + 1)
                if due(q):
                    pe.wait_ge(s_xo, q)
                for j in range(GROUP):
                    ins = pe.transpose(pO[:, j * D:(j + 1) * D], hw[:, b, j * D:(j + 1) * D], ident[:])
                ins.then_inc(s_to, 1)

            def gates(q, b, more=True):
                pe.wait_ge(s_aT, q + 1)
                pe.wait_ge(s_cT, q + 1)
                pe.wait_ge(s_hT, q + 1)
                for p, g, parts, done, free in ((pR, 0, "hic", s_gr, s_r), (pH, 2, "h", s_gh, s_t),
                                                (pI, 2, "ic", s_gi, s_u), (pZ, 1, "hic", s_gz, s_z)):
                    if due(q):
                        pe.wait_ge(free, q)
                    for part in parts:
                        w, rhs = {"h": (K["w_hh"], hT), "i": (K["w_in"], aT), "c": (K["emb_in"], cT)}[part]
                        ins = pe.matmul(p[:], w[:, g * D:(g + 1) * D], rhs[:, b, :],
                                        start=(part == parts[0]), stop=(part == parts[-1]))
                    ins.then_inc(done, 1)
                    if p is pR and more:
                        turn_counts(q + 1, 1 - b)
                    if p is pH and due(q):
                        back(q - 1, 1 - b)

            def turn_rows(q, b):
                pe.wait_ge(s_hn, q + 1)
                if due(q):
                    pe.wait_ge(s_hT, q)
                for j in range(GROUP):
                    ins = pe.transpose(pA[:, j * D:(j + 1) * D], hn[:, b, j * D:(j + 1) * D], ident[:])
                ins.then_inc(s_ta, 1)

            def body(i):
                for k in range(GROUP):
                    q = i * GROUP + k
                    turn_sums(i, q, k)
                    turn_rows(q, k % 2)
                    if due(q):
                        gates(q - 1, (k - 1) % 2)
                    else:
                        turn_counts(q, k % 2)
            looped(pe, body, GROUPS // GROUP)
            gates(GROUPS - 1, 1, more=False)
            back(GROUPS - 1, 1)


def gin_nodes(nc, K, x_in, x_out):
    with ExitStack() as st:
        c = Ctx(nc, st)
        W = GROUP * D
        x = c.sb("gin_x", [P, GROUP, W]); ag = c.sb("gin_sum", [P, GROUP, W])
        rn = c.sb("gin_rn", [P, GROUP, 2 * GROUP]); hn = c.sb("gin_hn", [P, 2, W]); tr = c.sb("gin_t", [P, 2, W])
        tT = c.sb("gin_tT", [P, 2, W]); xo = c.sb("gin_xo", [P, GROUP, W])
        bs = c.sb("gin_bn", [P, 2, GROUP, 6]); mv = c.sb("gin_mv", [P, 2, GROUP, 2])
        sd = c.sb("gin_sd", [P, 2, GROUP]); rs = c.sb("gin_rs", [P, GROUP, GROUP]); nm = c.sb("gin_nm", [P, GROUP, GROUP])
        h2 = c.sb("gin_h2", [P, 2, W]); h2T = c.sb("gin_h2T", [P, 2, W])
        xt = c.sb("gin_xt", [P, GROUP, GROUP, XT_W]); ad = c.sb("gin_ad", [P, GROUP, GROUP, HEADS])
        pA = [c.ps(f"gin_pA{b}", [P, W]) for b in range(2)]; pB = [c.ps(f"gin_pB{b}", [P, W]) for b in range(2)]
        pC = [c.ps(f"gin_pC{b}", [P, W]) for b in range(2)]; pD = [c.ps(f"gin_pD{b}", [P, 2, XT_W]) for b in range(2)]
        s_x = [c.sem(f"gin_x_in{k}") for k in range(GROUP)]; s_a = [c.sem(f"gin_sum_in{k}") for k in range(GROUP)]
        s_o = [c.sem(f"gin_x_out{k}") for k in range(GROUP)]; s_xs = [c.sem(f"gin_xt_out{k}") for k in range(GROUP)]
        s_as = [c.sem(f"gin_ad_out{k}") for k in range(GROUP)]
        s_k = c.sem("gin_const"); s_rn = c.sem("gin_rn_done"); s_hn = c.sem("gin_hn_done"); s_tr = c.sem("gin_t_done")
        s_ta = c.sem("gin_t_turned"); s_tT = c.sem("gin_tT_done"); s_mb = c.sem("gin_product"); s_xo = c.sem("gin_xo_done")
        s_bn = c.sem("gin_bn_done"); s_mv = c.sem("gin_mv_done"); s_sd = c.sem("gin_sd_done"); s_rs = c.sem("gin_rs_done")
        s_nm = c.sem("gin_nm_done"); s_h2 = c.sem("gin_h2_done"); s_tc = c.sem("gin_h2_turned")
        s_h2T = c.sem("gin_h2T_done"); s_md = c.sem("gin_xt_product"); s_xt = c.sem("gin_xt_done"); s_ad = c.sem("gin_ad_done")
        block = c.phase()
        xr, ar, xw = rows_by_group(x_in, D), rows_by_group(K["ag"], D), rows_by_group(x_out, D)
        xtw, adw = rows_by_group(K["xt"], XT_W), rows_by_group(K["ad"], HEADS)
        N = GROUPS // GROUP

        @block.sync
        def _(sp):
            def store_x(q, k):
                sp.wait_ge(s_xo, q + 1)
                sp.dma_start(xw[:, bass.ds(q * W, W)], xo[:, k, :]).then_inc(s_o[k], 16)

            def store_xt(q, k):
                sp.wait_ge(s_ad, q + 1)
                sp.dma_start(xtw[:, bass.ds(q * (GROUP * XT_W), GROUP * XT_W)].rearrange("p (j w) -> p j w", w=XT_W),
                             xt[:, k, :, :]).then_inc(s_xs[k], 16)
                sp.dma_start(adw[:, bass.ds(q * (GROUP * HEADS), GROUP * HEADS)].rearrange("p (j w) -> p j w", w=HEADS),
                             ad[:, k, :, :]).then_inc(s_as[k], 16)

            def body(i):
                for k in range(GROUP):
                    q = i * GROUP + k
                    if due(q - GROUP + 1):
                        sp.wait_ge(s_xo, q - GROUP + 1)
                    sp.dma_start(x[:, k, :], xr[:, bass.ds(q * W, W)]).then_inc(s_x[k], 16)
                    sp.dma_start(ag[:, k, :], ar[:, bass.ds(q * W, W)]).then_inc(s_a[k], 16)
                    if due(q - 2):
                        store_x(q - 3, (k - 3) % GROUP)
                    if due(q - 6):
                        store_xt(q - 7, (k - 7) % GROUP)
            looped(sp, body, N, peel=2)
            for q in range(GROUPS - 3, GROUPS):
                store_x(q, q % GROUP)
            for q in range(GROUPS - 7, GROUPS):
                store_xt(q, q % GROUP)
            for k in range(GROUP):
                sp.wait_ge(s_o[k], 16 * N)
                sp.wait_ge(s_xs[k], 16 * N)
                sp.wait_ge(s_as[k], 16 * N)

        @block.gpsimd
        def _(pool):
            reg = pool.alloc_register("gin_pool")

            def normalise(i, q, k):
                if k == 0:
                    if due(i):
                        n0 = held(pool, reg, i * GROUP)
                        pool.wait_ge(s_k, 1)
                        pool.wait_ge(s_hn, n0)
                    pool.tensor_copy(rn[:].rearrange("p k c -> p (k c)"),
                                     K["node_rn"][:, bass.ds(i * (2 * GROUP * GROUP), 2 * GROUP * GROUP)]).then_inc(s_rn, 1)
                    n1 = held(pool, reg, i + 1)
                    pool.wait_ge(s_k, 1)
                    pool.wait_ge(s_rn, n1)
                n2 = held(pool, reg, i * 16 + 16)
                pool.wait_ge(s_k, 1)
                pool.wait_ge(s_x[k], n2)
                if due(q - 1):
                    n3 = held(pool, reg, q - 1)
                    pool.wait_ge(s_k, 1)
                    pool.wait_ge(s_tr, n3)
                for j in range(GROUP):
                    ins = pool.tensor_scalar(hn[:, k % 2, j * D:(j + 1) * D], x[:, k, j * D:(j + 1) * D],
                                             rn[:, k, 2 * j:2 * j + 1], rn[:, k, 2 * j + 1:2 * j + 2],
                                             ALU.mult, ALU.add)
                ins.then_inc(s_hn, 1)

            def normalise_new(q, k):
                b = k % 2
                n1 = held(pool, reg, q + 1)
                pool.wait_ge(s_k, 1)
                pool.wait_ge(s_nm, n1)
                if due(q - 1):
                    n2 = held(pool, reg, q - 1)
                    pool.wait_ge(s_k, 1)
                    pool.wait_ge(s_tc, n2)
                for j in range(GROUP):
                    ins = pool.tensor_scalar(h2[:, b, j * D:(j + 1) * D], xo[:, k, j * D:(j + 1) * D],
                                             rs[:, k, j:j + 1], nm[:, k, j:j + 1], ALU.mult, ALU.add)
                ins.then_inc(s_h2, 1)

            def body(i):
                for k in range(GROUP):
                    q = i * GROUP + k
                    normalise(i, q, k)
                    if due(q - 2):
                        normalise_new(q - 3, (k - 3) % GROUP)
            looped(pool, body, N, peel=2)
            for q in range(GROUPS - 3, GROUPS):
                normalise_new(q, q % GROUP)

        @block.scalar
        def _(act):
            def turned(q, b):
                act.wait_ge(s_ta, q + 1)
                act.activation(tT[:, b, :], pA[b][:], ACT.Identity, bias=K["v_col"][:, 0:1]).then_inc(s_tT, 1)

            def deviation(q, b):
                act.wait_ge(s_mv, q + 1)
                if due(q - 1):
                    act.wait_ge(s_rs, q - 1)
                act.activation(sd[:, b, :], mv[:, b, :, 1], ACT.Sqrt, bias=K["eps"][:, 0:1]).then_inc(s_sd, 1)

            def turned_new(q, b):
                act.wait_ge(s_tc, q + 1)
                act.activation(h2T[:, b, :], pC[b][:], ACT.Relu).then_inc(s_h2T, 1)

            def rows(q, k, stored):
                act.wait_ge(s_md, q + 1)
                if due(stored):
                    act.wait_ge(s_xs[k], stored)
                    act.wait_ge(s_as[k], stored)
                act.activation(xt[:, k, 0:2, :], pD[0][:], ACT.Identity)
                act.activation(xt[:, k, 2:4, :], pD[1][:], ACT.Identity).then_inc(s_xt, 1)
                act.wait_ge(s_xt, q + 1)
                act.copy(ad[:, k, :, :], xt[:, k, :, D + HEADS:XT_W]).then_inc(s_ad, 1)

            def body(i):
                for k in range(GROUP):
                    q = i * GROUP + k
                    turned(q, k % 2)
                    if due(q):
                        deviation(q - 1, (k - 1) % 2)
                    if due(q - 3):
                        turned_new(q - 4, k % 2)
                    if due(q - 4):
                        rows(q - 5, (k - 5) % GROUP, (i - 1 if k >= 1 else i - 2) * 16)
            looped(act, body, N, peel=3)
            deviation(GROUPS - 1, 1)
            turned_new(GROUPS - 4, 0)
            rows(GROUPS - 5, GROUP - 1, (N - 2) * 16)
            rows(GROUPS - 4, 0, (N - 1) * 16)
            for q in range(GROUPS - 3, GROUPS):
                turned_new(q, q % 2)
                rows(q, q % GROUP, (N - 1) * 16)

        @block.vector
        def _(v):
            reg = v.alloc_register("gin_vector")
            v.memset(sd[:], 1.0).then_inc(s_k, 1)

            def add_sums(i, q, k):
                v.wait_ge(s_hn, q + 1)
                v.wait_ge(s_a[k], i * 16 + 16)
                if due(q - 1):
                    v.wait_ge(s_ta, q - 1)
                v.scalar_tensor_tensor(tr[:, k % 2, :], hn[:, k % 2, :], 0.0, ag[:, k, :], ALU.max, ALU.add).then_inc(s_tr, 1)

            def add(q, k, stored):
                v.wait_ge(s_mb, q + 1)
                if due(stored):
                    v.wait_ge(s_o[k], stored)
                if due(q - 3):
                    v.wait_ge(s_h2, q - 3)
                v.scalar_tensor_tensor(xo[:, k, :], pB[k % 2][:], 0.0, x[:, k, :], ALU.max, ALU.add).then_inc(s_xo, 1)

            def stats(q, k):
                b = k % 2
                v.wait_ge(s_xo, q + 1)
                for j in range(GROUP):
                    ins = v.bn_stats(bs[:, b, j, :], xo[:, k, j * D:(j + 1) * D])
                ins.then_inc(s_bn, 1)
                if due(q - 1):
                    v.wait_ge(s_nm, q - 1)
                count = held(v, reg, q + 1)
                v.wait_ge(s_k, 1)
                v.wait_ge(s_bn, count)
                v.bn_aggr(mv[:, b, 0, :], bs[:, b, 0, :])
                for j in range(1, GROUP):
                    ins = v.bn_aggr(mv[:, b, j, :], bs[:, b, j, :])
                ins.then_inc(s_mv, 1)

            def scale(q, k):
                b = k % 2
                v.wait_ge(s_sd, q + 1)
                if due(q - 3):
                    v.wait_ge(s_h2, q - 3)
                v.reciprocal(rs[:, k, :], sd[:, b, :]).then_inc(s_rs, 1)
                v.wait_ge(s_rs, q + 1)
                v.scalar_tensor_tensor(nm[:, k, :], mv[:, b, :, 0], -1.0, rs[:, k, :], ALU.mult, ALU.mult).then_inc(s_nm, 1)

            def body(i):
                for k in range(GROUP):
                    q = i * GROUP + k
                    add_sums(i, q, k)
                    if due(q - 1):
                        scale(q - 2, (k - 2) % GROUP)
                    if due(q):
                        add(q - 1, (k - 1) % GROUP, (i if k >= 1 else i - 1) * 16)
                        stats(q - 1, (k - 1) % GROUP)
            looped(v, body, N, peel=2)
            last = GROUPS - 1
            scale(last - 1, GROUP - 2)
            add(last, GROUP - 1, (N - 1) * 16)
            stats(last, GROUP - 1)
            scale(last, GROUP - 1)

        @block.tensor
        def _(pe):
            ident = K["ident"]

            def turn(q, b):
                pe.wait_ge(s_tr, q + 1)
                if due(q - 1):
                    pe.wait_ge(s_tT, q - 1)
                for j in range(GROUP):
                    ins = pe.transpose(pA[b][:, j * D:(j + 1) * D], tr[:, b, j * D:(j + 1) * D], ident[:])
                ins.then_inc(s_ta, 1)

            def product(q, b):
                pe.wait_ge(s_tT, q + 1)
                if due(q - 1):
                    pe.wait_ge(s_xo, q - 1)
                for j in range(GROUP):
                    ins = pe.matmul(pB[b][:, j * D:(j + 1) * D], tT[:, b, j * D:(j + 1) * D], K["w1"][:],
                                    start=True, stop=True)
                ins.then_inc(s_mb, 1)

            def turn_new(q, b):
                pe.wait_ge(s_h2, q + 1)
                if due(q - 1):
                    pe.wait_ge(s_h2T, q - 1)
                for j in range(GROUP):
                    ins = pe.transpose(pC[b][:, j * D:(j + 1) * D], h2[:, b, j * D:(j + 1) * D], ident[:])
                ins.then_inc(s_tc, 1)

            def transform(q, b):
                pe.wait_ge(s_h2T, q + 1)
                if due(q):
                    pe.wait_ge(s_xt, q)
                for j in range(GROUP):
                    pe.matmul(pD[j // 2][:, j % 2, :], h2T[:, b, j * D:(j + 1) * D], K["w_cat"][:],
                              start=True, stop=False)
                    ins = pe.matmul(pD[j // 2][:, j % 2, :], K["one_row"][:], K["xt_bias"][:],
                                    start=False, stop=True)
                ins.then_inc(s_md, 1)

            def body(i):
                for k in range(GROUP):
                    q = i * GROUP + k
                    turn(q, k % 2)
                    if due(q - 3):
                        turn_new(q - 4, k % 2)
                    product(q, k % 2)
                    if due(q - 3):
                        transform(q - 4, k % 2)
            looped(pe, body, N, peel=2)
            for q in range(GROUPS - 4, GROUPS):
                turn_new(q, q % 2)
                transform(q, q % 2)


def gat_gather(nc, K, G):
    at = earlier(K, gathered=16 * STEPS, scattered=16 * STEPS)
    g0, sc0 = at["gathered"], at["scattered"]
    with ExitStack() as st:
        c = Ctx(nc, st)
        gi = c.sb("gat_src", [P, RING], I32); di = c.sb("gat_dst", [P, RING], I32)
        g = c.sb("gat_rows", [P, RING, XT_W]); a = c.sb("gat_alpha", [P, RING, HEADS])
        s_start = c.sem("gat_start"); s_gi = c.sem("gat_src_ready"); s_di = c.sem("gat_dst_ready")
        s_g = K["gather_sems"]; s_a = K["scatter_sems"]
        s_cp = c.sem("gat_row_kept"); s_al = c.sem("gat_alpha_kept")
        block = c.phase()

        @block.gpsimd
        def _(pool):
            reg = pool.alloc_register("gat_pool")
            pool.memset(a[:], 0.0).then_inc(s_start, 1)
            pool.wait_ge(s_start, 1)

            def body(i):
                for k in range(RING):
                    if k % HALF == 0:
                        if due(i):
                            for kk in range(k, k + HALF):
                                pool.wait_ge(s_g[kk], g0 + i * 16)
                                pool.wait_ge(s_a[kk], sc0 + i * 16)
                        pool.wait_ge(s_start, 1)
                        pool.tensor_copy(gi[:, k:k + HALF], K["src_idx"][:, bass.ds(i * RING + k, HALF)]).then_inc(s_gi, 1)
                        pool.tensor_copy(di[:, k:k + HALF], K["dst_row"][:, bass.ds(i * RING + k, HALF)]).then_inc(s_di, 1)
                    n = held(pool, reg, i * 2 + k // HALF + 1)
                    pool.wait_ge(s_start, 1)
                    pool.wait_ge(s_gi, n)
                    pool.wait_ge(s_di, n)
                    if due(i):
                        n = held(pool, reg, i * RING - RING + k + 1)
                        pool.wait_ge(s_start, 1)
                        pool.wait_ge(s_cp, n)
                        pool.wait_ge(s_al, n)
                    pool.indirect_dma_start(g[:, k, :], None, K["xt"], bass.IndirectOffsetOnAxis(gi[:, k:k + 1], 0),
                                            bounds_check=NODES_PAD - 1, oob_is_err=False).then_inc(s_g[k], 16)
                    pool.indirect_dma_start(a[:, k, :], None, K["ad"], bass.IndirectOffsetOnAxis(di[:, k:k + 1], 0),
                                            bounds_check=NODES_PAD - 1, oob_is_err=False).then_inc(s_a[k], 16)
            looped(pool, body, STEPS)

        @block.scalar
        def _(act):
            def body(i):
                for k in range(RING):
                    act.wait_ge(s_start, 1)
                    act.wait_ge(s_g[k], g0 + i * 16 + 16)
                    act.copy(G["rows"][:, bass.ds(i * RING + k, 1), :].rearrange("p a w -> p (a w)"),
                             g[:, k, :]).then_inc(s_cp, 1)
            looped(act, body, STEPS)

        @block.vector
        def _(v):
            def body(i):
                for k in range(RING):
                    v.wait_ge(s_g[k], g0 + i * 16 + 16)
                    v.wait_ge(s_a[k], sc0 + i * 16 + 16)
                    v.tensor_tensor(G["alpha"][:, bass.ds(i * RING + k, 1), :].rearrange("p a w -> p (a w)"),
                                    g[:, k, D:D + HEADS], a[:, k, :], ALU.add).then_inc(s_al, 1)
            looped(v, body, STEPS)


def gat_weights(nc, K, G):
    with ExitStack() as st:
        c = Ctx(nc, st)
        pen = c.sb("gat_pen", [P, COLS]); d = c.sb("gat_drop", [P, COLS, HEADS])
        s_v = c.sem("gat_vector"); s_d = c.sem("gat_differences"); s_e = c.sem("gat_exponentials")
        block = c.phase()
        al, top, rescale, w = G["alpha"], G["top"], G["rescale"], G["weight"]

        @block.vector
        def _(v):
            step = stepper(v, s_v)
            step(v.scalar_tensor_tensor(al[:], al[:], 0.2, al[:], ALU.mult, ALU.max))
            step(v.tensor_scalar(pen[:], K["same"][:], -1.0, FAR, ALU.add, ALU.mult))
            for h in range(HEADS):
                step(v.tensor_tensor_scan(top[:, :, h], pen[:], al[:, :, h], -FAR, ALU.add, ALU.max))
            step(v.memset(d[:, 0:1, :], 0.0))
            step(v.tensor_tensor(d[:, 1:COLS, :], top[:, 0:COLS - 1, :], top[:, 1:COLS, :], ALU.subtract))
            step(v.tensor_scalar(d[:], d[:], 0.0, None, ALU.min))
            step(v.tensor_tensor(w[:], al[:], top[:], ALU.subtract))
            v.tensor_copy(pen[:, 0:1], pen[:, 1:2]).then_inc(s_d, 1)
            v.wait_ge(s_e, 2)
            step(v.tensor_tensor(rescale[:], rescale[:], K["same"][:].unsqueeze(2).to_broadcast([P, COLS, HEADS]), ALU.mult))
            for h in range(HEADS):
                step(v.tensor_tensor_scan(al[:, :, h], rescale[:, :, h], w[:, :, h], 0.0, ALU.mult, ALU.add))
            for o, src in ((G["head_den"], al), (G["head_top"], top)):
                step(v.tensor_tensor(d[:], src[:], K["head_end"][:].unsqueeze(2).to_broadcast([P, COLS, HEADS]), ALU.mult))
                step(v.tensor_reduce(o[:], d[:].rearrange("p c h -> p h c"), AX_X, ALU.add))
            step(v.tensor_copy(G["tail_den"][:], al[:, COLS - 1, :]))
            step(v.tensor_copy(G["tail_top"][:], top[:, COLS - 1, :]))
            step(v.tensor_scalar(al[:], al[:], 1e-16, None, ALU.add))
            step(v.reciprocal(al[:], al[:]))

        @block.scalar
        def _(act):
            act.wait_ge(s_d, 1)
            act.activation(rescale[:], d[:], ACT.Exp).then_inc(s_e, 1)
            act.activation(w[:], w[:], ACT.Exp).then_inc(s_e, 1)


def gat_sum(nc, K, G, x):
    at = earlier(K, scattered=16 * STEPS, fix_written=16)
    sc0 = at["scattered"]
    with ExitStack() as st:
        c = Ctx(nc, st)
        si = c.sb("gsum_idx", [P, RING], I32); run = c.sb("gsum_run", [P, RING, D]); tmp = c.sb("gsum_tmp", [P, 2, D])
        res = c.sb("gsum_result", [P, RING, D]); wr = c.sb("gsum_rows", [P, RING, D]); hd = c.sb("gsum_head", [P, D])
        fixed = c.sb("gsum_fixed", [P, D]); num = c.sb("gsum_num", [P, D + HEADS]); rd = c.sb("gsum_rden", [P, HEADS])
        tb = c.sb("gsum_tail_bc", [P, HEADS, P]); mb = c.sb("gsum_top_bc", [P, HEADS, P])
        pen = c.sb("gsum_pen", [P, P]); cm = c.sb("gsum_cmp", [P, HEADS, P])
        mt = c.sb("gsum_top", [P, HEADS]); hs = c.sb("gsum_head_scale", [P, HEADS]); dd = c.sb("gsum_diff", [P, HEADS, P])
        ge = c.sb("gsum_factor", [P, HEADS, P])
        pt = c.ps("gsum_pt", [P, HEADS, P]); pm = c.ps("gsum_pm", [P, HEADS, P]); pc = c.ps("gsum_pc", [P, D + HEADS])
        s_clear = c.sem("gsum_cleared"); s_si = c.sem("gsum_idx_ready"); s_w = c.sem("gsum_weighted")
        s_t = c.sem("gsum_rescaled"); s_run = c.sem("gsum_run_done"); s_res = c.sem("gsum_result_done")
        s_hd = c.sem("gsum_head_done"); s_sc = K["scatter_sems"]; s_out = K["fix_sems"][1]
        s_v = c.sem("gsum_vector"); s_tb = c.sem("gsum_tail_spread")
        s_pt = c.sem("gsum_tail_turned"); s_mb = c.sem("gsum_top_spread"); s_pm = c.sem("gsum_top_turned")
        s_dd = c.sem("gsum_diff_done"); s_ex = c.sem("gsum_exp_done"); s_ge = c.sem("gsum_factor_done")
        s_pc = c.sem("gsum_carry_done"); s_fd = c.sem("gsum_fixed_done")
        block = c.phase()

        def heads(row):
            return row.rearrange("p (h e) -> p h e", h=HEADS)

        def spread(col):
            return col.unsqueeze(2).to_broadcast([P, HEADS, HD])

        @block.gpsimd
        def _(pool):
            reg = pool.alloc_register("gsum_pool")

            def body(i):
                for k in range(RING):
                    if k % HALF == 0:
                        if due(i):
                            for kk in range(k, k + HALF):
                                pool.wait_ge(s_sc[kk], sc0 + i * 16)
                        pool.wait_ge(s_clear, 2)
                        pool.tensor_copy(si[:, k:k + HALF],
                                         K["add_idx_whole"][:, bass.ds(i * RING + k, HALF)]).then_inc(s_si, 1)
                    count = held(pool, reg, i * 2 + k // HALF + 1)
                    pool.wait_ge(s_clear, 2)
                    pool.wait_ge(s_si, count)
                    count = held(pool, reg, i * RING + k + 1)
                    pool.wait_ge(s_clear, 2)
                    pool.wait_ge(s_res, count)
                    if k >= HALF or due(i):
                        turn = held(pool, reg, sc0 + (i * 16 + 16 if k >= HALF else i * 16))
                        pool.wait_ge(s_clear, 2)
                        pool.wait_ge(s_sc[(k - HALF) % RING], turn)
                    pool.indirect_dma_start(x, bass.IndirectOffsetOnAxis(si[:, k:k + 1], 0), res[:, k, :], None,
                                            bounds_check=NODES_PAD - 1, oob_is_err=True, compute_op=ALU.add).then_inc(s_sc[k], 16)
            looped(pool, body, STEPS)
            for k in range(RING):
                pool.wait_ge(s_sc[k], sc0 + 16 * STEPS)
            pool.wait_ge(s_fd, 1)
            pool.indirect_dma_start(x, bass.IndirectOffsetOnAxis(K["head_add_idx"][:, 0:1], 0), fixed[:], None,
                                    bounds_check=NODES_PAD - 1, oob_is_err=True, compute_op=ALU.add).then_inc(s_out, 16)
            pool.wait_ge(s_out, at["fix_written"] + 16)

        @block.scalar
        def _(act):
            act.wait_ge(s_dd, 1)
            act.activation(hs[:], hs[:], ACT.Exp).then_inc(s_ex, 1)
            act.activation(ge[:], dd[:], ACT.Exp, scale=-1.0).then_inc(s_ex, 1)

        @block.vector
        def _(v):
            v.memset(run[:], 0.0).then_inc(s_clear, 1)
            v.memset(hd[:], 0.0).then_inc(s_clear, 1)
            v.wait_ge(s_clear, 2)

            def body(i):
                if due(i):
                    v.wait_ge(s_run, i * RING)
                rows = G["rows"][:, bass.ds(i * RING, RING), 0:D].rearrange("p c (h e) -> p c h e", h=HEADS)
                w = G["weight"][:, bass.ds(i * RING, RING), :].unsqueeze(3).to_broadcast([P, RING, HEADS, HD])
                v.tensor_tensor(wr[:].rearrange("p c (h e) -> p c h e", h=HEADS), rows, w, ALU.mult).then_inc(s_w, 1)
                v.wait_ge(s_w, i + 1)
                for k in range(RING):
                    col = i * RING + k
                    rescale = G["rescale"][:, bass.ds(col, 1), :].rearrange("p a h -> p (a h)")
                    rden = G["alpha"][:, bass.ds(col, 1), :].rearrange("p a h -> p (a h)")
                    if due(col):
                        v.wait_ge(s_run, col)
                    v.tensor_tensor(heads(tmp[:, k % 2, :]), heads(run[:, (k - 1) % RING, :]), spread(rescale),
                                    ALU.mult).then_inc(s_t, 1)
                    if due(col):
                        v.wait_ge(s_hd, col)
                        v.scalar_tensor_tensor(hd[:], run[:, (k - 1) % RING, :], K["head_end"][:, bass.ds(col - 1, 1)],
                                               hd[:], ALU.mult, ALU.add).then_inc(s_hd, 1)
                    else:
                        v.tensor_copy(hd[:], run[:, RING - 1, :]).then_inc(s_hd, 1)
                    v.wait_ge(s_t, col + 1)
                    v.tensor_tensor(run[:, k, :], tmp[:, k % 2, :], wr[:, k, :], ALU.add).then_inc(s_run, 1)
                    v.wait_ge(s_run, col + 1)
                    if due(i):
                        v.wait_ge(s_sc[k], sc0 + i * 16)
                    v.tensor_tensor(heads(res[:, k, :]), heads(run[:, k, :]), spread(rden), ALU.mult).then_inc(s_res, 1)
            looped(v, body, STEPS)

            step = stepper(v, s_v)
            v.wait_ge(s_hd, COLS)
            step(v.scalar_tensor_tensor(hd[:], run[:, RING - 1, :], K["head_end"][:, COLS - 1:COLS], hd[:],
                                        ALU.mult, ALU.add))
            v.tensor_copy(tb[:], G["tail_top"][:].unsqueeze(2).to_broadcast([P, HEADS, P])).then_inc(s_tb, 1)
            step(v.tensor_scalar(pen[:], K["carry_pq"][:], -1.0, FAR, ALU.add, ALU.mult))
            v.wait_ge(s_pt, 1)
            step(v.tensor_tensor(cm[:], pt[:], pen[:].unsqueeze(1).to_broadcast([P, HEADS, P]), ALU.add))
            step(v.tensor_reduce(mt[:], cm[:], AX_X, ALU.max))
            step(v.tensor_tensor(mt[:], mt[:], G["head_top"][:], ALU.max))
            v.tensor_copy(mb[:], mt[:].unsqueeze(2).to_broadcast([P, HEADS, P])).then_inc(s_mb, 1)
            step(v.tensor_tensor(hs[:], G["head_top"][:], mt[:], ALU.subtract))
            v.wait_ge(s_pm, 1)
            for h in range(HEADS):
                ins = v.tensor_scalar(dd[:, h, :], pm[:, h, :], G["tail_top"][:, h:h + 1], 0.0, ALU.subtract, ALU.max)
            ins.then_inc(s_dd, 1)
            v.wait_ge(s_ex, 2)
            v.tensor_tensor(ge[:], ge[:], K["carry_qp"][:].unsqueeze(1).to_broadcast([P, HEADS, P]), ALU.mult).then_inc(s_ge, 1)
            step(v.tensor_tensor(heads(num[:, 0:D]), heads(hd[:]), spread(hs[:]), ALU.mult))
            step(v.tensor_tensor(num[:, D:D + HEADS], G["head_den"][:], hs[:], ALU.mult))
            v.wait_ge(s_pc, 1)
            step(v.tensor_tensor(num[:], num[:], pc[:], ALU.add))
            step(v.tensor_scalar(rd[:], num[:, D:D + HEADS], 1e-16, None, ALU.add))
            step(v.reciprocal(rd[:], rd[:]))
            v.tensor_tensor(heads(fixed[:]), heads(num[:, 0:D]), spread(rd[:]), ALU.mult).then_inc(s_fd, 1)

        @block.tensor
        def _(pe):
            pe.wait_ge(s_tb, 1)
            for h in range(HEADS):
                ins = pe.transpose(pt[:, h, :], tb[:, h, :], K["ident"][:])
            ins.then_inc(s_pt, 1)
            pe.wait_ge(s_mb, 1)
            for h in range(HEADS):
                ins = pe.transpose(pm[:, h, :], mb[:, h, :], K["ident"][:])
            ins.then_inc(s_pm, 1)
            pe.wait_ge(s_ge, 1)
            for h in range(HEADS):
                pe.matmul(pc[:, h * HD:(h + 1) * HD], ge[:, h, :], run[:, RING - 1, h * HD:(h + 1) * HD],
                          start=True, stop=True)
                ins = pe.matmul(pc[:, D + h:D + h + 1], ge[:, h, :], G["tail_den"][:, h:h + 1],
                                start=True, stop=True)
            ins.then_inc(s_pc, 1)


def sage_first(nc, K, x_in, u_out, y_out):
    with ExitStack() as st:
        c = Ctx(nc, st)
        W = GROUP * D
        x = c.sb("s1_x", [P, GROUP, W]); ag = c.sb("s1_sum", [P, GROUP, W]); rn = c.sb("s1_rn", [P, GROUP, 2 * GROUP])
        hn = c.sb("s1_hn", [P, 2, W]); hT = c.sb("s1_hT", [P, 2, W])
        aT = c.sb("s1_aT", [P, 2, W]); hA = c.sb("s1_h1", [P, 2, W]); xb = c.sb("s1_xb", [P, GROUP, W])
        uo = c.sb("s1_u", [P, GROUP, W]); yo = c.sb("s1_y", [P, GROUP, W])
        pA = c.ps("s1_pA", [P, W]); pB = c.ps("s1_pB", [P, W]); pC = c.ps("s1_pC", [P, W])
        pU = [c.ps(f"s1_pU{b}", [P, W]) for b in range(2)]; pY = [c.ps(f"s1_pY{b}", [P, W]) for b in range(2)]
        s_x = [c.sem(f"s1_x_in{k}") for k in range(GROUP)]; s_a = [c.sem(f"s1_sum_in{k}") for k in range(GROUP)]
        s_uo = [c.sem(f"s1_u_out{k}") for k in range(GROUP)]; s_yo = [c.sem(f"s1_y_out{k}") for k in range(GROUP)]
        s_k = c.sem("s1_const"); s_rn = c.sem("s1_rn_done"); s_hn = c.sem("s1_hn_done"); s_xb = c.sem("s1_xb_done")
        s_ta = c.sem("s1_h_turned"); s_tb = c.sem("s1_mean_turned"); s_hT = c.sem("s1_hT_done")
        s_aT = c.sem("s1_aT_done"); s_mc = c.sem("s1_product"); s_hA = c.sem("s1_h1_done"); s_md = c.sem("s1_product2")
        s_u = c.sem("s1_u_done"); s_y = c.sem("s1_y_done")
        block = c.phase()
        xr, ar = rows_by_group(x_in, D), rows_by_group(K["ag"], D)
        uw, yw = rows_by_group(u_out, D), rows_by_group(y_out, D)
        N = GROUPS // GROUP

        @block.sync
        def _(sp):
            def store(q, k):
                sp.wait_ge(s_u, q + 1)
                sp.dma_start(uw[:, bass.ds(q * W, W)], uo[:, k, :]).then_inc(s_uo[k], 16)
                sp.wait_ge(s_y, q + 1)
                sp.dma_start(yw[:, bass.ds(q * W, W)], yo[:, k, :]).then_inc(s_yo[k], 16)

            def body(i):
                for k in range(GROUP):
                    q = i * GROUP + k
                    if due(q - GROUP + 1):
                        sp.wait_ge(s_xb, q - GROUP + 1)
                        sp.wait_ge(s_tb, q - GROUP + 1)
                    sp.dma_start(x[:, k, :], xr[:, bass.ds(q * W, W)]).then_inc(s_x[k], 16)
                    sp.dma_start(ag[:, k, :], ar[:, bass.ds(q * W, W)]).then_inc(s_a[k], 16)
                    if due(q - 2):
                        store(q - 3, (k - 3) % GROUP)
            looped(sp, body, N)
            for q in range(GROUPS - 3, GROUPS):
                store(q, q % GROUP)
            for k in range(GROUP):
                sp.wait_ge(s_uo[k], 16 * N)
                sp.wait_ge(s_yo[k], 16 * N)

        @block.gpsimd
        def _(pool):
            reg = pool.alloc_register("s1_pool")

            def body(i):
                for k in range(GROUP):
                    q = i * GROUP + k
                    if k == 0:
                        if due(i):
                            n0 = held(pool, reg, i * GROUP)
                            pool.wait_ge(s_k, 1)
                            pool.wait_ge(s_hn, n0)
                        pool.tensor_copy(rn[:].rearrange("p k c -> p (k c)"),
                                         K["node_rn"][:, bass.ds(i * (2 * GROUP * GROUP), 2 * GROUP * GROUP)]).then_inc(s_rn, 1)
                        n1 = held(pool, reg, i + 1)
                        pool.wait_ge(s_k, 1)
                        pool.wait_ge(s_rn, n1)
                    n2 = held(pool, reg, i * 16 + 16)
                    pool.wait_ge(s_k, 1)
                    pool.wait_ge(s_x[k], n2)
                    if due(q - 1):
                        n3 = held(pool, reg, q - 1)
                        pool.wait_ge(s_k, 1)
                        pool.wait_ge(s_ta, n3)
                    for j in range(GROUP):
                        ins = pool.tensor_scalar(hn[:, k % 2, j * D:(j + 1) * D], x[:, k, j * D:(j + 1) * D],
                                                 rn[:, k, 2 * j:2 * j + 1], rn[:, k, 2 * j + 1:2 * j + 2],
                                                 ALU.mult, ALU.add)
                    ins.then_inc(s_hn, 1)
                    if due(q - GROUP + 1):
                        pool.wait_ge(s_y, q - GROUP + 1)
                    pool.tensor_tensor(xb[:, k, :].rearrange("p (j d) -> p j d", d=D),
                                       x[:, k, :].rearrange("p (j d) -> p j d", d=D),
                                       K["b2_bc"][:].unsqueeze(1).to_broadcast([P, GROUP, D]), ALU.add).then_inc(s_xb, 1)
            looped(pool, body, N)

        @block.scalar
        def _(act):
            def body(i):
                for k in range(GROUP):
                    q = i * GROUP + k
                    act.wait_ge(s_ta, q + 1)
                    act.activation(hT[:, k % 2, :], pA[:], ACT.Relu).then_inc(s_hT, 1)
                    if due(q):
                        copy_u(q - 1, (k - 1) % GROUP, (i if k >= 1 else i - 1) * 16)
                    act.wait_ge(s_mc, q + 1)
                    act.activation(hA[:, k % 2, :], pC[:], ACT.Relu, bias=K["b1"][:, 0:1]).then_inc(s_hA, 1)

            def copy_u(q, k, stored):
                act.wait_ge(s_md, q + 1)
                if due(stored):
                    act.wait_ge(s_uo[k], stored)
                act.activation(uo[:, k, :], pU[k % 2][:], ACT.Identity).then_inc(s_u, 1)
            looped(act, body, N, peel=2)
            copy_u(GROUPS - 1, GROUP - 1, (N - 1) * 16)

        @block.vector
        def _(v):
            v.memset(aT[:], 0.0).then_inc(s_k, 1)
            v.wait_ge(s_k, 1)

            def add(q, k, stored):
                v.wait_ge(s_md, q + 1)
                v.wait_ge(s_xb, q + 1)
                if due(stored):
                    v.wait_ge(s_yo[k], stored)
                v.tensor_tensor(yo[:, k, :], pY[k % 2][:], xb[:, k, :], ALU.add).then_inc(s_y, 1)

            def body(i):
                for k in range(GROUP):
                    q = i * GROUP + k
                    v.wait_ge(s_tb, q + 1)
                    v.tensor_copy(aT[:, k % 2, :], pB[:]).then_inc(s_aT, 1)
                    if due(q):
                        add(q - 1, (k - 1) % GROUP, (i if k >= 1 else i - 1) * 16)
            looped(v, body, N, peel=2)
            add(GROUPS - 1, GROUP - 1, (N - 1) * 16)

        @block.tensor
        def _(pe):
            def second(q, k):
                pe.wait_ge(s_hA, q + 1)
                if due(q - 1):
                    pe.wait_ge(s_u, q - 1)
                    pe.wait_ge(s_y, q - 1)
                for bank, w in ((pU, 0), (pY, D)):
                    for j in range(GROUP):
                        ins = pe.matmul(bank[k % 2][:, j * D:(j + 1) * D], hA[:, k % 2, j * D:(j + 1) * D],
                                        K["w2lr"][:, w:w + D], start=True, stop=True)
                ins.then_inc(s_md, 1)

            def body(i):
                for k in range(GROUP):
                    q = i * GROUP + k
                    b = k % 2
                    pe.wait_ge(s_hn, q + 1)
                    if due(q):
                        pe.wait_ge(s_hT, q)
                    for j in range(GROUP):
                        ins = pe.transpose(pA[:, j * D:(j + 1) * D], hn[:, b, j * D:(j + 1) * D], K["ident"][:])
                    ins.then_inc(s_ta, 1)
                    pe.wait_ge(s_a[k], i * 16 + 16)
                    if due(q):
                        pe.wait_ge(s_aT, q)
                    for j in range(GROUP):
                        ins = pe.transpose(pB[:, j * D:(j + 1) * D], ag[:, k, j * D:(j + 1) * D], K["ident"][:])
                    ins.then_inc(s_tb, 1)
                    if due(q):
                        second(q - 1, k - 1)
                    pe.wait_ge(s_hT, q + 1)
                    pe.matmul(pC[:], K["w1r"][:], hT[:, b, :], start=True, stop=False)
                    pe.wait_ge(s_aT, q + 1)
                    pe.matmul(pC[:], K["w1l"][:], aT[:, b, :], start=False, stop=True).then_inc(s_mc, 1)
            looped(pe, body, N)
            second(GROUPS - 1, GROUP - 1)


def program(nc, A, out):
    with ExitStack() as st:
        c = Ctx(nc, st)
        K = {"counts": dict(gathered=0, scattered=0, fix_rows=0, fix_written=0)}
        for name, shape in (("ident", [P, P]), ("ones", [P, 1]), ("eps", [P, 1]), ("real", [P, 1]), ("valid", [P, COLS]),
                            ("same", [P, COLS]), ("carry_qp", [P, P]), ("carry_pq", [P, P]),
                            ("node_mv", [P, 2 * TILES]), ("node_rn", [P, 2 * TILES]), ("inv_edge", [P, COLS]), ("inv_head", [P, 1]),
                            ("head_end", [P, COLS]),
                            ("w_in", [P, 3 * D]), ("w_hh", [P, 3 * D]),
                            ("b_rz", [P, 2]), ("b_n", [P, 2]), ("w1", [P, D]), ("vn", [P, 1]), ("v_col", [P, 1]),
                            ("w_cat", [P, XT_W]), ("w1l", [P, D]), ("w1r", [P, D]),
                            ("w2lr", [P, 2 * D]), ("b1", [P, 1]), ("b2_bc", [P, D])):
            K[name] = c.sb(name, shape)
        for name, width in (("emb_in", 3 * D), ("xt_bias", XT_W), ("one_row", P)):
            K[name] = c.sb(name, [STACK, width], BF16)
        for name in ("src_idx", "dst_idx", "add_idx", "add_idx_whole", "dst_row"):
            K[name] = c.sb(name, [P, COLS], I32)
        K["gather_sems"] = [c.sem(f"gathered{k}") for k in range(RING)]
        K["scatter_sems"] = [c.sem(f"scattered{k}") for k in range(RING)]
        K["fix_sems"] = [c.sem("fix_rows"), c.sem("fix_written")]
        K["head_idx"] = c.sb("head_idx", [P, 1], I32); K["head_add_idx"] = c.sb("head_add_idx", [P, 1], I32)

        def dram(name, width):
            return nc.dram_tensor(name, [NODES_PAD, width], F32, kind="Internal").ap()
        K["ag_wide"], K["ag"] = dram("sums_wide", WIDE), dram("sums", D)
        K["xt"], K["ad"] = dram("gat_rows_t", XT_W), dram("gat_alpha_t", HEADS)
        x1, x2, u = (dram(n, D) for n in ("x1", "x2", "u_rows"))
        K["wide_cleared"] = c.sem("wide_cleared")

        with ExitStack() as s0:
            K["onehot"] = s0.enter_context(nc.sbuf_tensor("onehot", [P, COLS, 16], F32))
            K["zero"] = s0.enter_context(nc.sbuf_tensor("zero", [P, CLEAR], F32))
            setup(nc, A, K)
            edge_pass(nc, K, "e0", A["x"], K["ag_wide"], WIDE, True, "stats")
        finish_stats(nc, K, "f0")
        gru_nodes(nc, K, A["x"], x1)
        finish_stats(nc, K, "f1")
        edge_pass(nc, K, "e1", x1, K["ag"], D, True, "colsum")
        gin_nodes(nc, K, x1, x2)
        with ExitStack() as s2:
            G = {"rows": s2.enter_context(nc.sbuf_tensor("edge_rows", [P, COLS, XT_W], F32))}
            for name in ("alpha", "top", "rescale", "weight"):
                G[name] = s2.enter_context(nc.sbuf_tensor("edge_" + name, [P, COLS, HEADS], F32))
            for name in ("head_den", "head_top", "tail_den", "tail_top"):
                G[name] = s2.enter_context(nc.sbuf_tensor(name, [P, HEADS], F32))
            gat_gather(nc, K, G)
            gat_weights(nc, K, G)
            gat_sum(nc, K, G, x2)
        edge_pass(nc, K, "e3", x2, K["ag"], D, True, "stats", mean=True)
        finish_stats(nc, K, "f3")
        sage_first(nc, K, x2, u, out)
        edge_pass(nc, K, "e4", u, out, D, False, mean=True, into=True)


def kernel(**inputs):
    import numpy as np
    import concourse.bacc as bacc
    from concourse.bass_utils import run_bass_kernel_spmd as run

    a = {k: np.asarray(v) for k, v in inputs.items()}
    pad_e = EDGES_PAD - EDGES
    q = np.arange(P)
    e = np.arange(EDGES_PAD)

    def by_partition(v, parts):
        return np.ascontiguousarray(v.reshape(parts, D).T)
    arrays = {
        "x": np.pad(a["x"], ((0, NODES_PAD - NODES), (0, 0))),
        "src": np.pad(a["src"], (0, pad_e)),
        "dst": np.concatenate([np.array([-1], np.int32), a["dst"], np.full(pad_e, PAD_DST, np.int32),
                               np.array([-1], np.int32)]),
        "etype": np.pad(a["edge_type_9"], (0, pad_e)),
        "ident": np.eye(P, dtype=np.float32),
        "iota": np.tile(np.arange(16, dtype=np.float32), (P, 1)),
        "tri": (q[:, None] < q[None, :]).astype(np.float32),
        "tri_t": (q[:, None] > q[None, :]).astype(np.float32),
        "real": (q < NODES // TILES).astype(np.float32)[:, None],
        "valid": (e < EDGES).astype(np.float32).reshape(P, COLS),
        "spare": (NODES + (e % COLS % HALF) * P + e // COLS).astype(np.float32).reshape(P, COLS),
        "blk": (q[:, None] // HD == np.arange(HEADS)[None, :]).astype(np.float32),
        "emb": np.tile(np.pad(a["L0_gnn_edge_embed"].T, ((0, 0), (0, SLOTS - TYPES))), (1, 2 * SPLIT)),
        "part": (np.arange(STACK)[:, None] // SLOTS % SPLIT == np.arange(SPLIT)[None, :]).astype(np.float32),
        "pick": np.repeat((np.arange(STACK)[:, None] % SLOTS == 0) & (np.arange(STACK)[:, None] < STACK // 2),
                          P, 1).astype(np.float32),
        "b_msg": a["L0_gnn_b_msg"][:, None],
        "w_msg": a["L0_gnn_W_msg"], "w_ih": a["L0_gnn_W_ih"].T, "w_hh": a["L0_gnn_W_hh"].T,
        "b_gru": np.stack([by_partition(a["L0_gnn_b_ih"], 3), by_partition(a["L0_gnn_b_hh"], 3)], 1),
        "w1": a["L1_gnn_W"], "vn": a["L1_gnn_virtual_node"].T,
        "coef": a["L2_gnn_coeffs_t"],
        "lin_w": a["L2_gnn_lin_weight"].transpose(1, 0, 2), "lin_wt": a["L2_gnn_lin_weight"].transpose(2, 0, 1),
        "att_cols": np.stack([a["L2_gnn_att_src"].reshape(3, D).T, a["L2_gnn_att_dst"].reshape(3, D).T,
                              a["L2_gnn_lin_bias"].reshape(3, D).T], 2).transpose(0, 1, 2),
        "w1l": a["L3_gnn_W1_l"].T, "w1r": a["L3_gnn_W1_r"].T,
        "w2lr": np.concatenate([a["L3_gnn_W2_l"].T, a["L3_gnn_W2_r"].T], 1),
        "b1": a["L3_gnn_b1"][:, None], "b2": a["L3_gnn_b2"],
    }
    arrays = {"in_" + k: np.ascontiguousarray(v) for k, v in arrays.items()}
    nc = bacc.Bacc("TRN2", target_bir_lowering=False, num_devices=1)
    A = {k[3:]: nc.dram_tensor(k, v.shape, mybir.dt.from_np(v.dtype), kind="ExternalInput").ap()
         for k, v in arrays.items()}
    out = nc.dram_tensor("out_rows", [NODES_PAD, D], F32, kind="ExternalOutput").ap()
    program(nc, A, out)
    r = run(nc, [arrays], core_ids=[0])
    return r.results[0]["out_rows"][:NODES]
```
